# Optimizing a Trainium2 kernel written in Bass

```python
import numpy as np
import jax
import jax.numpy as jnp

def _softmax(x, axis=-1):
    return jax.nn.softmax(x, axis=axis)

def _gelu(x):
    return jax.nn.gelu(x, approximate=True)

def _silu(x):
    return jax.nn.silu(x)

def _sigmoid(x):
    return jax.nn.sigmoid(x)

def _layernorm(x, axis=-1, eps=1e-05):
    m = jnp.mean(x, axis=axis, keepdims=True)
    v = jnp.var(x, axis=axis, keepdims=True)
    return (x - m) / jnp.sqrt(v + eps)

def _scatter_add(tgt, idx, src, axis=0):
    return tgt.at[idx].add(src)

def _segment_sum(src, seg, n):
    return jax.ops.segment_sum(src, seg, n)
kernel_name = 'mk_adaln_ffn_d2_seqx_r8_bc1cfe'

def setup_inputs(seed: int=0):
    np.random.seed(seed)
    _w = jnp.asarray

    def _rec_inputs():
        import jax
        import jax.numpy as jnp
        _rk = jax.random.key(seed)
        x = -7.109e-05 + 0.9999 * jax.random.normal(jax.random.fold_in(_rk, 1), (128, 32, 128), jnp.float32)
        _lenS = 32 - jax.random.randint(jax.random.fold_in(_rk, 7), (128,), 0, max(1, 32 // 4) + 1, jnp.int32)
        _lenS2 = 32 - jax.random.randint(jax.random.fold_in(_rk, 8), (128,), 0, max(1, 32 // 4) + 1, jnp.int32)
        itok_B_0_8 = jax.random.randint(jax.random.fold_in(_rk, 11), (128,), 0, 9, jnp.int32)
        itok_B_0_2 = jax.random.randint(jax.random.fold_in(_rk, 12), (128,), 0, 3, jnp.int32)
        return (x, itok_B_0_8, itok_B_0_2)
    x, itok_B_0_8, itok_B_0_2 = _rec_inputs()

    def _L0_cond_setup():
        import jax, jax.numpy as jnp
        import numpy as np
        LN_EPS = 1e-05
        key = jax.random.key(seed)
        ks = jax.random.split(key, 8)
        B, S, H, A, L = (32, 256, 128, 32, 10)
        return {'hidden_states': jax.random.normal(ks[0], (B, S, H), dtype=jnp.float32), 'language_ids': jax.random.randint(ks[1], (B,), 0, L, dtype=jnp.int64), 'W1': jax.random.normal(ks[2], (L, H, A), dtype=jnp.float32) * (1.0 / np.sqrt(H)), 'b1': jnp.zeros((L, A), dtype=jnp.float32), 'W2': jax.random.normal(ks[3], (L, A, H), dtype=jnp.float32) * (1.0 / np.sqrt(A)), 'b2': jnp.zeros((L, H), dtype=jnp.float32), 'gamma': jnp.ones((L, H), dtype=jnp.float32), 'beta': jnp.zeros((L, H), dtype=jnp.float32)}
    _L0_cond_all = _L0_cond_setup()
    _L0_cond_in = {k: v for k, v in _L0_cond_all.items() if k in ('W1', 'b1', 'W2', 'b2', 'gamma', 'beta')}
    del _L0_cond_all

    def _L0_ffn_setup():
        import jax, jax.numpy as jnp
        import numpy as np
        HIDDEN = 128
        INNER = 512

        def _weight_quant(w):
            scale = 1.0 / jnp.clip(jnp.mean(jnp.abs(w)), 1e-05)
            wq = jnp.clip(jnp.round(w * scale), -1.0, 1.0) / scale
            return w + jax.lax.stop_gradient(wq - w)

        def _act_quant(x):
            scale = 127.0 / jnp.clip(jnp.max(jnp.abs(x), axis=-1, keepdims=True), 1e-05)
            xq = jnp.clip(jnp.round(x * scale), -128.0, 127.0) / scale
            return x + jax.lax.stop_gradient(xq - x)

        def _bitlinear(x, w):
            return jnp.einsum('bsi,oi->bso', _act_quant(x), _weight_quant(w))
        key = jax.random.key(seed)
        k0, k1, k2, k3 = jax.random.split(key, 4)
        x = jax.random.normal(k0, (4, 256, HIDDEN), dtype=jnp.float32)
        w_gate = jax.random.normal(k1, (INNER, HIDDEN), dtype=jnp.float32) / np.sqrt(HIDDEN)
        w_up = jax.random.normal(k2, (INNER, HIDDEN), dtype=jnp.float32) / np.sqrt(HIDDEN)
        w_down = jax.random.normal(k3, (HIDDEN, INNER), dtype=jnp.float32) / np.sqrt(INNER)
        return {'x': x, 'w_gate': w_gate, 'w_up': w_up, 'w_down': w_down}
    _L0_ffn_all = _L0_ffn_setup()
    _L0_ffn_in = {k: v for k, v in _L0_ffn_all.items() if k in ('w_gate', 'w_up', 'w_down')}
    del _L0_ffn_all

    def _L1_cond_setup():
        import jax, jax.numpy as jnp
        import numpy as np
        B, S, D, F, E = (8, 256, 128, 512, 5)

        def _dense(x, wi_, wo_):
            return jax.nn.relu(x @ wi_) @ wo_
        key = jax.random.key(seed)
        ks = jax.random.split(key, 9)
        sc = 0.02
        return {'hidden_states': jax.random.normal(ks[0], (B, S, D), jnp.float32), 'type_label': jax.random.randint(ks[1], (B,), 0, E, jnp.int32), 'wi': jax.random.normal(ks[2], (E, D, F), jnp.float32) * sc, 'wo': jax.random.normal(ks[3], (E, F, D), jnp.float32) * sc, 'swi': jax.random.normal(ks[4], (2, D, F), jnp.float32) * sc, 'swo': jax.random.normal(ks[5], (2, F, D), jnp.float32) * sc, 'g1': jax.random.normal(ks[6], (3 * D, D), jnp.float32) * sc, 'g2': jax.random.normal(ks[7], (D, 3), jnp.float32) * sc}
    _L1_cond_all = _L1_cond_setup()
    _L1_cond_in = {k: v for k, v in _L1_cond_all.items() if k in ('wi', 'wo', 'swi', 'swo', 'g1', 'g2')}
    del _L1_cond_all

    def _L1_ffn_setup():
        import jax, jax.numpy as jnp
        import numpy as np
        D = 128
        H = 16
        DK = D // H
        E = 8
        DFF = 4 * D
        TOPK = 2
        EPS = 1e-05

        def _layernorm(x, g, b):
            m = jnp.mean(x, axis=-1, keepdims=True)
            v = jnp.mean(jnp.square(x - m), axis=-1, keepdims=True)
            return (x - m) * jax.lax.rsqrt(v + EPS) * g + b
        key = jax.random.key(seed)
        ks = jax.random.split(key, 16)
        s_in = 1.0 / np.sqrt(D)
        s_ff = 1.0 / np.sqrt(DFF)
        return {'x': jax.random.normal(ks[0], (2, 256, D), dtype=jnp.float32), 'ln1_g': jnp.ones((D,), jnp.float32), 'ln1_b': jnp.zeros((D,), jnp.float32), 'w_qkv': jax.random.normal(ks[1], (D, 3 * D), jnp.float32) * s_in, 'b_qkv': jnp.zeros((3 * D,), jnp.float32), 'w_o': jax.random.normal(ks[2], (D, D), jnp.float32) * s_in, 'b_o': jnp.zeros((D,), jnp.float32), 'ln2_g': jnp.ones((D,), jnp.float32), 'ln2_b': jnp.zeros((D,), jnp.float32), 'gate_w': jax.random.normal(ks[3], (D, E), jnp.float32) * s_in, 'gate_b': jnp.zeros((E,), jnp.float32), 'W1': jax.random.normal(ks[4], (E, D, DFF), jnp.float32) * s_in, 'b1': jnp.zeros((E, DFF), jnp.float32), 'W2': jax.random.normal(ks[5], (E, DFF, D), jnp.float32) * s_ff, 'b2': jnp.zeros((E, D), jnp.float32)}
    _L1_ffn_all = _L1_ffn_setup()
    _L1_ffn_in = {k: v for k, v in _L1_ffn_all.items() if k in ('ln1_g', 'ln1_b', 'w_qkv', 'b_qkv', 'w_o', 'b_o', 'ln2_g', 'ln2_b', 'gate_w', 'gate_b', 'W1', 'b1', 'W2', 'b2')}
    del _L1_ffn_all
    return {'x': x, 'itok_B_0_8': itok_B_0_8, 'itok_B_0_2': itok_B_0_2, 'L0_cond_W1': _L0_cond_in['W1'], 'L0_cond_b1': _L0_cond_in['b1'], 'L0_cond_W2': _L0_cond_in['W2'], 'L0_cond_b2': _L0_cond_in['b2'], 'L0_cond_gamma': _L0_cond_in['gamma'], 'L0_cond_beta': _L0_cond_in['beta'], 'L0_ffn_w_gate': _L0_ffn_in['w_gate'], 'L0_ffn_w_up': _L0_ffn_in['w_up'], 'L0_ffn_w_down': _L0_ffn_in['w_down'], 'L1_cond_wi': _L1_cond_in['wi'], 'L1_cond_wo': _L1_cond_in['wo'], 'L1_cond_swi': _L1_cond_in['swi'], 'L1_cond_swo': _L1_cond_in['swo'], 'L1_cond_g1': _L1_cond_in['g1'], 'L1_cond_g2': _L1_cond_in['g2'], 'L1_ffn_ln1_g': _L1_ffn_in['ln1_g'], 'L1_ffn_ln1_b': _L1_ffn_in['ln1_b'], 'L1_ffn_w_qkv': _L1_ffn_in['w_qkv'], 'L1_ffn_b_qkv': _L1_ffn_in['b_qkv'], 'L1_ffn_w_o': _L1_ffn_in['w_o'], 'L1_ffn_b_o': _L1_ffn_in['b_o'], 'L1_ffn_ln2_g': _L1_ffn_in['ln2_g'], 'L1_ffn_ln2_b': _L1_ffn_in['ln2_b'], 'L1_ffn_gate_w': _L1_ffn_in['gate_w'], 'L1_ffn_gate_b': _L1_ffn_in['gate_b'], 'L1_ffn_W1': _L1_ffn_in['W1'], 'L1_ffn_b1': _L1_ffn_in['b1'], 'L1_ffn_W2': _L1_ffn_in['W2'], 'L1_ffn_b2': _L1_ffn_in['b2']}

def reference(x, itok_B_0_8, itok_B_0_2, L0_cond_W1, L0_cond_b1, L0_cond_W2, L0_cond_b2, L0_cond_gamma, L0_cond_beta, L0_ffn_w_gate, L0_ffn_w_up, L0_ffn_w_down, L1_cond_wi, L1_cond_wo, L1_cond_swi, L1_cond_swo, L1_cond_g1, L1_cond_g2, L1_ffn_ln1_g, L1_ffn_ln1_b, L1_ffn_w_qkv, L1_ffn_b_qkv, L1_ffn_w_o, L1_ffn_b_o, L1_ffn_ln2_g, L1_ffn_ln2_b, L1_ffn_gate_w, L1_ffn_gate_b, L1_ffn_W1, L1_ffn_b1, L1_ffn_W2, L1_ffn_b2):
    import jax
    import jax.numpy as jnp

    def _L0_cond_ref(hidden_states, language_ids, W1, b1, W2, b2, gamma, beta):
        import jax, jax.numpy as jnp
        import numpy as np
        LN_EPS = 1e-05
        w1 = W1[language_ids]
        w2 = W2[language_ids]
        h = jnp.einsum('bsh,bha->bsa', hidden_states, w1) + b1[language_ids][:, None, :]
        h = jax.nn.relu(h)
        adapted = jnp.einsum('bsa,bah->bsh', h, w2) + b2[language_ids][:, None, :]
        x = hidden_states + adapted
        mean = jnp.mean(x, axis=-1, keepdims=True)
        var = jnp.mean(jnp.square(x - mean), axis=-1, keepdims=True)
        normed = (x - mean) * jax.lax.rsqrt(var + LN_EPS)
        return normed * gamma[language_ids][:, None, :] + beta[language_ids][:, None, :]

    def _L0_ffn_ref(x, w_gate, w_up, w_down):
        import jax, jax.numpy as jnp
        import numpy as np
        HIDDEN = 128
        INNER = 512

        def _weight_quant(w):
            scale = 1.0 / jnp.clip(jnp.mean(jnp.abs(w)), 1e-05)
            wq = jnp.clip(jnp.round(w * scale), -1.0, 1.0) / scale
            return w + jax.lax.stop_gradient(wq - w)

        def _act_quant(x):
            scale = 127.0 / jnp.clip(jnp.max(jnp.abs(x), axis=-1, keepdims=True), 1e-05)
            xq = jnp.clip(jnp.round(x * scale), -128.0, 127.0) / scale
            return x + jax.lax.stop_gradient(xq - x)

        def _bitlinear(x, w):
            return jnp.einsum('bsi,oi->bso', _act_quant(x), _weight_quant(w))
        gate = jax.nn.silu(_bitlinear(x, w_gate))
        up = _bitlinear(x, w_up)
        return _bitlinear(gate * up, w_down)

    def _L1_cond_ref(hidden_states, type_label, wi, wo, swi, swo, g1, g2):
        import jax, jax.numpy as jnp
        import numpy as np
        B, S, D, F, E = (8, 256, 128, 512, 5)

        def _dense(x, wi_, wo_):
            return jax.nn.relu(x @ wi_) @ wo_
        x = hidden_states
        s0 = _dense(x, swi[0], swo[0])
        s1 = _dense(x, swi[1], swo[1])
        wi_sel = wi[type_label]
        wo_sel = wo[type_label]
        h = jax.nn.relu(jnp.einsum('bsd,bdf->bsf', x, wi_sel))
        eo = jnp.einsum('bsf,bfd->bsd', h, wo_sel)
        gate_in = jnp.concatenate([eo[:, 0], s0[:, 0], s1[:, 0]], axis=-1)
        w = jax.nn.softmax(jax.nn.relu(gate_in @ g1) @ g2, axis=-1)
        w = w[:, :, None, None]
        return eo * w[:, 0] + s0 * w[:, 1] + s1 * w[:, 2]

    def _L1_ffn_ref(x, ln1_g, ln1_b, w_qkv, b_qkv, w_o, b_o, ln2_g, ln2_b, gate_w, gate_b, W1, b1, W2, b2):
        import jax, jax.numpy as jnp
        import numpy as np
        D = 128
        H = 16
        DK = D // H
        E = 8
        DFF = 4 * D
        TOPK = 2
        EPS = 1e-05

        def _layernorm(x, g, b):
            m = jnp.mean(x, axis=-1, keepdims=True)
            v = jnp.mean(jnp.square(x - m), axis=-1, keepdims=True)
            return (x - m) * jax.lax.rsqrt(v + EPS) * g + b
        B, S, _ = x.shape
        h = _layernorm(x, ln1_g, ln1_b)
        qkv = h @ w_qkv + b_qkv
        q, k, v = jnp.split(qkv, 3, axis=-1)
        q = q.reshape(B, S, H, DK)
        k = k.reshape(B, S, H, DK)
        v = v.reshape(B, S, H, DK)
        scores = jnp.einsum('bqhd,bkhd->bhqk', q, k) / np.sqrt(DK)
        attn = jax.nn.softmax(scores, axis=-1)
        o = jnp.einsum('bhqk,bkhd->bqhd', attn, v).reshape(B, S, D)
        x = x + o @ w_o + b_o
        h = _layernorm(x, ln2_g, ln2_b).reshape(B * S, D)
        logits = h @ gate_w + gate_b
        topv, topi = jax.lax.top_k(logits, TOPK)
        gw = jax.nn.softmax(topv, axis=-1)
        ew = jnp.sum(jax.nn.one_hot(topi, E, dtype=h.dtype) * gw[..., None], axis=1)
        hid = jax.nn.relu(jnp.einsum('td,edf->etf', h, W1) + b1[:, None, :])
        out_e = jnp.einsum('etf,efd->etd', hid, W2) + b2[:, None, :]
        moe = jnp.einsum('etd,te->td', out_e, ew)
        return x + moe.reshape(B, S, D)
    x = x + _L0_ffn_ref(_L0_cond_ref(x, itok_B_0_8, L0_cond_W1, L0_cond_b1, L0_cond_W2, L0_cond_b2, L0_cond_gamma, L0_cond_beta), L0_ffn_w_gate, L0_ffn_w_up, L0_ffn_w_down)
    x = x + _L1_ffn_ref(_L1_cond_ref(x, itok_B_0_2, L1_cond_wi, L1_cond_wo, L1_cond_swi, L1_cond_swo, L1_cond_g1, L1_cond_g2), L1_ffn_ln1_g, L1_ffn_ln1_b, L1_ffn_w_qkv, L1_ffn_b_qkv, L1_ffn_w_o, L1_ffn_b_o, L1_ffn_ln2_g, L1_ffn_ln2_b, L1_ffn_gate_w, L1_ffn_gate_b, L1_ffn_W1, L1_ffn_b1, L1_ffn_W2, L1_ffn_b2)
    return x

_drawn_inputs = setup_inputs


def setup_inputs(seed=0):
    import zlib

    import numpy as np

    out = dict(_drawn_inputs(seed))
    spreads = {'L0_cond_b1': (0.0, 0.445),
     'L0_cond_b2': (0.0, 0.329),
     'L0_cond_gamma': (1.0, 0.2),
     'L0_cond_beta': (0.0, 0.293),
     'L1_ffn_ln1_g': (1.0, 0.2),
     'L1_ffn_ln1_b': (0.0, 0.1),
     'L1_ffn_b_qkv': (0.0, 0.1),
     'L1_ffn_b_o': (0.0, 0.1),
     'L1_ffn_ln2_g': (1.0, 0.2),
     'L1_ffn_ln2_b': (0.0, 0.1),
     'L1_ffn_gate_b': (0.0, 0.1),
     'L1_ffn_b1': (0.0, 0.1),
     'L1_ffn_b2': (0.0, 0.1)}
    factors = {'L1_cond_g1': 8.0, 'L1_cond_g2': 8.0}
    for name, (base, spread) in spreads.items():
        noise = np.random.default_rng([zlib.crc32(name.encode()), seed]).standard_normal(out[name].shape)
        drawn = base * np.exp(spread * noise) if base else spread * noise
        out[name] = jnp.asarray(drawn.astype(out[name].dtype))
    for name, factor in factors.items():
        out[name] = (out[name] * factor).astype(out[name].dtype)
    return out
```

```python
from contextlib import ExitStack

import numpy as np
import concourse.bass as bass
from concourse import mybir

F32 = mybir.dt.float32
F32R = mybir.dt.float32r
BF16 = mybir.dt.bfloat16
I32 = mybir.dt.int32
ALU = mybir.AluOpType
ACT = mybir.ActivationFunctionType
AX = mybir.AxisListType.X

P = 128
B, S, D = 128, 32, 128
T = B * S
LANG, AD = 10, 32
LA = LANG * AD
INNER = 512
TYPES, NSH = 5, 2
H, DK = 16, 8
E = 8
FF = 512
KF = FF // P
SB = 4
NB = S // SB
W = SB * D
BT = P // S
TT = (B + TYPES * (BT - 1)) // BT
TT += TT % 2
ET = (2 * T + E * (P - 1)) // P
ET += ET % 2
CW = (TYPES + NSH) * (FF + KF * D)
C_WO = TYPES * FF
C_SWI = C_WO + TYPES * KF * D
C_SWO = C_SWI + NSH * FF
MW = 2 * E * FF
M_W2 = E * FF
ROW = D + 2
CH = 1024
MAGIC = 1.5 * 2.0 ** 23
OFF = -1.0e30
EPS = 1e-5
HB = 8
NH = B // HB
HG = H // 4
LO = 32


def adaln_ffn_moe_kernel(nc, a, out, dump=None):
    ctx = ExitStack()

    def sb(name, shape, dt=F32, stack=None):
        return (stack or ctx).enter_context(nc.sbuf_tensor(name, shape, dt))

    def pb(name, shape, dt=F32, stack=None):
        return (stack or ctx).enter_context(nc.psum_tensor(name, shape, dt))

    def sem(name, stack=None):
        if name in kept:
            return kept[name]
        handle = sems[-1].enter_context(nc.semaphore(name))
        numbers.append(handle.num)
        return handle

    def reuse_semaphores():
        nc.all_engine_barrier(sems_to_clear=range(min(numbers), max(numbers) + 1))
        sems.pop().close()
        sems.append(ctx.enter_context(ExitStack()))
        numbers.clear()

    with ctx:
        kept = {n: ctx.enter_context(nc.semaphore(n)) for n in ("b_sent", "c_eo_loaded")}
        sems, numbers = [ctx.enter_context(ExitStack())], []
        x1 = sb("x1", [P, S, D])
        ident = sb("ident", [P, P])
        tri = sb("tri", [P, P])
        ones = sb("ones", [P, P])
        hmask = sb("hmask", [P, HG])
        type_slot = sb("type_slot", [P, S], I32)
        type_of_tile = sb("type_of_tile", [1, TT], I32)
        xs_dram = nc.dram_tensor("xs_dram", (TT * P, D), F32, kind="Internal").ap()
        eo_dram = nc.dram_tensor("eo_dram", (TT * P, D), F32, kind="Internal").ap()
        v_dram = nc.dram_tensor("v_dram", (B, S, D), F32, kind="Internal").ap()
        att_dram = nc.dram_tensor("att_dram", (B, S, D), F32, kind="Internal").ap()

        cres = sb("cres", [P, S, D])
        qT = sb("qT", [P, B, S])
        kT = sb("kT", [P, B, S])
        bqkv = sb("bqkv", [P, 3])
        with ExitStack() as cond:
            cwh = sb("cwh", [P, CW], F32R, cond)
            cwl = sb("cwl", [P, CW], F32R, cond)
            with ExitStack() as layer0:
                nrm = sb("nrm", [P, S, D], stack=layer0)
                w1h = sb("w1h", [P, LA], F32R, layer0)
                w1l = sb("w1l", [P, LA], F32R, layer0)
                w2h = sb("w2h", [P, 3, D], F32R, layer0)
                w2l = sb("w2l", [P, 3, D], F32R, layer0)
                bias1 = sb("bias1", [2 * LO, LA], F32R, layer0)
                tab = sb("tab", [2 * LO, 3, D], F32R, layer0)
                lang1h = sb("lang1h", [2 * LO, B], F32R, layer0)
                gb = sb("gb", [P, 2, D], stack=layer0)
                wgq = sb("wgq", [P, INNER], BF16, layer0)
                wuq = sb("wuq", [P, INNER], BF16, layer0)
                wdq = sb("wdq", [P, KF, D], BF16, layer0)
                wsc = sb("wsc", [P, 3], stack=layer0)

                KT = [(0, P), (P, P), (2 * P, LA - 2 * P)]
                setup(nc, a, sb, pb, sem, x1, ident, tri, ones, hmask, type_slot, type_of_tile, xs_dram,
                      w1h, w1l, w2h, w2l, bias1, tab, lang1h, gb, wgq, wuq, wdq, wsc, KT)
                adapter(nc, a, sb, pb, sem, x1, ident, nrm, w1h, w1l, w2h, w2l, bias1, tab, lang1h, gb, KT)
                if dump == "A":
                    dump_out(nc, sem, out, nrm)
                    return
                quantised_ffn(nc, a, sb, pb, sem, x1, ident, nrm, wgq, wuq, wdq, wsc, type_slot, xs_dram, cwh, cwl)
                if dump == "B":
                    dump_out(nc, sem, out, x1)
                    return
            typed_experts(nc, sb, pb, sem, ident, type_of_tile, xs_dram, eo_dram, cwh, cwl)
            shared_experts(nc, a, sb, pb, sem, x1, ident, type_slot, eo_dram, v_dram, cwh, cwl, cres, qT, kT, bqkv)
            if dump == "C":
                dump_out(nc, sem, out, cres)
                return
        reuse_semaphores()
        ms_dram = nc.dram_tensor("ms_dram", (ET * P, ROW), F32, kind="Internal").ap()
        y_dram = nc.dram_tensor("y_dram", (2 * T + ET * P, D), F32, kind="Internal").ap()
        mwh = sb("mwh", [P, MW], F32R)
        mwl = sb("mwl", [P, MW], F32R)
        attention(nc, a, sb, pb, sem, ident, hmask, qT, kT, bqkv, v_dram, att_dram, mwh, mwl)
        expert_of_tile = sb("expert_of_tile", [1, ET], I32)
        with ExitStack() as st:
            h2 = sb("h2", [P, S, ROW], stack=st)
            logits = sb("logits", [P, S, E], stack=st)
            second_norm(nc, a, sb, pb, sem, ident, x1, cres, att_dram, h2, logits, ms_dram)
            if dump == "D":
                dump_out(nc, sem, out, x1)
                return
            if dump == "h2":
                dump_out(nc, sem, out, h2[:, :, 0:D])
                return
            route(nc, a, sb, pb, sem, ones, tri, h2, logits, expert_of_tile, ms_dram)
        experts(nc, a, sb, pb, sem, ident, expert_of_tile, ms_dram, y_dram, mwh, mwl)
        combine(nc, sb, pb, sem, x1, y_dram, out)


def dump_out(nc, sem, out, t):
    done = sem("dumped")
    with nc.Block() as block:
        @block.sync
        def _(sp):
            sp.dma_start(out, t[:]).then_inc(done, 16)
            sp.wait_ge(done, 16)


def setup(nc, a, sb, pb, sem, x1, ident, tri, ones, hmask, type_slot, type_of_tile, xs_dram,
          w1h, w1l, w2h, w2l, bias1, tab, lang1h, gb, wgq, wuq, wdq, wsc, KT):
    with ExitStack() as st:
        w1 = sb("s_w1", [P, LA], stack=st)
        w2 = sb("s_w2", [P, 3, D], stack=st)
        braw = sb("s_braw", [2 * LO, LA], stack=st)
        traw = sb("s_traw", [2 * LO, 3, D], stack=st)
        bhi = sb("s_bhi", [2 * LO, LA], F32R, st)
        thi = sb("s_thi", [2 * LO, 3, D], F32R, st)
        ids = sb("s_ids", [2 * LO, B], I32, st)
        idf = sb("s_idf", [2 * LO, B], stack=st)
        ty = sb("s_ty", [P, 1], I32, st)
        tyf = sb("s_tyf", [P, 1], stack=st)
        consts = sb("s_consts", [P, 3 * P + HG + 1 + TYPES + S + TT], stack=st)
        ffw = sb("s_ffw", [P, 3, INNER], stack=st)
        tot = sb("s_tot", [P, 3], stack=st)
        msc = sb("s_msc", [P, 3], stack=st)
        inv = sb("s_inv", [P, 3], stack=st)
        rnd = sb("s_rnd", [P, 3, INNER], stack=st)
        t1h = sb("s_t1h", [P, TYPES], stack=st)
        cnt = sb("s_cnt", [P, TYPES], stack=st)
        cnti = sb("s_cnti", [P, TYPES], I32, st)
        cnts = sb("s_cnts", [P, TYPES], I32, st)
        padf = sb("s_padf", [P, TYPES], stack=st)
        zero = sb("s_zero", [P, D], stack=st)
        endt = sb("s_endt", [P, TYPES], stack=st)
        offs = sb("s_offs", [P, TYPES], stack=st)
        slot = sb("s_slot", [P, TYPES], stack=st)
        slotw = sb("s_slotw", [P, TYPES], stack=st)
        slot1 = sb("s_slot1", [P, 1], stack=st)
        row1 = sb("s_row1", [P, 1], stack=st)
        tslot = sb("s_tslot", [P, S], stack=st)
        past = sb("s_past", [1, TYPES - 1, TT], stack=st)
        totile = sb("s_totile", [1, TT], stack=st)
        ps = pb("s_ps", [P, 512], stack=st)
        ps2 = pb("s_ps2", [P, 512], stack=st)
        ps3 = pb("s_ps3", [P, 512], stack=st)
        ps4 = pb("s_ps4", [P, 512], stack=st)
        ld_x, ld_w, ld_t, ld_f, ld_c = (sem(n, st) for n in ("ld_x", "ld_w", "ld_t", "ld_f", "ld_c"))
        cleared, rows_cleared, diag, sums, means, onehot, tabs, ranks, ty1h, step, gbd = (
            sem("s_" + n, st) for n in
            ("cleared", "rows_cleared", "diag", "sums", "means", "onehot", "tabs", "ranks", "ty1h", "step", "gbd"))
        pool_step = sem("s_pool_step", st)
        C_I, C_T, C_1, C_H, C_M, C_P, C_S, C_J = np.cumsum([0, P, P, P, HG, 1, TYPES, S]).tolist()

        with nc.Block() as block:
            @block.sync
            def _(sp):
                sp.dma_start(consts[:], a["consts"]).then_inc(ld_c, 16)
                sp.dma_start(w1[:], a["W1"]).then_inc(ld_w, 16)
                for k, (o, n) in enumerate(KT):
                    sp.dma_start(w2[0:n, k, :], a["W2"][o:o + n, :]).then_inc(ld_w, 16)
                for n, name in enumerate(("w_gate", "w_up", "w_down")):
                    sp.dma_start(ffw[:, n, :], a[name]).then_inc(ld_f, 16)
                sp.wait_ge(cleared, 1)
                for j in range(TT):
                    sp.dma_start(xs_dram[j * P:(j + 1) * P, :], zero[:]).then_inc(rows_cleared, 16)
                sp.wait_ge(rows_cleared, 16 * TT)
                sp.wait_ge(ld_x, 16 * 4)

            @block.scalar
            def _(act):
                act.dma_start(ty[:], a["types"]).then_inc(ld_t, 16)
                act.dma_start(ids[:], a["langs"].to_broadcast([2 * LO, B])).then_inc(ld_t, 16)
                act.wait_ge(cleared, 2)
                for r in (0, LO):
                    act.dma_start(braw[r:r + LANG, :], a["b1"].to_broadcast([LANG, LA])).then_inc(ld_t, 16)
                    act.dma_start(traw[r:r + LANG, :, :], a["tab"]).then_inc(ld_t, 16)
                for q in range(4):
                    act.dma_start(x1[:, q * 8:(q + 1) * 8, :], a["x"][:, q * 8:(q + 1) * 8, :]).then_inc(ld_x, 16)

            @block.gpsimd
            def _(pool):
                pool.memset(zero[:], 0.0).then_inc(cleared, 1)
                pool.memset(braw[:], 0.0)
                pool.memset(traw[:], 0.0).then_inc(cleared, 1)
                pool.wait_ge(ld_t, 16 * 6)
                for n, r in enumerate((0, LO)):
                    v = braw[r:r + LO, :].rearrange("p (l c) -> p l c", l=LANG)
                    pool.affine_select(out=v, in_=v, compare_op=ALU.is_equal, fill=OFF if n == 0 else 0.0, base=0,
                                       pattern=[[-1, LANG], [0, AD]], channel_multiplier=1).then_inc(diag, 1)
                    pool.wait_ge(diag, n + 1)
                pool.wait_ge(ld_w, 16 * 4)
                pool.tensor_copy(w1h[:], w1[:]).then_inc(pool_step, 1)
                pool.wait_ge(pool_step, 1)
                pool.tensor_tensor(w1l[:], w1[:], w1h[:].bitcast(F32), ALU.subtract).then_inc(pool_step, 1)
                pool.wait_ge(pool_step, 2)
                for k, (o, n) in enumerate(KT):
                    pool.tensor_copy(w2h[0:n, k, :], w2[0:n, k, :]).then_inc(pool_step, 1)
                    pool.wait_ge(pool_step, 2 * k + 3)
                    pool.tensor_tensor(w2l[0:n, k, :], w2[0:n, k, :], w2h[0:n, k, :].bitcast(F32), ALU.subtract)\
                        .then_inc(pool_step, 1)
                    pool.wait_ge(pool_step, 2 * k + 4)

            @block.vector
            def _(dve):
                done = [0]

                def link(ins):
                    done[0] += 1
                    ins.then_inc(step, 1)
                    dve.wait_ge(step, done[0])

                dve.wait_ge(ld_c, 16)
                nc.vector.tensor_copy(ident[:], consts[:, C_I:C_T])
                nc.vector.tensor_copy(tri[:], consts[:, C_T:C_1])
                nc.vector.tensor_copy(hmask[:], consts[:, C_H:C_M])
                link(nc.vector.tensor_copy(ones[:], consts[:, C_1:C_H]))
                dve.wait_ge(ld_t, 16 * 6)
                link(nc.vector.tensor_copy(tyf[:], ty[:]))
                link(nc.vector.tensor_scalar(t1h[:], consts[:, C_P:C_S], tyf[:, 0:1], None, ALU.is_equal))
                nc.vector.memset(endt[:], 0.0).then_inc(ty1h, 1)
                link(nc.vector.tensor_copy(idf[:], ids[:]))
                nc.vector.tensor_scalar(lang1h[:], idf[:], consts[0:2 * LO, C_M:C_P], None, ALU.is_equal)
                nc.vector.tensor_copy(thi[:], traw[:])
                dve.wait_ge(diag, 2)
                link(nc.vector.tensor_copy(bhi[:], braw[:]))
                nc.vector.tensor_copy(tab[0:LO], thi[0:LO].bitcast(F32))
                nc.vector.tensor_copy(bias1[0:LO, :], bhi[0:LO, :].bitcast(F32))
                nc.vector.tensor_tensor(tab[LO:2 * LO], traw[LO:2 * LO], thi[LO:2 * LO].bitcast(F32), ALU.subtract)
                nc.vector.tensor_tensor(bias1[LO:2 * LO, :], braw[LO:2 * LO, :], bhi[LO:2 * LO, :].bitcast(F32),
                                        ALU.subtract).then_inc(tabs, 1)
                dve.wait_ge(ld_f, 16 * 3)
                nc.vector.tensor_reduce(tot[:], ffw[:], AX, ALU.add, apply_absolute_value=True).then_inc(sums, 1)
                dve.wait_ge(means, 1)
                link(nc.vector.tensor_scalar(msc[:], ps[:, 0:3], 1.0 / (D * INNER), 1e-5, ALU.mult, ALU.max))
                link(nc.vector.tensor_scalar(wsc[:], msc[:], 1.0 / 127.0, None, ALU.mult))
                link(nc.vector.reciprocal(inv[:], msc[:]))
                for n in range(3):
                    link(nc.vector.tensor_scalar(rnd[:, n, :], ffw[:, n, :], inv[:, n:n + 1], MAGIC, ALU.mult, ALU.add))
                link(nc.vector.tensor_scalar(rnd[:], rnd[:], MAGIC - 1.0, MAGIC + 1.0, ALU.max, ALU.min))
                for n, q in enumerate((wgq[:], wuq[:], wdq[:].rearrange("p k d -> p (k d)"))):
                    link(nc.vector.tensor_scalar(q, rnd[:, n, :], MAGIC, None, ALU.subtract))
                dve.wait_ge(ranks, 1)
                link(nc.vector.tensor_scalar(cnt[:], ps2[:, 0:TYPES], float(BT - 1), None, ALU.add))
                link(nc.vector.tensor_copy(cnti[:], cnt[:]))
                link(nc.vector.tensor_scalar(cnts[:], cnti[:], 2, 2, ALU.logical_shift_right, ALU.logical_shift_left))
                link(nc.vector.tensor_copy(padf[:], cnts[:]))
                link(nc.vector.tensor_copy(endt[:, 0:1], padf[:, 0:1]))
                for n in range(1, TYPES):
                    link(nc.vector.tensor_tensor(endt[:, n:n + 1], endt[:, n - 1:n], padf[:, n:n + 1], ALU.add))
                link(nc.vector.tensor_tensor(offs[:], endt[:], padf[:], ALU.subtract))
                link(nc.vector.tensor_tensor(slot[:], offs[:], ps3[:, 0:TYPES], ALU.add))
                link(nc.vector.tensor_tensor(slotw[:], slot[:], t1h[:], ALU.mult))
                link(nc.vector.tensor_reduce(slot1[:], slotw[:], AX, ALU.add))
                link(nc.vector.tensor_scalar(row1[:], slot1[:], float(S), None, ALU.mult))
                link(nc.vector.tensor_scalar(tslot[:], consts[:, C_S:C_J], row1[:, 0:1], None, ALU.add))
                nc.vector.tensor_copy(type_slot[:], tslot[:])
                for n in range(TYPES - 1):
                    link(nc.vector.tensor_scalar(past[0:1, n, :], consts[0:1, C_J:C_J + TT], endt[0:1, n:n + 1], None,
                                                 ALU.is_ge))
                link(nc.vector.tensor_reduce(totile[0:1, :], past[0:1, :, :].rearrange("p n j -> p j n"), AX, ALU.add))
                link(nc.vector.tensor_copy(type_of_tile[0:1, :], totile[0:1, :]))
                dve.wait_ge(gbd, 1)
                link(nc.vector.tensor_copy(gb[:], ps4[:, 0:2 * D].rearrange("p (n d) -> p n d", n=2)))

            @block.tensor
            def _(pe):
                pe.wait_ge(ty1h, 1)
                nc.tensor.matmul(ps2[:, 0:TYPES], ones[:], t1h[:], start=True, stop=True)
                nc.tensor.matmul(ps3[:, 0:TYPES], tri[:], t1h[:], start=True, stop=True).then_inc(ranks, 1)
                pe.wait_ge(tabs, 1)
                nc.tensor.matmul(ps4[:, 0:2 * D], lang1h[:], tab[:, 0:2, :], start=True, stop=True).then_inc(gbd, 1)
                pe.wait_ge(sums, 1)
                nc.tensor.matmul(ps[:, 0:3], ones[:], tot[:], start=True, stop=True).then_inc(means, 1)


def adapter(nc, a, sb, pb, sem, x1, ident, nrm, w1h, w1l, w2h, w2l, bias1, tab, lang1h, gb, KT):
    with ExitStack() as st:
        xin = sb("a_xin", [P, 2, SB, D], stack=st)
        xh = sb("a_xh", [P, W], F32R, st)
        xl = sb("a_xl", [P, W], F32R, st)
        hh = sb("a_hh", [P, 3, W], F32R, st)
        hl = sb("a_hl", [P, 3, W], F32R, st)
        y = sb("a_y", [P, SB, D], stack=st)
        bs = sb("a_bs", [P, SB, 6], stack=st)
        mv = sb("a_mv", [P, SB, 2], stack=st)
        ve = sb("a_ve", [P, SB], stack=st)
        rs = sb("a_rs", [P, SB], stack=st)
        half = sb("a_half", [P, SB], stack=st)
        nm = sb("a_nm", [P, SB, D], stack=st)
        ng = sb("a_ng", [P, SB, D], stack=st)
        pT = pb("a_pT", [P, W], stack=st)
        pz = [pb(f"a_pz{k}", [P, W], stack=st) for k in range(3)]
        pa = pb("a_pa", [P, SB, D], stack=st)
        x_turned, xh_made, xl_made, z_made, hh_made, hl_made, a_made, y_made, mv_made, ve_made, rs_made, nm_made, \
            ng_made, out_made, stats = (sem("a_" + n, st) for n in (
                "x_turned", "xh_made", "xl_made", "z_made", "hh_made", "hl_made", "a_made", "y_made", "mv_made",
                "ve_made", "rs_made", "nm_made", "ng_made", "out_made", "stats"))
        halfed = sem("a_halfed", st)
        x_loaded = [sem(f"a_x_loaded{q}", st) for q in range(2)]

        with nc.Block() as block:
            @block.tensor
            def _(pe):
                def block_of(j, i, q):
                    pe.wait_ge(x_loaded[q], 16 * j + 16)
                    pe.wait_ge(xl_made, i)
                    for u in range(SB):
                        last = nc.tensor.transpose(pT[:, u * D:(u + 1) * D], xin[:, q, u, :], ident[:])
                    last.then_inc(x_turned, 1)
                    pe.wait_ge(xh_made, i + 1)
                    pe.wait_ge(xl_made, i + 1)
                    for k, (o, n) in enumerate(KT):
                        pe.wait_ge(hl_made, 3 * i)
                        nc.tensor.matmul(pz[k][0:n, :], w1h[:, o:o + n], xh[:], start=True, stop=False)
                        nc.tensor.matmul(pz[k][0:n, :], w1h[:, o:o + n], xl[:], start=False, stop=False)
                        nc.tensor.matmul(pz[k][0:n, :], w1l[:, o:o + n], xh[:], start=False, stop=False)
                        nc.tensor.matmul(pz[k][0:n, :], bias1[:, o:o + n],
                                         lang1h[:, None, :].to_broadcast([2 * LO, SB, B]),
                                         start=False, stop=True).then_inc(z_made, 1)
                    pe.wait_ge(hh_made, 3 * i + 3)
                    pe.wait_ge(hl_made, 3 * i + 3)
                    pe.wait_ge(y_made, i)
                    for u in range(SB):
                        c = slice(u * D, (u + 1) * D)
                        for k, (o, n) in enumerate(KT):
                            nc.tensor.matmul(pa[:, u, :], hh[0:n, k, c], w2h[0:n, k, :], start=(k == 0), stop=False)
                            nc.tensor.matmul(pa[:, u, :], hl[0:n, k, c], w2h[0:n, k, :], start=False, stop=False)
                            nc.tensor.matmul(pa[:, u, :], hh[0:n, k, c], w2l[0:n, k, :], start=False, stop=False)
                        last = nc.tensor.matmul(pa[:, u, :], lang1h[:], tab[:, 2, :], start=False, stop=True)
                    last.then_inc(a_made, 1)

                with pe.Fori(0, NB // 2) as j:
                    for q in range(2):
                        block_of(j, 2 * j + q, q)

            @block.sync
            def _(sp):
                for q in range(2):
                    sp.dma_start(xin[:, q], a["x"][:, q * SB:(q + 1) * SB, :]).then_inc(x_loaded[q], 16)
                with sp.Fori(1, NB // 2) as j:
                    for q in range(2):
                        sp.wait_ge(x_turned, 2 * j + q - 1)
                        sp.dma_start(xin[:, q], a["x"][:, bass.ds((2 * j + q) * SB, SB), :]).then_inc(x_loaded[q], 16)

            @block.scalar
            def _(act):
                with act.Fori(0, NB) as i:
                    act.wait_ge(x_turned, i + 1)
                    act.wait_ge(z_made, 3 * i)
                    nc.scalar.activation(xh[:], pT[:], ACT.Copy).then_inc(xh_made, 1)
                    act.wait_ge(a_made, i)
                    for k, (o, n) in enumerate(KT):
                        act.wait_ge(z_made, 3 * i + k + 1)
                        nc.scalar.activation(hh[0:n, k, :], pz[k][0:n, :], ACT.Relu).then_inc(hh_made, 1)

            @block.gpsimd
            def _(pool):
                pool.memset(half[:], -0.5).then_inc(halfed, 1)
                pool.wait_ge(halfed, 1)
                with pool.Fori(0, NB) as i:
                    pool.wait_ge(ve_made, i + 1)
                    pool.wait_ge(nm_made, i)
                    pool.tensor_tensor(rs[:], ve[:], half[:], ALU.pow).then_inc(rs_made, 1)
                    pool.wait_ge(nm_made, i + 1)
                    pool.tensor_tensor(ng[:], nm[:], gb[:, 0:1, :].to_broadcast([P, SB, D]), ALU.mult).then_inc(ng_made, 1)
                    pool.wait_ge(ng_made, i + 1)
                    pool.tensor_tensor(nrm[:, bass.ds(i * SB, SB), :], ng[:], gb[:, 1:2, :].to_broadcast([P, SB, D]),
                                       ALU.add).then_inc(out_made, 1)

            @block.vector
            def _(dve):
                def products(i):
                    dve.wait_ge(xh_made, i + 1)
                    nc.vector.tensor_tensor(xl[:], pT[:], xh[:].bitcast(F32), ALU.subtract).then_inc(xl_made, 1)
                    for k, (o, n) in enumerate(KT):
                        dve.wait_ge(hh_made, 3 * i + k + 1)
                        nc.vector.scalar_tensor_tensor(hl[0:n, k, :], pz[k][0:n, :], 0.0, hh[0:n, k, :].bitcast(F32),
                                                       ALU.max, ALU.subtract).then_inc(hl_made, 1)

                def statistics(i):
                    dve.wait_ge(a_made, i + 1)
                    nc.vector.tensor_tensor(y[:], pa[:], x1[:, bass.ds(i * SB, SB), :], ALU.add).then_inc(y_made, 1)
                    carry(dve, a_made)
                    dve.wait_ge(y_made, i + 1)
                    for u in range(SB):
                        last = nc.vector.bn_stats(bs[:, u, :], y[:, u, :])
                    last.then_inc(stats, 1)
                    carry(dve, y_made)
                    dve.wait_ge(stats, i + 1)
                    for u in range(SB):
                        last = nc.vector.bn_aggr(mv[:, u, :], bs[:, u, :])
                    last.then_inc(mv_made, 1)
                    dve.wait_ge(mv_made, i + 1)
                    dve.wait_ge(rs_made, i)
                    nc.vector.tensor_scalar(ve[:], mv[:, :, 1], EPS, None, ALU.add).then_inc(ve_made, 1)

                def normalise(i):
                    dve.wait_ge(rs_made, i + 1)
                    dve.wait_ge(ng_made, i)
                    for u in range(SB):
                        last = nc.vector.tensor_scalar(nm[:, u, :], y[:, u, :], mv[:, u, 0:1],
                                                       rs[:, u:u + 1], ALU.subtract, ALU.mult)
                    last.then_inc(nm_made, 1)

                with dve.Fori(0, NB) as i:
                    products(i)
                    statistics(i)
                    normalise(i)


def quantised_ffn(nc, a, sb, pb, sem, x1, ident, nrm, wgq, wuq, wdq, wsc, type_slot, xs_dram, cwh, cwl):
    with ExitStack() as st:
        amx = sb("b_amx", [P, S], stack=st)
        sc = sb("b_sc", [P, S], stack=st)
        qs = sb("b_qs", [P, S], stack=st)
        sg = sb("b_sg", [P, S], stack=st)
        su = sb("b_su", [P, S], stack=st)
        xq = sb("b_xq", [P, SB, D], stack=st)
        xqT = sb("b_xqT", [P, 2, W], BF16, st)
        g = sb("b_g", [P, 2, INNER], stack=st)
        m = sb("b_m", [P, 2, 2, INNER], stack=st)
        mq = sb("b_mq", [P, 2, INNER], stack=st)
        mqT = sb("b_mqT", [P, 2, INNER], BF16, st)
        magic = sb("b_magic", [P, 1], stack=st)
        raw = sb("b_raw", [P, 2, CH], stack=st)
        raw_loaded = [sem(f"b_raw_loaded{q}", st) for q in range(2)]
        parted = sem("b_parted", st)
        am2 = sb("b_am2", [P, 2], stack=st)
        sc2 = sb("b_sc2", [P, 2], stack=st)
        qs2 = sb("b_qs2", [P, 2, 2], stack=st)
        sd = sb("b_sd", [P, 2, 2], stack=st)
        pT = pb("b_pT", [P, SB, D], stack=st)
        pg = pb("b_pg", [P, 2, INNER], stack=st)
        pu = pb("b_pu", [P, 2, INNER], stack=st)
        pm = [pb(f"b_pm{u}", [P, INNER], stack=st) for u in range(2)]
        po = pb("b_po", [P, 2, D], stack=st)
        xq_made, xq_turned, xqT_made, g_prod, u_prod, g_made, m_made, am_made, qs_made, mq_made, mqc_made, m_turned, \
            mqT_made, o_made, x1_made, step, sent = (sem("b_" + n, st) for n in (
                "xq_made", "xq_turned", "xqT_made", "g_prod", "u_prod", "g_made", "m_made", "am_made", "qs_made",
                "mq_made", "mqc_made", "m_turned", "mqT_made", "o_made", "x1_made", "step", "sent"))
        xq_raw = sem("b_xq_raw", st)
        NP2 = S // 2

        with nc.Block() as block:
            @block.tensor
            def _(pe):
                def turn(i):
                    pe.wait_ge(xq_made, i + 1)
                    pe.wait_ge(xqT_made, i)
                    for u in range(SB):
                        last = nc.tensor.transpose(pT[:, u, :], xq[:, u, :], ident[:])
                    last.then_inc(xq_turned, 1)

                def up(p, b2, h):
                    for n in range(2):
                        c = slice((2 * h + n) * D, (2 * h + n + 1) * D)
                        if n == 0:
                            pe.wait_ge(g_made, 2 * p)
                        nc.tensor.matmul(pg[:, n, :], xqT[:, b2, c], wgq[:], start=True, stop=True).then_inc(g_prod, 1)
                        if n == 0:
                            pe.wait_ge(m_made, 2 * p)
                        nc.tensor.matmul(pu[:, n, :], xqT[:, b2, c], wuq[:], start=True, stop=True).then_inc(u_prod, 1)

                def down(p):
                    for n in range(2):
                        pe.wait_ge(mqc_made, p + 1)
                        pe.wait_ge(mqT_made, 2 * p + n)
                        if n == 0:
                            pe.wait_ge(mqT_made, 2 * p)
                        for k in range(KF):
                            last = nc.tensor.transpose(pm[n][:, k * P:(k + 1) * P], mq[:, n, k * P:(k + 1) * P], ident[:])
                        last.then_inc(m_turned, 1)
                    pe.wait_ge(x1_made, p)
                    for n in range(2):
                        pe.wait_ge(mqT_made, 2 * p + n + 1)
                        for k in range(KF):
                            last = nc.tensor.matmul(po[:, n, :], mqT[:, n, k * P:(k + 1) * P], wdq[:, k, :],
                                                    start=(k == 0), stop=(k == KF - 1))
                    last.then_inc(o_made, 1)

                turn(0)
                pe.wait_ge(xqT_made, 1)
                up(0, 0, 0)
                with pe.Fori(0, NB - 1) as i:
                    up(2 * i + 1, i % 2, 1)
                    down(2 * i)
                    turn(i + 1)
                    pe.wait_ge(xqT_made, i + 2)
                    up(2 * i + 2, (i + 1) % 2, 0)
                    down(2 * i + 1)
                up(NP2 - 1, (NB - 1) % 2, 1)
                down(NP2 - 2)
                down(NP2 - 1)

            @block.scalar
            def _(act):
                def turned(i):
                    act.wait_ge(xq_turned, i + 1)
                    act.activation(xqT[:, i % 2, :], pT[:].rearrange("p u d -> p (u d)"), ACT.Copy, bias=-MAGIC)\
                       .then_inc(xqT_made, 1)

                def gate(p, b2, h):
                    for n in range(2):
                        act.wait_ge(g_prod, 2 * p + n + 1)
                        act.wait_ge(m_made, 2 * p + n)
                        if n == 0:
                            act.wait_ge(m_made, 2 * p)
                        act.activation(g[:, n, :], pg[:, n, :], ACT.Silu, scale=sg[:, bass.ds(2 * p + n, 1)])\
                           .then_inc(g_made, 1)

                def quantise(p):
                    act.wait_ge(qs_made, p + 1)
                    act.wait_ge(m_turned, 2 * p)
                    for n in range(2):
                        act.activation(mq[:, n, :], m[:, p % 2, n, :], ACT.Identity, bias=magic[:],
                                       scale=qs2[:, p % 2, n:n + 1]).then_inc(mq_made, 1)

                def turned_back(p):
                    for n in range(2):
                        act.wait_ge(m_turned, 2 * p + n + 1)
                        if n == 0:
                            act.wait_ge(o_made, p)
                        act.activation(mqT[:, n, :], pm[n][:], ACT.Copy, bias=-MAGIC).then_inc(mqT_made, 1)

                turned(0)
                gate(0, 0, 0)
                with act.Fori(0, NB - 1) as i:
                    quantise(2 * i)
                    gate(2 * i + 1, i % 2, 1)
                    turned_back(2 * i)
                    turned(i + 1)
                    quantise(2 * i + 1)
                    gate(2 * i + 2, (i + 1) % 2, 0)
                    turned_back(2 * i + 1)
                quantise(NP2 - 2)
                gate(NP2 - 1, (NB - 1) % 2, 1)
                turned_back(NP2 - 2)
                quantise(NP2 - 1)
                turned_back(NP2 - 1)

            @block.vector
            def _(dve):
                def link(ins, n):
                    ins.then_inc(step, 1)
                    dve.wait_ge(step, n)

                link(nc.vector.memset(magic[:], MAGIC), 1)
                link(nc.vector.tensor_reduce(amx[:], nrm[:], AX, ALU.max, apply_absolute_value=True), 2)
                link(nc.vector.tensor_scalar(sc[:], amx[:], 1e-5, 1.0 / 127.0, ALU.max, ALU.mult), 3)
                link(nc.vector.reciprocal(qs[:], sc[:]), 4)
                nc.vector.tensor_scalar(sg[:], sc[:], wsc[:, 0:1], 127.0, ALU.mult, ALU.mult)
                link(nc.vector.tensor_scalar(su[:], sc[:], wsc[:, 1:2], 127.0, ALU.mult, ALU.mult), 5)

                def rows(i):
                    dve.wait_ge(xq_turned, i)
                    for u in range(SB):
                        last = nc.vector.tensor_scalar(xq[:, u, :], nrm[:, i * SB + u, :],
                                                       qs[:, bass.ds(i * SB + u, 1)], MAGIC, ALU.mult, ALU.add)
                    last.then_inc(xq_raw, 1)
                    dve.wait_ge(xq_raw, i + 1)
                    nc.vector.tensor_scalar(xq[:], xq[:], MAGIC - 128.0, MAGIC + 127.0,
                                            ALU.max, ALU.min).then_inc(xq_made, 1)

                def inner(p):
                    for n in range(2):
                        dve.wait_ge(g_made, 2 * p + n + 1)
                        dve.wait_ge(u_prod, 2 * p + n + 1)
                        nc.vector.scalar_tensor_tensor(m[:, p % 2, n, :], pu[:, n, :], su[:, bass.ds(2 * p + n, 1)],
                                                       g[:, n, :], ALU.mult, ALU.mult).then_inc(m_made, 1)
                    dve.wait_ge(m_made, 2 * p + 2)
                    nc.vector.tensor_reduce(am2[:], m[:, p % 2], AX, ALU.max, apply_absolute_value=True).then_inc(am_made, 1)
                    dve.wait_ge(am_made, 3 * p + 1)
                    nc.vector.tensor_scalar(sc2[:], am2[:], 1e-5, 1.0 / 127.0, ALU.max, ALU.mult).then_inc(am_made, 1)
                    dve.wait_ge(am_made, 3 * p + 2)
                    nc.vector.reciprocal(qs2[:, p % 2, :], sc2[:]).then_inc(qs_made, 1)
                    nc.vector.tensor_scalar(sd[:, p % 2, :], sc2[:], wsc[:, 2:3], 127.0, ALU.mult, ALU.mult)\
                        .then_inc(am_made, 1)

                def clamp(p):
                    dve.wait_ge(mq_made, 2 * p + 2)
                    nc.vector.tensor_scalar(mq[:], mq[:], MAGIC - 128.0, MAGIC + 127.0, ALU.max, ALU.min)\
                        .then_inc(mqc_made, 1)

                def residual(p):
                    dve.wait_ge(o_made, p + 1)
                    dve.wait_ge(am_made, 3 * p + 3)
                    for n in range(2):
                        v = x1[:, 2 * p + n, :]
                        last = nc.vector.scalar_tensor_tensor(v, po[:, n, :], sd[:, p % 2, n:n + 1], v, ALU.mult, ALU.add)
                    last.then_inc(x1_made, 1)

                rows(0)
                inner(0)
                with dve.Fori(0, NB - 1) as i:
                    clamp(2 * i)
                    rows(i + 1)
                    inner(2 * i + 1)
                    residual(2 * i)
                    clamp(2 * i + 1)
                    inner(2 * i + 2)
                    residual(2 * i + 1)
                clamp(NP2 - 2)
                inner(NP2 - 1)
                residual(NP2 - 2)
                clamp(NP2 - 1)
                residual(NP2 - 1)

            @block.sync
            def _(sp):
                for n in range(CW // CH):
                    if n >= 2:
                        sp.wait_ge(parted, 2 * n - 2)
                    sp.dma_start(raw[:, n % 2, :], a["cw"][:, n * CH:(n + 1) * CH]).then_inc(raw_loaded[n % 2], 16)

            @block.gpsimd
            def _(pool):
                def part(n):
                    c = slice(n * CH, (n + 1) * CH)
                    pool.wait_ge(raw_loaded[n % 2], 16 * (n // 2 + 1))
                    pool.tensor_copy(cwh[:, c], raw[:, n % 2, :]).then_inc(parted, 1)
                    pool.wait_ge(parted, 2 * n + 1)
                    pool.tensor_tensor(cwl[:, c], raw[:, n % 2, :], cwh[:, c].bitcast(F32), ALU.subtract).then_inc(parted, 1)
                    pool.wait_ge(parted, 2 * n + 2)

                for s in range(S):
                    if s % 4 == 0 and s // 4 < CW // CH:
                        part(s // 4)
                    pool.wait_ge(x1_made, s // 2 + 1)
                    pool.indirect_dma_start(xs_dram, bass.IndirectOffsetOnAxis(ap=type_slot[:, s:s + 1], axis=0),
                                            x1[:, s, :], None).then_inc(sent, 16)
                pool.wait_ge(sent, 16 * S)


def carry(eng, signal):
    eng.wait_ge(signal, 1)


def after(eng, signal, value):
    if not (isinstance(value, int) and value <= 0):
        eng.wait_ge(signal, value)


def typed_experts(nc, sb, pb, sem, ident, type_of_tile, xs_dram, eo_dram, cwh, cwl):
    with ExitStack() as st:
        xs = sb("e_xs", [P, 2, D], stack=st)
        xh = sb("e_xh", [P, P], F32R, st)
        xl = sb("e_xl", [P, P], F32R, st)
        r = sb("e_r", [P, 2, FF], stack=st)
        hh = sb("e_hh", [P, FF], F32R, st)
        hl = sb("e_hl", [P, FF], F32R, st)
        y = sb("e_y", [P, 2, D], stack=st)
        pT = pb("e_pT", [P, P], stack=st)
        pz = [pb(f"e_pz{q}", [P, FF], stack=st) for q in range(2)]
        pt = [pb(f"e_pt{q}", [P, FF], stack=st) for q in range(2)]
        py = [pb(f"e_py{q}", [P, 512], stack=st) for q in range(2)]
        loaded = [sem(f"e_loaded{q}", st) for q in range(2)]
        stored = [sem(f"e_stored{q}", st) for q in range(2)]
        x_turned, xh_made, xl_made, z_made, r_made, r_turned, hh_made, hl_made, y_summed, y_made = (
            sem("e_" + n, st) for n in ("x_turned", "xh_made", "xl_made", "z_made", "r_made", "r_turned", "hh_made",
                                        "hl_made", "y_summed", "y_made"))
        LAST = TT // 2 - 1

        def pairs(eng, step):
            for q in range(2):
                step(0, q, q)
            with eng.Fori(1, LAST) as jj:
                for q in range(2):
                    step(jj, 2 * jj + q, q)
            for q in range(2):
                step(LAST, 2 * LAST + q, q)

        with nc.Block() as block:
            @block.sync
            def _(sp):
                for q in range(2):
                    sp.dma_start(xs[:, q], xs_dram[q * P:(q + 1) * P, :]).then_inc(loaded[q], 16)

                def step(jj, j, q):
                    if not (isinstance(jj, int) and jj == LAST):
                        sp.wait_ge(x_turned, j + 1)
                        sp.dma_start(xs[:, q], xs_dram[bass.ds((j + 2) * P, P), :]).then_inc(loaded[q], 16)
                    sp.wait_ge(y_made, j + 1)
                    sp.dma_start(eo_dram[bass.ds(j * P, P), :], y[:, q]).then_inc(stored[q], 16)

                pairs(sp, step)
                for q in range(2):
                    sp.wait_ge(stored[q], 16 * (TT // 2))

            @block.tensor
            def _(pe):
                def turn(jj, j, q):
                    pe.wait_ge(loaded[q], 16 * jj + 16)
                    after(pe, xl_made, j)
                    nc.tensor.transpose(pT[:], xs[:, q], ident[:]).then_inc(x_turned, 1)

                def first(j, q):
                    e = pe.value_load(type_of_tile[0:1, bass.ds(j, 1)], min_val=0, max_val=TYPES - 1)
                    pe.wait_ge(xl_made, j + 1)
                    after(pe, r_made, j - 1)
                    c = bass.ds(e * FF, FF)
                    nc.tensor.matmul(pz[q][:], xh[:], cwh[:, c], start=True, stop=False)
                    nc.tensor.matmul(pz[q][:], xh[:], cwl[:, c], start=False, stop=False)
                    nc.tensor.matmul(pz[q][:], xl[:], cwh[:, c], start=False, stop=True).then_inc(z_made, 1)

                def turn_hidden(j, q):
                    pe.wait_ge(r_made, j + 1)
                    after(pe, hl_made, j - 1)
                    for k in range(KF):
                        last = nc.tensor.transpose(pt[q][:, k * P:(k + 1) * P], r[:, q, k * P:(k + 1) * P], ident[:])
                    last.then_inc(r_turned, 1)

                def second(j, q):
                    e = pe.value_load(type_of_tile[0:1, bass.ds(j, 1)], min_val=0, max_val=TYPES - 1)
                    pe.wait_ge(hl_made, j + 1)
                    after(pe, y_made, j - 1)
                    for k in range(KF):
                        c = bass.ds(e * (KF * D) + (C_WO + k * D), D)
                        h = slice(k * P, (k + 1) * P)
                        nc.tensor.matmul(py[q][:, 0:D], hh[:, h], cwh[:, c], start=(k == 0), stop=False)
                        nc.tensor.matmul(py[q][:, 0:D], hh[:, h], cwl[:, c], start=False, stop=False)
                        last = nc.tensor.matmul(py[q][:, 0:D], hl[:, h], cwh[:, c], start=False, stop=(k == KF - 1))
                    last.then_inc(y_summed, 1)

                turn(0, 0, 0)

                def step(jj, j, q):
                    first(j, q)
                    if not (isinstance(jj, int) and jj == 0 and q == 0):
                        second(j - 1, 1 - q)
                    if not (isinstance(jj, int) and jj == LAST and q == 1):
                        turn(jj + q, j + 1, 1 - q)
                    turn_hidden(j, q)

                pairs(pe, step)
                second(TT - 1, 1)

            @block.scalar
            def _(act):
                def high(j):
                    act.wait_ge(x_turned, j + 1)
                    after(act, z_made, j)
                    act.activation(xh[:], pT[:], ACT.Copy).then_inc(xh_made, 1)

                high(0)

                def step(jj, j, q):
                    act.wait_ge(z_made, j + 1)
                    after(act, r_turned, j - 1)
                    act.activation(r[:, q], pz[q][:], ACT.Relu).then_inc(r_made, 1)
                    if not (isinstance(jj, int) and jj == LAST and q == 1):
                        high(j + 1)
                    act.wait_ge(r_turned, j + 1)
                    after(act, y_summed, j)
                    act.activation(hh[:], pt[q][:], ACT.Copy).then_inc(hh_made, 1)

                pairs(act, step)

            @block.vector
            def _(dve):
                def low(j):
                    dve.wait_ge(xh_made, j + 1)
                    nc.vector.tensor_tensor(xl[:], pT[:], xh[:].bitcast(F32), ALU.subtract).then_inc(xl_made, 1)

                def result(jj, j, q):
                    dve.wait_ge(y_summed, j + 1)
                    after(dve, stored[q], 16 * jj)
                    nc.vector.tensor_copy(y[:, q], py[q][:, 0:D]).then_inc(y_made, 1)

                low(0)

                def step(jj, j, q):
                    if not (isinstance(jj, int) and jj == LAST and q == 1):
                        low(j + 1)
                    if not (isinstance(jj, int) and jj == 0 and q == 0):
                        result(jj + q - 1, j - 1, 1 - q)
                    dve.wait_ge(hh_made, j + 1)
                    nc.vector.tensor_tensor(hl[:], pt[q][:], hh[:].bitcast(F32), ALU.subtract).then_inc(hl_made, 1)

                pairs(dve, step)
                result(LAST, TT - 1, 1)


def shared_experts(nc, a, sb, pb, sem, x1, ident, type_slot, eo_dram, v_dram, cwh, cwl, cres, qT, kT, bqkv):
    NF = NSH * KF
    with ExitStack() as st:
        wraw = sb("c_wraw", [P, 3 * D], stack=st)
        wgm = sb("c_wgm", [P, 3 * D], stack=st)
        wh = sb("c_wh", [P, 3 * D], F32R, st)
        wl = sb("c_wl", [P, 3 * D], F32R, st)
        lng = sb("c_lng", [P, 1], stack=st)
        lnb = sb("c_lnb", [P, 1], stack=st)
        braw = sb("c_braw", [P, 3], stack=st)
        g1 = sb("c_g1", [P, 3, D], stack=st)
        g2 = sb("c_g2", [P, 3], stack=st)
        gin = sb("c_gin", [P, 3, D], stack=st)
        gT = sb("c_gT", [P, 3, B], stack=st)
        gr = sb("c_gr", [P, B], stack=st)
        gmx = sb("c_gmx", [P, 1], stack=st)
        gx = sb("c_gx", [P, 3], stack=st)
        ge = sb("c_ge", [P, 3], stack=st)
        gs = sb("c_gs", [P, 1], stack=st)
        gi = sb("c_gi", [P, 1], stack=st)
        wgt = sb("c_wgt", [P, 3], stack=st)
        xb = sb("c_xb", [P, SB, D], stack=st)
        xh = sb("c_xh", [P, W], F32R, st)
        xl = sb("c_xl", [P, W], F32R, st)
        hh = sb("c_hh", [P, NF, W], F32R, st)
        hl = sb("c_hl", [P, NF, W], F32R, st)
        rows = sb("c_rows", [P, SB], I32, st)
        rows_made = sem("c_rows_made", st)
        eo = sb("c_eo", [P, SB, D], stack=st)
        t0 = sb("c_t0", [P, SB, D], stack=st)
        t1 = sb("c_t1", [P, SB, D], stack=st)
        bs = sb("c_bs", [P, SB, 6], stack=st)
        mv = sb("c_mv", [P, SB, 2], stack=st)
        ve = sb("c_ve", [P, SB], stack=st)
        rs = sb("c_rs", [P, SB], stack=st)
        half = sb("c_half", [P, SB], stack=st)
        nm = sb("c_nm", [P, SB, D], stack=st)
        nh = sb("c_nh", [P, W], F32R, st)
        nl = sb("c_nl", [P, W], F32R, st)
        v = sb("c_v", [P, SB, D], stack=st)
        pT = pb("c_pT", [P, W], stack=st)
        pz = [pb(f"c_pz{k}", [P, W], stack=st) for k in range(3)]
        py = [pb(f"c_py{n}", [P, SB, D], stack=st) for n in range(NSH)]
        pq = [pb(f"c_pq{n}", [P, W], stack=st) for n in range(2)]
        names = ("w_loaded wg_made wh_made wl_made bias_summed xb_made x_turned xh_made xl_made z_made hh_made hl_made "
                 "y_summed eo_loaded t0_made t1_made c_made stats mv_made ve_made rs_made nm_made n_turned nh_made "
                 "nl_made qk_summed qk_made v_summed v_made v_stored gin_made g_turned gT_made g_first gr_made g_second "
                 "gate_step ge_made halfed").split()
        s_ = {n: sem("c_" + n, st) for n in names}
        (w_loaded, wg_made, wh_made, wl_made, bias_summed, xb_made, x_turned, xh_made, xl_made, z_made, hh_made, hl_made,
         y_summed, eo_loaded, t0_made, t1_made, c_made, stats, mv_made, ve_made, rs_made, nm_made, n_turned, nh_made,
         nl_made, qk_summed, qk_made, v_summed, v_made, v_stored, gin_made, g_turned, gT_made, g_first, gr_made,
         g_second, gate_step, ge_made, halfed) = (s_[n] for n in names)

        with nc.Block() as block:
            @block.sync
            def _(sp):
                for dst, name in ((wraw[:], "w_qkv"), (lng[:], "ln1_g"), (lnb[:], "ln1_b"), (braw[:], "b_qkv"),
                                  (g1[:], "g1"), (g2[:], "g2")):
                    sp.dma_start(dst, a[name]).then_inc(w_loaded, 16)
                with sp.Fori(0, NB) as i:
                    sp.wait_ge(v_made, i + 1)
                    sp.dma_start(v_dram[:, bass.ds(i * SB, SB), :], v[:]).then_inc(v_stored, 16)
                sp.wait_ge(v_stored, 16 * NB)

            @block.gpsimd
            def _(pool):
                pool.memset(half[:], -0.5).then_inc(halfed, 1)
                pool.wait_ge(halfed, 1)

                def fetch(i):
                    after(pool, x_turned, i)
                    pool.tensor_copy(xb[:], x1[:, bass.ds(i * SB, SB), :]).then_inc(xb_made, 1)
                    after(pool, eo_loaded, 16 * SB * i)
                    pool.wait_ge(xb_made, i + 1)
                    pool.tensor_copy(rows[:], type_slot[:, bass.ds(i * SB, SB)]).then_inc(rows_made, 1)
                    carry(pool, xb_made)
                    pool.wait_ge(rows_made, i + 1)
                    after(pool, t0_made, i)
                    for u in range(SB):
                        pool.indirect_dma_start(eo[:, u, :], None, eo_dram,
                                                bass.IndirectOffsetOnAxis(ap=rows[:, u:u + 1], axis=0))\
                            .then_inc(eo_loaded, 16)

                def root(i):
                    pool.wait_ge(ve_made, i + 1)
                    after(pool, nm_made, i)
                    pool.tensor_tensor(rs[:], ve[:], half[:], ALU.pow).then_inc(rs_made, 1)

                fetch(0)
                with pool.Fori(0, NB - 1) as i:
                    fetch(i + 1)
                    root(i)
                root(NB - 1)

            @block.tensor
            def _(pe):
                pe.wait_ge(w_loaded, 16 * 6)
                for n in range(3):
                    last = nc.tensor.matmul(pz[0][:, n:n + 1], wraw[:, n * D:(n + 1) * D], lnb[:], start=True, stop=True)
                last.then_inc(bias_summed, 1)
                pe.wait_ge(wl_made, 1)

                def turn(i):
                    pe.wait_ge(xb_made, i + 1)
                    after(pe, v_made, i)
                    for u in range(SB):
                        last = nc.tensor.transpose(pT[:, u * D:(u + 1) * D], xb[:, u, :], ident[:])
                    last.then_inc(x_turned, 1)

                def experts(i):
                    pe.wait_ge(xl_made, i + 1)
                    for f in range(NF):
                        after(pe, hl_made, NF * i + f - 2)
                        z = pz[f % 3]
                        c = slice(C_SWI + f * P, C_SWI + (f + 1) * P)
                        nc.tensor.matmul(z[:], cwh[:, c], xh[:], start=True, stop=False)
                        nc.tensor.matmul(z[:], cwh[:, c], xl[:], start=False, stop=False)
                        nc.tensor.matmul(z[:], cwl[:, c], xh[:], start=False, stop=True).then_inc(z_made, 1)
                    for n in range(NSH):
                        pe.wait_ge(hl_made, NF * i + KF * (n + 1))
                        after(pe, c_made, i)
                        for u in range(SB):
                            for k in range(KF):
                                f = n * KF + k
                                c = slice(C_SWO + f * D, C_SWO + (f + 1) * D)
                                t = slice(u * B, (u + 1) * B)
                                nc.tensor.matmul(py[n][:, u, :], hh[:, f, t], cwh[:, c], start=(k == 0), stop=False)
                                nc.tensor.matmul(py[n][:, u, :], hh[:, f, t], cwl[:, c], start=False, stop=False)
                                last = nc.tensor.matmul(py[n][:, u, :], hl[:, f, t], cwh[:, c], start=False,
                                                        stop=(k == KF - 1))
                        last.then_inc(y_summed, 1)

                def gate():
                    pe.wait_ge(gin_made, 1)
                    for n in range(3):
                        last = nc.tensor.transpose(pq[0][:, n * B:(n + 1) * B], gin[:, n, :], ident[:])
                    last.then_inc(g_turned, 1)
                    pe.wait_ge(gT_made, 1)
                    for n in range(3):
                        last = nc.tensor.matmul(pq[1][:, 0:B], g1[:, n, :], gT[:, n, :], start=(n == 0), stop=(n == 2))
                    last.then_inc(g_first, 1)
                    pe.wait_ge(gr_made, 1)
                    nc.tensor.matmul(pq[0][:, 0:3], gr[:], g2[:], start=True, stop=True).then_inc(g_second, 1)

                def project(i):
                    pe.wait_ge(nm_made, i + 1)
                    pe.wait_ge(xl_made, i + 1)
                    for u in range(SB):
                        last = nc.tensor.transpose(pT[:, u * D:(u + 1) * D], nm[:, u, :], ident[:])
                    last.then_inc(n_turned, 1)
                    pe.wait_ge(nl_made, i + 1)
                    for n in range(2):
                        after(pe, qk_made, 2 * i + n - 1)
                        c = slice(n * D, (n + 1) * D)
                        nc.tensor.matmul(pq[n][:], wh[:, c], nh[:], start=True, stop=False)
                        nc.tensor.matmul(pq[n][:], wh[:, c], nl[:], start=False, stop=False)
                        nc.tensor.matmul(pq[n][:], wl[:, c], nh[:], start=False, stop=True).then_inc(qk_summed, 1)
                    for u in range(SB):
                        t = slice(u * B, (u + 1) * B)
                        o = pT[:, t]
                        nc.tensor.matmul(o, nh[:, t], wh[:, 2 * D:], start=True, stop=False)
                        nc.tensor.matmul(o, nh[:, t], wl[:, 2 * D:], start=False, stop=False)
                        last = nc.tensor.matmul(o, nl[:, t], wh[:, 2 * D:], start=False, stop=True)
                    last.then_inc(v_summed, 1)

                turn(0)
                experts(0)
                gate()
                project(0)
                with pe.Fori(1, NB) as i:
                    turn(i)
                    experts(i)
                    project(i)

            @block.scalar
            def _(act):
                act.wait_ge(wg_made, 1)
                act.activation(wh[:], wgm[:], ACT.Copy).then_inc(wh_made, 1)

                def hidden(i):
                    act.wait_ge(x_turned, i + 1)
                    after(act, z_made, NF * i)
                    act.activation(xh[:], pT[:], ACT.Copy).then_inc(xh_made, 1)
                    after(act, y_summed, NSH * i)
                    for f in range(NF):
                        act.wait_ge(z_made, NF * i + f + 1)
                        act.activation(hh[:, f, :], pz[f % 3][:], ACT.Relu).then_inc(hh_made, 1)

                def gate():
                    act.wait_ge(g_turned, 1)
                    act.activation(gT[:].rearrange("p n b -> p (n b)"), pq[0][:, 0:3 * B], ACT.Copy).then_inc(gT_made, 1)
                    act.wait_ge(g_first, 1)
                    act.activation(gr[:], pq[1][:, 0:B], ACT.Relu).then_inc(gr_made, 1)
                    act.wait_ge(gate_step, 2)
                    act.activation(ge[:], gx[:], ACT.Exp).then_inc(ge_made, 1)

                def project(i):
                    act.wait_ge(n_turned, i + 1)
                    after(act, v_summed, i)
                    act.activation(nh[:], pT[:], ACT.Copy).then_inc(nh_made, 1)
                    for n, dst in enumerate((qT, kT)):
                        act.wait_ge(qk_summed, 2 * i + n + 1)
                        act.activation(dst[:, :, bass.ds(i * SB, SB)].rearrange("p b u -> p u b"),
                                       pq[n][:].rearrange("p (u b) -> p u b", u=SB), ACT.Identity,
                                       bias=bqkv[:, n:n + 1]).then_inc(qk_made, 1)
                    act.wait_ge(v_summed, i + 1)
                    after(act, v_stored, 16 * i)
                    act.activation(v[:].rearrange("p u d -> p (u d)"), pT[:], ACT.Copy).then_inc(v_made, 1)

                def scaled(i):
                    act.wait_ge(eo_loaded, 16 * SB * (i + 1))
                    after(act, t1_made, i)
                    act.activation(t0[:], eo[:], ACT.Copy, scale=wgt[:, 0:1]).then_inc(t0_made, 1)

                hidden(0)
                gate()
                act.wait_ge(gate_step, 6)
                scaled(0)
                project(0)
                with act.Fori(1, NB) as i:
                    hidden(i)
                    scaled(i)
                    project(i)

            @block.vector
            def _(dve):
                dve.wait_ge(w_loaded, 16 * 6)
                nc.vector.tensor_scalar(wgm[:], wraw[:], lng[:, 0:1], None, ALU.mult).then_inc(wg_made, 1)
                dve.wait_ge(bias_summed, 1)
                nc.vector.tensor_tensor(bqkv[:], pz[0][:, 0:3], braw[:], ALU.add)
                dve.wait_ge(wh_made, 1)
                nc.vector.tensor_tensor(wl[:], wgm[:], wh[:].bitcast(F32), ALU.subtract).then_inc(wl_made, 1)

                def hidden(i):
                    dve.wait_ge(xh_made, i + 1)
                    nc.vector.tensor_tensor(xl[:], pT[:], xh[:].bitcast(F32), ALU.subtract).then_inc(xl_made, 1)
                    for f in range(NF):
                        dve.wait_ge(hh_made, NF * i + f + 1)
                        nc.vector.scalar_tensor_tensor(hl[:, f, :], pz[f % 3][:], 0.0, hh[:, f, :].bitcast(F32),
                                                       ALU.max, ALU.subtract).then_inc(hl_made, 1)

                def gate():
                    def link(ins, n):
                        ins.then_inc(gate_step, 1)
                        dve.wait_ge(gate_step, n)

                    dve.wait_ge(eo_loaded, 16 * SB)
                    dve.wait_ge(y_summed, NSH)
                    nc.vector.tensor_copy(gin[:, 0, :], eo[:, 0, :])
                    for n in range(NSH):
                        last = nc.vector.tensor_copy(gin[:, n + 1, :], py[n][:, 0, :])
                    last.then_inc(gin_made, 1)
                    dve.wait_ge(g_second, 1)
                    link(nc.vector.tensor_reduce(gmx[:], pq[0][:, 0:3], AX, ALU.max), 1)
                    link(nc.vector.tensor_scalar(gx[:], pq[0][:, 0:3], gmx[:, 0:1], None, ALU.subtract), 2)
                    dve.wait_ge(ge_made, 1)
                    link(nc.vector.tensor_reduce(gs[:], ge[:], AX, ALU.add), 3)
                    link(nc.vector.reciprocal(gi[:], gs[:]), 4)
                    link(nc.vector.tensor_scalar(wgt[:], ge[:], gi[:, 0:1], None, ALU.mult), 5)
                    link(nc.vector.memset(gs[:], 0.0), 6)

                def mix(i):
                    dve.wait_ge(t0_made, i + 1)
                    dve.wait_ge(y_summed, NSH * (i + 1))
                    nc.vector.scalar_tensor_tensor(t1[:], py[0][:], wgt[:, 1:2], t0[:], ALU.mult, ALU.add).then_inc(t1_made, 1)
                    dve.wait_ge(t1_made, i + 1)
                    c = cres[:, bass.ds(i * SB, SB), :]
                    nc.vector.scalar_tensor_tensor(c, py[1][:], wgt[:, 2:3], t1[:], ALU.mult, ALU.add).then_inc(c_made, 1)
                    carry(dve, t1_made)
                    dve.wait_ge(c_made, i + 1)
                    for u in range(SB):
                        last = nc.vector.bn_stats(bs[:, u, :], cres[:, i * SB + u, :])
                    last.then_inc(stats, 1)
                    carry(dve, c_made)
                    dve.wait_ge(stats, i + 1)
                    for u in range(SB):
                        last = nc.vector.bn_aggr(mv[:, u, :], bs[:, u, :])
                    last.then_inc(mv_made, 1)
                    dve.wait_ge(mv_made, i + 1)
                    nc.vector.tensor_scalar(ve[:], mv[:, :, 1], EPS, None, ALU.add).then_inc(ve_made, 1)
                    dve.wait_ge(rs_made, i + 1)
                    after(dve, n_turned, i)
                    for u in range(SB):
                        last = nc.vector.tensor_scalar(nm[:, u, :], cres[:, i * SB + u, :], mv[:, u, 0:1],
                                                       rs[:, u:u + 1], ALU.subtract, ALU.mult)
                    last.then_inc(nm_made, 1)
                    dve.wait_ge(nh_made, i + 1)
                    nc.vector.tensor_tensor(nl[:], pT[:], nh[:].bitcast(F32), ALU.subtract).then_inc(nl_made, 1)

                hidden(0)
                gate()
                mix(0)
                with dve.Fori(1, NB) as i:
                    hidden(i)
                    mix(i)


def attention(nc, a, sb, pb, sem, ident, hmask, qT, kT, bqkv, v_dram, att_dram, mwh, mwl):
    SC = 1.0 / float(np.sqrt(DK))
    NT = HB // BT
    with ExitStack() as st:
        qs = sb("t_qs", [P, HB, HG, S], stack=st)
        ks = sb("t_ks", [P, HB, S], stack=st)
        sm = sb("t_sm", [P, HG, HB, S], stack=st)
        p = sb("t_p", [P, HG, HB, S], stack=st)
        ptT = sb("t_ptT", [P, HG, NT, P], stack=st)
        on = sb("t_on", [P, HB, HG, S], stack=st)
        oT = sb("t_oT", [P, NT, HG, BT, S], stack=st)
        v = sb("t_v", [P, NT, D], stack=st)
        mx = sb("t_mx", [P, HG, HB], stack=st)
        su = sb("t_su", [P, HG, HB], stack=st)
        ri = sb("t_ri", [P, HG, HB], stack=st)
        wo = sb("t_wo", [P, D], stack=st)
        wom = sb("t_wom", [P, HG, D], stack=st)
        bo = sb("t_bo", [P, D], stack=st)
        att = sb("t_att", [P, NT, D], stack=st)
        raw = sb("t_raw", [P, FF], stack=st)
        ps = pb("t_ps", [P, HG, 512], stack=st)
        po = pb("t_po", [P, BT, 512], stack=st)
        half_bank = HB * S
        names = ("w_loaded wom_made qs_made ks_made scored mx_made sub_made p_made su_made ri_made p_turned ptT_made "
                 "v_loaded o_summed on_made o_turned oT_made w_summed att_made att_stored raw_loaded high low").split()
        s_ = {n: sem("t_" + n, st) for n in names}
        (w_loaded, wom_made, qs_made, ks_made, scored, mx_made, sub_made, p_made, su_made, ri_made, p_turned, ptT_made,
         v_loaded, o_summed, on_made, o_turned, oT_made, w_summed, att_made, att_stored, raw_loaded, high,
         low) = (s_[n] for n in names)
        v_rows = v_dram.rearrange("(n t b) s d -> n (b s) t d", t=NT, b=BT)
        att_rows = att_dram.rearrange("(n t b) s d -> n (b s) t d", t=NT, b=BT)

        with nc.Block() as block:
            @block.sync
            def _(sp):
                sp.dma_start(wo[:], a["w_o"]).then_inc(w_loaded, 16)
                sp.dma_start(bo[:], a["b_o"].to_broadcast([P, D])).then_inc(w_loaded, 16)
                sp.dma_start(v[:], v_rows[0]).then_inc(v_loaded, 16)
                sp.dma_start(raw[:], a["mw"][:, 0:FF]).then_inc(raw_loaded, 16)
                with sp.Fori(0, NH - 1) as i:
                    sp.wait_ge(low, i + 1)
                    sp.dma_start(raw[:], a["mw"][:, bass.ds((i + 1) * FF, FF)]).then_inc(raw_loaded, 16)
                    sp.wait_ge(o_summed, i + 1)
                    sp.dma_start(v[:], v_rows[bass.ds(i + 1, 1)].rearrange("o p t d -> p (o t) d")).then_inc(v_loaded, 16)
                    sp.wait_ge(att_made, i + 1)
                    sp.dma_start(att_rows[bass.ds(i, 1)].rearrange("o p t d -> p (o t) d"), att[:]).then_inc(att_stored, 16)
                sp.wait_ge(att_made, NH)
                sp.dma_start(att_rows[NH - 1], att[:]).then_inc(att_stored, 16)
                sp.wait_ge(att_stored, 16 * NH)

            @block.gpsimd
            def _(pool):
                with pool.Fori(0, NH) as i:
                    pool.wait_ge(scored, i)
                    pool.tensor_copy(ks[:], kT[:, bass.ds(i * HB, HB), :]).then_inc(ks_made, 1)
                    pool.tensor_tensor(qs[:], qT[:, bass.ds(i * HB, HB), None, :].to_broadcast([P, HB, HG, S]),
                                       hmask[:, None, :, None].to_broadcast([P, HB, HG, S]), ALU.mult).then_inc(qs_made, 1)
                    pool.wait_ge(raw_loaded, 16 * (i + 1))
                    pool.tensor_copy(mwh[:, bass.ds(i * FF, FF)], raw[:]).then_inc(high, 1)
                    pool.wait_ge(high, i + 1)
                    pool.tensor_tensor(mwl[:, bass.ds(i * FF, FF)], raw[:], mwh[:, bass.ds(i * FF, FF)].bitcast(F32),
                                       ALU.subtract).then_inc(low, 1)

            @block.tensor
            def _(pe):
                def scores(i):
                    pe.wait_ge(qs_made, i + 1)
                    pe.wait_ge(ks_made, i + 1)
                    after(pe, sub_made, i)
                    for b in range(HB):
                        for g in range(HG):
                            r = slice(32 * g, 32 * g + 32)
                            last = nc.tensor.matmul(ps[:, g, b * S:(b + 1) * S], qs[r, b, :, :], ks[r, b, :],
                                                    start=True, stop=True)
                    last.then_inc(scored, 1)

                def turn_p(i):
                    pe.wait_ge(p_made, i + 1)
                    after(pe, att_made, i)
                    for g in range(HG):
                        for t in range(NT):
                            n = g * NT + t
                            c = half_bank + (n // BT) * P
                            last = nc.tensor.transpose(po[:, n % BT, c:c + P], p[:, g, t * BT:(t + 1) * BT, :], ident[:])
                    last.then_inc(p_turned, 1)

                def values(i):
                    pe.wait_ge(ptT_made, i + 1)
                    pe.wait_ge(v_loaded, 16 * (i + 1))
                    for t in range(NT):
                        for g in range(HG):
                            for b in range(BT):
                                r = slice(32 * b, 32 * b + 32)
                                c = t * P + g * 32
                                last = nc.tensor.matmul(po[:, b, c:c + 32], ptT[r, g, t, :], v[r, t, g * 32:(g + 1) * 32],
                                                        start=True, stop=True)
                    last.then_inc(o_summed, 1)

                def turn_o(i):
                    pe.wait_ge(on_made, i + 1)
                    for b in range(HB):
                        last = nc.tensor.transpose(po[:, b // 4, (b % 4) * P:(b % 4 + 1) * P], on[:, b, :, :], ident[:])
                    last.then_inc(o_turned, 1)

                def project(i):
                    pe.wait_ge(oT_made, i + 1)
                    for t in range(NT):
                        for j in range(HG):
                            last = nc.tensor.matmul(po[:, 2, t * D:(t + 1) * D], oT[:, t, j, :, :],
                                                    wom[:, j, :], start=(j == 0), stop=(j == HG - 1))
                    last.then_inc(w_summed, 1)

                scores(0)
                pe.wait_ge(wom_made, 1)
                with pe.Fori(0, NH - 1) as i:
                    turn_p(i)
                    scores(i + 1)
                    values(i)
                    turn_o(i)
                    project(i)
                turn_p(NH - 1)
                values(NH - 1)
                turn_o(NH - 1)
                project(NH - 1)

            @block.scalar
            def _(act):
                def exps(i):
                    act.wait_ge(sub_made, i + 1)
                    after(act, su_made, i)
                    after(act, p_turned, i)
                    act.activation(p[:], sm[:], ACT.Exp, scale=SC).then_inc(p_made, 1)

                def probs(i):
                    act.wait_ge(p_turned, i + 1)
                    after(act, o_summed, i)
                    for n2 in range(HG * NT // BT):
                        last = act.activation(ptT[:].rearrange("p g t c -> p (g t) c")[:, n2 * BT:(n2 + 1) * BT, :],
                                              po[:, :, half_bank + n2 * P:half_bank + (n2 + 1) * P], ACT.Copy)
                    last.then_inc(ptT_made, 1)

                def outs(i):
                    act.wait_ge(o_turned, i + 1)
                    after(act, w_summed, i)
                    for t in range(NT):
                        last = act.activation(oT[:, t].rearrange("p j b q -> p b j q"),
                                              po[:, t, :].rearrange("p (b j q) -> p b j q", b=BT, j=HG),
                                              ACT.Identity, bias=bqkv[:, 2:3])
                    last.then_inc(oT_made, 1)

                exps(0)
                with act.Fori(0, NH - 1) as i:
                    probs(i)
                    exps(i + 1)
                    outs(i)
                probs(NH - 1)
                outs(NH - 1)

            @block.vector
            def _(dve):
                dve.wait_ge(w_loaded, 32)
                for j in range(HG):
                    last = nc.vector.tensor_scalar(wom[:, j, :], wo[:], hmask[:, j:j + 1], None, ALU.mult)
                last.then_inc(wom_made, 1)

                def maxima(i):
                    dve.wait_ge(scored, i + 1)
                    sv = ps[:, :, 0:half_bank].rearrange("p g (b k) -> p g b k", k=S)
                    nc.vector.tensor_reduce(mx[:], sv, AX, ALU.max).then_inc(mx_made, 1)
                    dve.wait_ge(mx_made, i + 1)
                    after(dve, p_made, i)
                    nc.vector.tensor_tensor(sm[:], sv, mx[:, :, :, None].to_broadcast([P, HG, HB, S]), ALU.subtract)\
                        .then_inc(sub_made, 1)

                def inverse(i):
                    dve.wait_ge(p_made, i + 1)
                    nc.vector.tensor_reduce(su[:], p[:], AX, ALU.add).then_inc(su_made, 1)
                    dve.wait_ge(su_made, i + 1)
                    after(dve, on_made, i)
                    nc.vector.reciprocal(ri[:], su[:]).then_inc(ri_made, 1)

                def normalised(i):
                    dve.wait_ge(o_summed, i + 1)
                    dve.wait_ge(ri_made, i + 1)
                    after(dve, o_turned, i)
                    for t in range(NT):
                        r = ri[:, :, t * BT:(t + 1) * BT].rearrange("p g b -> p b g")
                        last = nc.vector.tensor_tensor(on[:, t * BT:(t + 1) * BT, :, :],
                                                       po[:, :, t * P:(t + 1) * P].rearrange("p b (g d) -> p b g d", g=HG),
                                                       r[:, :, :, None].to_broadcast([P, BT, HG, S]), ALU.mult)
                    last.then_inc(on_made, 1)

                def result(i):
                    dve.wait_ge(w_summed, i + 1)
                    after(dve, att_stored, 16 * i)
                    nc.vector.tensor_tensor(att[:], po[:, 2, 0:NT * D].rearrange("p (t d) -> p t d", t=NT),
                                            bo[:, None, :].to_broadcast([P, NT, D]), ALU.add).then_inc(att_made, 1)

                maxima(0)
                with dve.Fori(0, NH - 1) as i:
                    inverse(i)
                    maxima(i + 1)
                    normalised(i)
                    result(i)
                inverse(NH - 1)
                normalised(NH - 1)
                result(NH - 1)


def second_norm(nc, a, sb, pb, sem, ident, x1, cres, att_dram, h2, logits, ms_dram):
    with ExitStack() as st:
        att = sb("d_att", [P, SB, D], stack=st)
        x2 = sb("d_x2", [P, SB, D], stack=st)
        bs = sb("d_bs", [P, SB, 6], stack=st)
        mv = sb("d_mv", [P, SB, 2], stack=st)
        ve = sb("d_ve", [P, SB], stack=st)
        rs = sb("d_rs", [P, SB], stack=st)
        half = sb("d_half", [P, SB], stack=st)
        nm = sb("d_nm", [P, SB, D], stack=st)
        ng = sb("d_ng", [P, SB, D], stack=st)
        hb = sb("d_hb", [P, SB, D], stack=st)
        hT = sb("d_hT", [P, W], stack=st)
        gbt = sb("d_gbt", [P, 2, D], stack=st)
        gw = sb("d_gw", [P, E], stack=st)
        gbias = sb("d_gbias", [P, E], stack=st)
        pT = pb("d_pT", [P, W], stack=st)
        pl = pb("d_pl", [P, 512], stack=st)
        names = ("w_loaded att_loaded x2_made x1_made stats mv_made ve_made rs_made nm_made ng_made hb_made h_turned "
                 "hT_made h2_made summed l_made halfed").split()
        s_ = {n: sem("d_" + n, st) for n in names}
        (w_loaded, att_loaded, x2_made, x1_made, stats, mv_made, ve_made, rs_made, nm_made, ng_made, hb_made, h_turned,
         hT_made, h2_made, summed, l_made, halfed) = (s_[n] for n in names)

        with nc.Block() as block:
            @block.sync
            def _(sp):
                sp.dma_start(gbt[:], a["ln2"].to_broadcast([P, 2 * D]).rearrange("p (n d) -> p n d", n=2)).then_inc(w_loaded, 16)
                sp.dma_start(gw[:], a["gate_w"]).then_inc(w_loaded, 16)
                sp.dma_start(gbias[:], a["gate_b"].to_broadcast([P, E])).then_inc(w_loaded, 16)
                sp.dma_start(att[:], att_dram[:, 0:SB, :]).then_inc(att_loaded, 16)
                with sp.Fori(0, NB - 1) as i:
                    sp.wait_ge(x2_made, i + 1)
                    sp.dma_start(att[:], att_dram[:, bass.ds((i + 1) * SB, SB), :]).then_inc(att_loaded, 16)

            @block.gpsimd
            def _(pool):
                pool.memset(half[:], -0.5).then_inc(halfed, 1)
                pool.wait_ge(halfed, 1)
                pool.wait_ge(w_loaded, 48)
                with pool.Fori(0, NB) as i:
                    pool.wait_ge(ve_made, i + 1)
                    pool.wait_ge(nm_made, i)
                    pool.tensor_tensor(rs[:], ve[:], half[:], ALU.pow).then_inc(rs_made, 1)
                    pool.wait_ge(x2_made, i + 1)
                    pool.wait_ge(x1_made, i)
                    v = x1[:, bass.ds(i * SB, SB), :]
                    pool.tensor_tensor(v, v, x2[:], ALU.add).then_inc(x1_made, 1)
                    pool.wait_ge(nm_made, i + 1)
                    pool.tensor_tensor(ng[:], nm[:], gbt[:, 0:1, :].to_broadcast([P, SB, D]), ALU.mult).then_inc(ng_made, 1)
                    pool.wait_ge(ng_made, i + 1)
                    pool.wait_ge(h2_made, i)
                    pool.wait_ge(h_turned, i)
                    pool.tensor_tensor(hb[:], ng[:], gbt[:, 1:2, :].to_broadcast([P, SB, D]), ALU.add).then_inc(hb_made, 1)

            @block.tensor
            def _(pe):
                pe.wait_ge(w_loaded, 48)
                with pe.Fori(0, NB) as i:
                    pe.wait_ge(hb_made, i + 1)
                    pe.wait_ge(hT_made, i)
                    for u in range(SB):
                        last = nc.tensor.transpose(pT[:, u * D:(u + 1) * D], hb[:, u, :], ident[:])
                    last.then_inc(h_turned, 1)
                    pe.wait_ge(hT_made, i + 1)
                    pe.wait_ge(l_made, i)
                    for u in range(SB):
                        last = nc.tensor.matmul(pl[:, u * E:(u + 1) * E], hT[:, u * B:(u + 1) * B], gw[:], start=True, stop=True)
                    last.then_inc(summed, 1)

            @block.scalar
            def _(act):
                with act.Fori(0, NB) as i:
                    act.wait_ge(hb_made, i + 1)
                    act.activation(h2[:, bass.ds(i * SB, SB), 0:D], hb[:], ACT.Copy).then_inc(h2_made, 1)
                    act.wait_ge(h_turned, i + 1)
                    act.wait_ge(summed, i)
                    act.activation(hT[:], pT[:], ACT.Copy).then_inc(hT_made, 1)

            @block.vector
            def _(dve):
                dve.wait_ge(w_loaded, 48)
                with dve.Fori(0, NB) as i:
                    dve.wait_ge(att_loaded, 16 * i + 16)
                    dve.wait_ge(x1_made, i)
                    nc.vector.tensor_tensor(x2[:], cres[:, bass.ds(i * SB, SB), :], att[:], ALU.add).then_inc(x2_made, 1)
                    dve.wait_ge(x2_made, i + 1)
                    for u in range(SB):
                        last = nc.vector.bn_stats(bs[:, u, :], x2[:, u, :])
                    last.then_inc(stats, 1)
                    carry(dve, x2_made)
                    dve.wait_ge(stats, i + 1)
                    for u in range(SB):
                        last = nc.vector.bn_aggr(mv[:, u, :], bs[:, u, :])
                    last.then_inc(mv_made, 1)
                    dve.wait_ge(mv_made, i + 1)
                    nc.vector.tensor_scalar(ve[:], mv[:, :, 1], EPS, None, ALU.add).then_inc(ve_made, 1)
                    dve.wait_ge(rs_made, i + 1)
                    dve.wait_ge(ng_made, i)
                    for u in range(SB):
                        last = nc.vector.tensor_scalar(nm[:, u, :], x2[:, u, :], mv[:, u, 0:1], rs[:, u:u + 1],
                                                       ALU.subtract, ALU.mult)
                    last.then_inc(nm_made, 1)
                    dve.wait_ge(summed, i + 1)
                    nc.vector.tensor_tensor(logits[:, bass.ds(i * SB, SB), :],
                                            pl[:, 0:SB * E].rearrange("p (u e) -> p u e", e=E),
                                            gbias[:, None, :].to_broadcast([P, SB, E]), ALU.add).then_inc(l_made, 1)


def route(nc, a, sb, pb, sem, ones, tri, h2, logits, expert_of_tile, ms_dram):
    SE = [P, S, E]
    with ExitStack() as st:
        c = sb("r_c", [P, 2 * E + S + ET + 2], stack=st)
        padr = sb("r_padr", [P, ROW], stack=st)
        padi = sb("r_padi", [P, ET], I32, st)
        zero = sb("r_zero", [P, ET, ROW], stack=st)
        m1, m2, r1, r2, dl, ex, ex1, w1, w2, sf = (sb("r_" + n, [P, S], stack=st) for n in
                                                  ("m1", "m2", "r1", "r2", "dl", "ex", "ex1", "w1", "w2", "sf"))
        eq, ew, k1, k2, l2, both, inc, exc, rank, pick = (sb("r_" + n, SE, stack=st) for n in
                                                          ("eq", "ew", "k1", "k2", "l2", "both", "inc", "exc", "rank", "pick"))
        tot, cnt, padf, endt, offs, base = (sb("r_" + n, [P, E], stack=st) for n in
                                            ("tot", "cnt", "padf", "endt", "offs", "base"))
        cnti = sb("r_cnti", [P, E], I32, st)
        cnts = sb("r_cnts", [P, E], I32, st)
        past = sb("r_past", [1, E - 1, ET], stack=st)
        totile = sb("r_totile", [1, ET], stack=st)
        slots = [sb(f"r_slots{k}", [P, S], I32, st) for k in range(2)]
        dests = [sb(f"r_dests{k}", [P, S], I32, st) for k in range(2)]
        rows = sb("r_rows", [P, SB], I32, st)
        pc = pb("r_pc", [P, 512], stack=st)
        pp = pb("r_pp", [P, 512], stack=st)
        c_loaded, pad_loaded, pad_made, pad_stored, step, totals, prefix, ex_made, dl_made, slots_made, sent, tagged, \
            zeroed, rows_made = (sem("r_" + n, st) for n in (
                "c_loaded", "pad_loaded", "pad_made", "pad_stored", "step", "totals", "prefix", "ex_made", "dl_made",
                "slots_made", "sent", "tagged", "zeroed", "rows_made"))
        C_W, C_1, C_T, C_Q, C_D = np.cumsum([0, E, E, ET, S]).tolist()

        with nc.Block() as block:
            @block.sync
            def _(sp):
                sp.dma_start(c[:, 0:E + E + ET + S], a["rconsts"]).then_inc(c_loaded, 16)
                sp.dma_start(padi[:], a["pads"]).then_inc(pad_loaded, 16)
                sp.wait_ge(pad_made, 1)
                sp.dma_start(ms_dram.rearrange("(j p) c -> p j c", p=P), zero[:]).then_inc(pad_stored, 16)

            @block.gpsimd
            def _(pool):
                pool.memset(zero[:], 0.0).then_inc(zeroed, 1)
                pool.wait_ge(zeroed, 1)
                pool.wait_ge(pad_loaded, 16)
                pool.tensor_copy(zero[:, :, D:D + 1].bitcast(I32), padi[:, :, None]).then_inc(pad_made, 1)
                pool.wait_ge(pad_stored, 16)
                for k in range(2):
                    pool.wait_ge(tagged, k + 1)
                    for s in range(S):
                        pool.indirect_dma_start(ms_dram, bass.IndirectOffsetOnAxis(ap=slots[k][:, s:s + 1], axis=0),
                                                h2[:, s, :], None).then_inc(sent, 16)
                    pool.wait_ge(sent, 16 * S * (k + 1))

            @block.tensor
            def _(pe):
                pe.wait_ge(totals, 1)
                nc.tensor.matmul(pc[:, 0:E], ones[:], tot[:], start=True, stop=True)
                nc.tensor.matmul(pp[:, 0:E], tri[:], tot[:], start=True, stop=True).then_inc(prefix, 1)

            @block.scalar
            def _(act):
                act.wait_ge(dl_made, 1)
                act.activation(ex[:], dl[:], ACT.Exp).then_inc(ex_made, 1)

            @block.vector
            def _(dve):
                done = [0]

                def link(ins):
                    done[0] += 1
                    ins.then_inc(step, 1)
                    dve.wait_ge(step, done[0])

                order = c[:, None, C_W:C_1].to_broadcast(SE)
                wide = lambda t: t[:, :, None].to_broadcast(SE)
                dve.wait_ge(c_loaded, 16)

                def best(values, m, r, k):
                    link(nc.vector.tensor_reduce(m[:], values, AX, ALU.max))
                    link(nc.vector.tensor_tensor(eq[:], values, wide(m), ALU.is_equal))
                    link(nc.vector.tensor_tensor(ew[:], eq[:], order, ALU.mult))
                    link(nc.vector.tensor_reduce(r[:], ew[:], AX, ALU.max))
                    link(nc.vector.tensor_tensor(k[:], order, wide(r), ALU.is_equal))

                best(logits[:], m1, r1, k1)
                link(nc.vector.scalar_tensor_tensor(l2[:], k1[:], -3.0e38, logits[:], ALU.mult, ALU.add))
                best(l2[:], m2, r2, k2)
                nc.vector.tensor_tensor(dl[:], m2[:], m1[:], ALU.subtract).then_inc(dl_made, 1)
                link(nc.vector.tensor_tensor(both[:], k1[:], k2[:], ALU.add))
                for e in range(E):
                    link(nc.vector.tensor_tensor_scan(inc[:, :, e], ones[:, 0:S], both[:, :, e], 0.0, ALU.mult, ALU.add))
                nc.vector.tensor_copy(tot[:], inc[:, S - 1, :]).then_inc(totals, 1)
                link(nc.vector.tensor_tensor(exc[:], inc[:], both[:], ALU.subtract))
                dve.wait_ge(prefix, 1)
                link(nc.vector.tensor_scalar(cnt[:], pc[:, 0:E], float(P - 1), None, ALU.add))
                link(nc.vector.tensor_copy(cnti[:], cnt[:]))
                link(nc.vector.tensor_scalar(cnts[:], cnti[:], 7, 7, ALU.logical_shift_right, ALU.logical_shift_left))
                link(nc.vector.tensor_copy(padf[:], cnts[:]))
                link(nc.vector.tensor_tensor_scan(endt[:], ones[:, 0:E], padf[:], 0.0, ALU.mult, ALU.add))
                link(nc.vector.tensor_tensor(offs[:], endt[:], padf[:], ALU.subtract))
                link(nc.vector.tensor_tensor(base[:], pp[:, 0:E], offs[:], ALU.add))
                link(nc.vector.tensor_tensor(rank[:], exc[:], base[:, None, :].to_broadcast(SE), ALU.add))
                for k, one in enumerate((k1, k2)):
                    link(nc.vector.tensor_tensor(pick[:], rank[:], one[:], ALU.mult))
                    link(nc.vector.tensor_reduce(sf[:], pick[:], AX, ALU.add))
                    link(nc.vector.tensor_copy(slots[k][:], sf[:]))
                    link(nc.vector.tensor_scalar(dests[k][:], c[:, C_Q:C_D], float(k * T), None, ALU.add))
                dve.wait_ge(ex_made, 1)
                link(nc.vector.tensor_scalar(ex1[:], ex[:], 1.0, None, ALU.add))
                link(nc.vector.reciprocal(w1[:], ex1[:]))
                link(nc.vector.tensor_tensor(w2[:], ex[:], w1[:], ALU.mult))
                for k, wk in enumerate((w1, w2)):
                    if k:
                        dve.wait_ge(sent, 16 * S)
                    link(nc.vector.tensor_copy(h2[:, :, D:D + 1].bitcast(I32), dests[k][:, :, None]))
                    nc.vector.tensor_copy(h2[:, :, D + 1:D + 2], wk[:, :, None]).then_inc(tagged, 1)
                for n in range(E - 1):
                    link(nc.vector.tensor_scalar(past[0:1, n, :], c[0:1, C_T:C_T + ET], endt[0:1, n:n + 1], None, ALU.is_ge))
                link(nc.vector.tensor_reduce(totile[0:1, :], past[0:1, :, :].rearrange("p n j -> p j n"), AX, ALU.add))
                link(nc.vector.tensor_copy(expert_of_tile[0:1, :], totile[0:1, :]))


def experts(nc, a, sb, pb, sem, ident, expert_of_tile, ms_dram, y_dram, mwh, mwl):
    with ExitStack() as st:
        b1 = sb("x_b1", [P, E * FF], stack=st)
        b2r = sb("x_b2r", [2, E * D], stack=st)
        b2h = sb("x_b2h", [2, E * D], F32R, st)
        b2m = sb("x_b2m", [2, E * D], stack=st)
        b2 = sb("x_b2", [2, E * D], F32R, st)
        sgn = sb("x_sgn", [2, 2], stack=st)
        onesf = sb("x_onesf", [2, P], stack=st)
        onesr = sb("x_onesr", [2, P], F32R, st)
        xs = [sb(f"x_xs{q}", [P, ROW], stack=st) for q in range(4)]
        idx = [sb(f"x_idx{q}", [P, 1], I32, st) for q in range(2)]
        xh = sb("x_xh", [P, P], F32R, st)
        xl = sb("x_xl", [P, P], F32R, st)
        r = sb("x_r", [P, 2, FF], stack=st)
        hh = sb("x_hh", [P, FF], F32R, st)
        hl = sb("x_hl", [P, FF], F32R, st)
        y = sb("x_y", [P, 2, D], stack=st)
        pT = pb("x_pT", [P, P], stack=st)
        pz = [pb(f"x_pz{q}", [P, FF], stack=st) for q in range(2)]
        pt = [pb(f"x_pt{q}", [P, FF], stack=st) for q in range(2)]
        py = [pb(f"x_py{q}", [P, 512], stack=st) for q in range(2)]
        loaded = [sem(f"x_loaded{q}", st) for q in range(4)]
        sent = [sem(f"x_sent{q}", st) for q in range(2)]
        names = ("x_turned xh_made xl_made z_made r_made r_turned hh_made hl_made y_summed y_made idx_made b_loaded "
                 "step").split()
        (x_turned, xh_made, xl_made, z_made, r_made, r_turned, hh_made, hl_made, y_summed, y_made, idx_made, b_loaded,
         step_) = (sem("x_" + n, st) for n in names)
        Q = 4
        LAST = ET // Q - 1

        def rounds(eng, step):
            for q in range(Q):
                step(0, q, q)
            with eng.Fori(1, LAST) as jj:
                for q in range(Q):
                    step(jj, Q * jj + q, q)
            for q in range(Q):
                step(LAST, Q * LAST + q, q)

        def at(jj, q, r_, q_):
            return isinstance(jj, int) and jj == r_ and q == q_

        none = sb("x_none", [P, 1], I32, st)
        none_made = sem("x_none_made", st)

        with nc.Block() as block:
            @block.sync
            def _(sp):
                sp.dma_start(b1[:], a["m_b1"].to_broadcast([P, E * FF])).then_inc(b_loaded, 16)
                sp.dma_start(b2r[:], a["m_b2"].to_broadcast([2, E * D])).then_inc(b_loaded, 16)
                sp.dma_start(sgn[:], a["signs"]).then_inc(b_loaded, 16)
                for q in range(Q):
                    sp.dma_start(xs[q][:], ms_dram[q * P:(q + 1) * P, :]).then_inc(loaded[q], 16)

                def step(jj, j, q):
                    if not (isinstance(jj, int) and jj == LAST):
                        sp.wait_ge(x_turned, j + 1)
                        sp.wait_ge(y_made, j + 1)
                        sp.wait_ge(idx_made, j + 1)
                        sp.dma_start(xs[q][:], ms_dram[bass.ds((j + Q) * P, P), :]).then_inc(loaded[q], 16)

                rounds(sp, step)

            @block.gpsimd
            def _(pool):
                def step(jj, j, q):
                    pool.wait_ge(y_made, j + 1)
                    pool.wait_ge(loaded[q], 16 * jj + 16)
                    after(pool, sent[q % 2], 16 * (2 * jj + q // 2))
                    pool.tensor_tensor(idx[q % 2][:], xs[q][:, D:D + 1].bitcast(I32), none[:], ALU.add).then_inc(idx_made, 1)
                    carry(pool, none_made)
                    pool.wait_ge(idx_made, j + 1)
                    pool.indirect_dma_start(y_dram, bass.IndirectOffsetOnAxis(ap=idx[q % 2][:, 0:1], axis=0),
                                            y[:, q % 2, :], None).then_inc(sent[q % 2], 16)

                pool.memset(none[:], 0).then_inc(none_made, 1)
                pool.wait_ge(none_made, 1)
                rounds(pool, step)
                for q in range(2):
                    pool.wait_ge(sent[q], 16 * (ET // 2))

            @block.tensor
            def _(pe):
                def turn(jj, j, q):
                    pe.wait_ge(loaded[q], 16 * jj + 16)
                    after(pe, xl_made, j)
                    nc.tensor.transpose(pT[:], xs[q][:, 0:D], ident[:]).then_inc(x_turned, 1)

                def first(j, q):
                    e = pe.value_load(expert_of_tile[0:1, bass.ds(j, 1)], min_val=0, max_val=E - 1)
                    pe.wait_ge(xl_made, j + 1)
                    after(pe, r_made, j - 1)
                    c = bass.ds(e * FF, FF)
                    nc.tensor.matmul(pz[q][:], xh[:], mwh[:, c], start=True, stop=False)
                    nc.tensor.matmul(pz[q][:], xh[:], mwl[:, c], start=False, stop=False)
                    nc.tensor.matmul(pz[q][:], xl[:], mwh[:, c], start=False, stop=True).then_inc(z_made, 1)

                def turn_hidden(j, q):
                    pe.wait_ge(r_made, j + 1)
                    after(pe, hl_made, j - 1)
                    for k in range(KF):
                        last = nc.tensor.transpose(pt[q][:, k * P:(k + 1) * P], r[:, q, k * P:(k + 1) * P], ident[:])
                    last.then_inc(r_turned, 1)

                def second(j, q):
                    e = pe.value_load(expert_of_tile[0:1, bass.ds(j, 1)], min_val=0, max_val=E - 1)
                    pe.wait_ge(hl_made, j + 1)
                    after(pe, y_made, j - 1)
                    nc.tensor.matmul(py[q][:, 0:D], onesr[:], b2[:, bass.ds(e * D, D)], start=True, stop=False)
                    for k in range(KF):
                        c = bass.ds(e * (KF * D) + (M_W2 + k * D), D)
                        h = slice(k * P, (k + 1) * P)
                        nc.tensor.matmul(py[q][:, 0:D], hh[:, h], mwh[:, c], start=False, stop=False)
                        nc.tensor.matmul(py[q][:, 0:D], hh[:, h], mwl[:, c], start=False, stop=False)
                        last = nc.tensor.matmul(py[q][:, 0:D], hl[:, h], mwh[:, c], start=False, stop=(k == KF - 1))
                    last.then_inc(y_summed, 1)

                pe.wait_ge(step_, 5)
                turn(0, 0, 0)

                def step(jj, j, q):
                    first(j, q % 2)
                    if not at(jj, q, 0, 0):
                        second(j - 1, 1 - q % 2)
                    if not at(jj, q, LAST, Q - 1):
                        turn(jj + (q + 1) // Q, j + 1, (q + 1) % Q)
                    turn_hidden(j, q % 2)

                rounds(pe, step)
                second(ET - 1, 1)

            @block.scalar
            def _(act):
                def high(j):
                    act.wait_ge(x_turned, j + 1)
                    after(act, z_made, j)
                    act.activation(xh[:], pT[:], ACT.Copy).then_inc(xh_made, 1)

                def result(jj, j, q):
                    act.wait_ge(y_summed, j + 1)
                    after(act, sent[q % 2], 16 * (2 * jj + q // 2))
                    act.activation(y[:, q % 2], py[q % 2][:, 0:D], ACT.Copy, scale=xs[q][:, D + 1:D + 2]).then_inc(y_made, 1)

                high(0)

                def step(jj, j, q):
                    if not at(jj, q, LAST, Q - 1):
                        high(j + 1)
                    if not at(jj, q, 0, 0):
                        result(jj if q else jj - 1, j - 1, (q - 1) % Q)
                    act.wait_ge(r_turned, j + 1)
                    after(act, y_summed, j)
                    act.activation(hh[:], pt[q % 2][:], ACT.Relu).then_inc(hh_made, 1)

                rounds(act, step)
                result(LAST, ET - 1, Q - 1)

            @block.vector
            def _(dve):
                def link(ins, n):
                    ins.then_inc(step_, 1)
                    dve.wait_ge(step_, n)

                dve.wait_ge(b_loaded, 48)
                link(nc.vector.memset(onesf[:], 1.0), 1)
                nc.vector.tensor_copy(onesr[:], onesf[:])
                link(nc.vector.tensor_copy(b2h[:], b2r[:]), 2)
                link(nc.vector.tensor_scalar(b2m[:], b2r[:], sgn[:, 0:1], None, ALU.mult), 3)
                link(nc.vector.scalar_tensor_tensor(b2[:], b2h[:].bitcast(F32), sgn[:, 1:2], b2m[:], ALU.mult, ALU.add), 4)
                link(nc.vector.memset(onesf[:], 1.0), 5)

                def low(j):
                    dve.wait_ge(xh_made, j + 1)
                    nc.vector.tensor_tensor(xl[:], pT[:], xh[:].bitcast(F32), ALU.subtract).then_inc(xl_made, 1)

                low(0)

                def step(jj, j, q):
                    e = dve.value_load(expert_of_tile[0:1, bass.ds(j, 1)], min_val=0, max_val=E - 1)
                    dve.wait_ge(z_made, j + 1)
                    after(dve, r_turned, j - 1)
                    nc.vector.tensor_tensor(r[:, q % 2], pz[q % 2][:], b1[:, bass.ds(e * FF, FF)], ALU.add).then_inc(r_made, 1)
                    if not at(jj, q, LAST, Q - 1):
                        low(j + 1)
                    dve.wait_ge(hh_made, j + 1)
                    nc.vector.scalar_tensor_tensor(hl[:], pt[q % 2][:], 0.0, hh[:].bitcast(F32), ALU.max, ALU.subtract)\
                        .then_inc(hl_made, 1)

                rounds(dve, step)


def combine(nc, sb, pb, sem, x1, y_dram, out):
    with ExitStack() as st:
        y = sb("f_y", [P, 2, 2, SB, D], stack=st)
        t = sb("f_t", [P, 2, SB, D], stack=st)
        o = sb("f_o", [P, 2, SB, D], stack=st)
        loaded = [sem(f"f_loaded{q}", st) for q in range(2)]
        stored = [sem(f"f_stored{q}", st) for q in range(2)]
        t_made = sem("f_t_made", st)
        o_made = sem("f_o_made", st)
        y_view = y_dram[0:2 * T, :].rearrange("(k b s) d -> b k s d", k=2, b=B)

        with nc.Block() as block:
            @block.sync
            def _(sp):
                for i in range(2):
                    for k in range(2):
                        sp.dma_start(y[:, i, k], y_view[:, k, i * SB:(i + 1) * SB, :]).then_inc(loaded[i], 16)
                with sp.Fori(1, NB // 2) as j:
                    for q in range(2):
                        sp.wait_ge(o_made, 2 * j + q - 1)
                        for k in range(2):
                            sp.dma_start(y[:, q, k], y_view[:, k, bass.ds((2 * j + q) * SB, SB), :]).then_inc(loaded[q], 16)

            @block.scalar
            def _(act):
                with act.Fori(0, NB // 2) as j:
                    for q in range(2):
                        act.wait_ge(o_made, 2 * j + q + 1)
                        act.dma_start(out[:, bass.ds((2 * j + q) * SB, SB), :], o[:, q]).then_inc(stored[q], 16)
                for q in range(2):
                    act.wait_ge(stored[q], 16 * (NB // 2))

            @block.vector
            def _(dve):
                with dve.Fori(0, NB // 2) as j:
                    for q in range(2):
                        dve.wait_ge(loaded[q], 32 * j + 32)
                        nc.vector.tensor_tensor(t[:, q], y[:, q, 0], y[:, q, 1], ALU.add).then_inc(t_made, 1)
                        dve.wait_ge(t_made, 2 * j + q + 1)
                        dve.wait_ge(stored[q], 16 * j)
                        nc.vector.tensor_tensor(o[:, q], t[:, q], x1[:, bass.ds((2 * j + q) * SB, SB), :], ALU.add)\
                            .then_inc(o_made, 1)


def constants():
    p = np.arange(P)
    f = np.float32
    parts = [np.eye(P, dtype=f), (p[:, None] < p[None, :]).astype(f), np.ones((P, P), f),
             ((p[:, None] // DK) % HG == np.arange(HG)[None, :]).astype(f), (p[:, None] % LO).astype(f),
             np.tile(np.arange(TYPES, dtype=f), (P, 1)), np.tile(np.arange(S, dtype=f), (P, 1)),
             np.tile(BT * np.arange(TT, dtype=f), (P, 1))]
    return np.ascontiguousarray(np.concatenate(parts, axis=1))


def route_constants():
    p = np.arange(P)
    f = np.float32
    parts = [np.tile(E - np.arange(E, dtype=f), (P, 1)), np.ones((P, E), f), np.tile(P * np.arange(ET, dtype=f), (P, 1)),
             (p[:, None] * S + np.arange(S)[None, :]).astype(f)]
    return np.ascontiguousarray(np.concatenate(parts, axis=1))


def arrays_of(inputs):
    g = {k: np.asarray(v) for k, v in inputs.items()}
    c = np.ascontiguousarray
    L0, C1, F1 = "L0_cond_", "L1_cond_", "L1_ffn_"
    return {
        "x": c(g["x"]),
        "langs": c(g["itok_B_0_8"].reshape(1, B)),
        "types": c(g["itok_B_0_2"].reshape(B, 1)),
        "consts": constants(),
        "W1": c(g[L0 + "W1"].transpose(1, 0, 2).reshape(D, LA)),
        "b1": c(g[L0 + "b1"].reshape(1, LA)),
        "W2": c(g[L0 + "W2"].reshape(LA, D)),
        "tab": c(np.stack([g[L0 + "gamma"], g[L0 + "beta"], g[L0 + "b2"]], axis=1)),
        "w_gate": c(g["L0_ffn_w_gate"].T),
        "w_up": c(g["L0_ffn_w_up"].T),
        "cw": c(np.concatenate(
            [g[C1 + "wi"].transpose(1, 0, 2).reshape(D, -1),
             g[C1 + "wo"].reshape(TYPES, KF, P, D).transpose(2, 0, 1, 3).reshape(P, -1),
             g[C1 + "swi"].transpose(1, 0, 2).reshape(D, -1),
             g[C1 + "swo"].reshape(NSH, KF, P, D).transpose(2, 0, 1, 3).reshape(P, -1)], axis=1)),
        "mw": c(np.concatenate(
            [g[F1 + "W1"].transpose(1, 0, 2).reshape(D, -1),
             g[F1 + "W2"].reshape(E, KF, P, D).transpose(2, 0, 1, 3).reshape(P, -1)], axis=1)),
        "m_b1": c(g[F1 + "b1"].reshape(1, -1)),
        "m_b2": c(g[F1 + "b2"].reshape(1, -1)),
        "signs": np.array([[0, 1], [1, -1]], np.float32),
        "rconsts": route_constants(),
        "pads": np.ascontiguousarray((2 * T + np.arange(ET * P, dtype=np.int32)).reshape(ET, P).T),
        "w_o": c(g[F1 + "w_o"]),
        "b_o": c(g[F1 + "b_o"].reshape(1, D)),
        "ln2": c(np.concatenate([g[F1 + "ln2_g"], g[F1 + "ln2_b"]]).reshape(1, 2 * D)),
        "gate_w": c(g[F1 + "gate_w"]),
        "gate_b": c(g[F1 + "gate_b"].reshape(1, E)),
        "g1": c(g[C1 + "g1"].reshape(3, D, D).transpose(1, 0, 2)),
        "g2": c(g[C1 + "g2"]),
        "w_qkv": c(g[F1 + "w_qkv"]),
        "b_qkv": c(g[F1 + "b_qkv"].reshape(3, D).T),
        "ln1_g": c(g[F1 + "ln1_g"].reshape(D, 1)),
        "ln1_b": c(g[F1 + "ln1_b"].reshape(D, 1)),
        "w_down": c(g["L0_ffn_w_down"].T.reshape(KF, P, D).transpose(1, 0, 2).reshape(P, KF * D)),
    }


def kernel(**inputs):
    import concourse.bacc as bacc
    from concourse.bass_utils import run_bass_kernel_spmd

    nc = bacc.Bacc("TRN2", target_bir_lowering=False, num_devices=1)
    arrays = {f"in_{n}": v for n, v in arrays_of(inputs).items()}
    a = {n[3:]: nc.dram_tensor(n, v.shape, mybir.dt.from_np(v.dtype), kind="ExternalInput").ap()
         for n, v in arrays.items()}
    out = nc.dram_tensor("out_dram", (B, S, D), F32, kind="ExternalOutput").ap()
    adaln_ffn_moe_kernel(nc, a, out)
    r = run_bass_kernel_spmd(nc, [arrays], core_ids=[0])
    return r.results[0]["out_dram"]
```

```python
from contextlib import ExitStack

import numpy as np
import concourse.bass as bass
from concourse import mybir

F32 = mybir.dt.float32
F32R = mybir.dt.float32r
BF16 = mybir.dt.bfloat16
I32 = mybir.dt.int32
ALU = mybir.AluOpType
ACT = mybir.ActivationFunctionType
AX = mybir.AxisListType.X

P = 128
B, S, D = 128, 32, 128
T = B * S
LANG, AD = 10, 32
LA = LANG * AD
INNER = 512
TYPES, NSH = 5, 2
H, DK = 16, 8
E = 8
FF = 512
KF = FF // P
SB = 4
NB = S // SB
W = SB * D
BT = P // S
TT = (B + TYPES * (BT - 1)) // BT
TILE_UNROLL = 6
TT += -TT % TILE_UNROLL
ET = (2 * T + E * (P - 1)) // P
ET += -ET % TILE_UNROLL
CB = (TYPES + NSH) * 2 * KF
B_WO = TYPES * KF
B_SWI = 2 * TYPES * KF
B_SWO = B_SWI + NSH * KF
MB = 2 * E * KF
ROW = D + 2
CHB = 8
MAGIC = 1.5 * 2.0 ** 23
OFF = -1.0e30
EPS = 1e-5
HG = H // 4
LO = 32


def adaln_ffn_moe_kernel(nc, a, out, dump=None):
    ctx = ExitStack()

    def sb(name, shape, dt=F32, stack=None):
        return (stack or ctx).enter_context(nc.sbuf_tensor(name, shape, dt))

    def pb(name, shape, dt=F32, stack=None):
        return (stack or ctx).enter_context(nc.psum_tensor(name, shape, dt))

    def sem(name, stack=None):
        if name in kept:
            return kept[name]
        handle = sems[-1].enter_context(nc.semaphore(name))
        numbers.append(handle.num)
        return handle

    def reuse_semaphores():
        nc.all_engine_barrier(sems_to_clear=range(min(numbers), max(numbers) + 1))
        sems.pop().close()
        sems.append(ctx.enter_context(ExitStack()))
        numbers.clear()

    with ctx:
        kept = {n: ctx.enter_context(nc.semaphore(n)) for n in ("b_sent", "c_eo_loaded")}
        sems, numbers = [ctx.enter_context(ExitStack())], []
        x1 = sb("x1", [P, S, D])
        ident = sb("ident", [P, P])
        tri = sb("tri", [P, P])
        ones = sb("ones", [P, P])
        hmask = sb("hmask", [P, HG])
        type_slot = sb("type_slot", [P, S], I32)
        type_of_tile = sb("type_of_tile", [1, TT], I32)
        xs_dram = nc.dram_tensor("xs_dram", (TT * P, D), F32, kind="Internal").ap()
        eo_dram = nc.dram_tensor("eo_dram", (TT * P, D), F32, kind="Internal").ap()
        qkv_dram = nc.dram_tensor("qkv_dram", (B, S, 3 * D), F32, kind="Internal").ap()
        att_dram = nc.dram_tensor("att_dram", (B, S, D), F32, kind="Internal").ap()

        cres = sb("cres", [P, S, D])
        with ExitStack() as cond:
            cwp = sb("cwp", [P, CB, 2, D], F32R, cond)
            with ExitStack() as layer0:
                nrm = sb("nrm", [P, S, D], stack=layer0)
                w1h = sb("w1h", [P, LA], F32R, layer0)
                w1l = sb("w1l", [P, LA], F32R, layer0)
                w2h = sb("w2h", [P, 3, D], F32R, layer0)
                w2l = sb("w2l", [P, 3, D], F32R, layer0)
                bias1 = sb("bias1", [2 * LO, LA], F32R, layer0)
                tab = sb("tab", [2 * LO, 3, D], F32R, layer0)
                lang1h = sb("lang1h", [2 * LO, B], F32R, layer0)
                gb = sb("gb", [P, 2, D], stack=layer0)
                wgq = sb("wgq", [P, INNER], BF16, layer0)
                wuq = sb("wuq", [P, INNER], BF16, layer0)
                wdq = sb("wdq", [P, KF, D], BF16, layer0)
                wsc = sb("wsc", [P, 3], stack=layer0)

                KT = [(0, P), (P, P), (2 * P, LA - 2 * P)]
                setup(nc, a, sb, pb, sem, x1, ident, tri, ones, hmask, type_slot, type_of_tile, xs_dram,
                      w1h, w1l, w2h, w2l, bias1, tab, lang1h, gb, wgq, wuq, wdq, wsc, KT)
                adapter(nc, a, sb, pb, sem, x1, ident, nrm, w1h, w1l, w2h, w2l, bias1, tab, lang1h, gb, KT)
                if dump == "A":
                    dump_out(nc, sem, out, nrm)
                    return
                quantised_ffn(nc, a, sb, pb, sem, x1, ident, nrm, wgq, wuq, wdq, wsc, type_slot, xs_dram, cwp)
                if dump == "B":
                    dump_out(nc, sem, out, x1)
                    return
            typed_experts(nc, sb, pb, sem, ident, type_of_tile, xs_dram, eo_dram, cwp)
            shared_experts(nc, a, sb, pb, sem, x1, ident, type_slot, eo_dram, qkv_dram, cwp, cres)
            if dump == "C":
                dump_out(nc, sem, out, cres)
                return
        reuse_semaphores()
        ms_dram = nc.dram_tensor("ms_dram", (ET * P, ROW), F32, kind="Internal").ap()
        y_dram = nc.dram_tensor("y_dram", (2 * T + ET * P, D), F32, kind="Internal").ap()
        mwp = sb("mwp", [P, MB, 2, D], F32R)
        attention(nc, a, sb, pb, sem, ident, hmask, qkv_dram, att_dram, mwp)
        expert_of_tile = sb("expert_of_tile", [1, ET], I32)
        with ExitStack() as st:
            h2 = sb("h2", [P, S, ROW], stack=st)
            logits = sb("logits", [P, S, E], stack=st)
            second_norm(nc, a, sb, pb, sem, ident, x1, cres, att_dram, h2, logits, ms_dram)
            if dump == "D":
                dump_out(nc, sem, out, x1)
                return
            if dump == "h2":
                dump_out(nc, sem, out, h2[:, :, 0:D])
                return
            route(nc, a, sb, pb, sem, ones, tri, h2, logits, expert_of_tile, ms_dram)
        experts(nc, a, sb, pb, sem, ident, expert_of_tile, ms_dram, y_dram, mwp)
        combine(nc, sb, pb, sem, x1, y_dram, out)


def dump_out(nc, sem, out, t):
    done = sem("dumped")
    with nc.Block() as block:
        @block.sync
        def _(sp):
            sp.dma_start(out, t[:]).then_inc(done, 16)
            sp.wait_ge(done, 16)


def setup(nc, a, sb, pb, sem, x1, ident, tri, ones, hmask, type_slot, type_of_tile, xs_dram,
          w1h, w1l, w2h, w2l, bias1, tab, lang1h, gb, wgq, wuq, wdq, wsc, KT):
    with ExitStack() as st:
        w1 = sb("s_w1", [P, LA], stack=st)
        w2 = sb("s_w2", [P, 3, D], stack=st)
        braw = sb("s_braw", [2 * LO, LA], stack=st)
        traw = sb("s_traw", [2 * LO, 3, D], stack=st)
        bhi = sb("s_bhi", [2 * LO, LA], F32R, st)
        thi = sb("s_thi", [2 * LO, 3, D], F32R, st)
        ids = sb("s_ids", [2 * LO, B], I32, st)
        idf = sb("s_idf", [2 * LO, B], stack=st)
        ty = sb("s_ty", [P, 1], I32, st)
        tyf = sb("s_tyf", [P, 1], stack=st)
        consts = sb("s_consts", [P, 3 * P + HG + 1 + TYPES + S + TT], stack=st)
        ffw = sb("s_ffw", [P, 3, INNER], stack=st)
        tot = sb("s_tot", [P, 3], stack=st)
        msc = sb("s_msc", [P, 3], stack=st)
        inv = sb("s_inv", [P, 3], stack=st)
        rnd = sb("s_rnd", [P, 3, INNER], stack=st)
        t1h = sb("s_t1h", [P, TYPES], stack=st)
        cnt = sb("s_cnt", [P, TYPES], stack=st)
        cnti = sb("s_cnti", [P, TYPES], I32, st)
        cnts = sb("s_cnts", [P, TYPES], I32, st)
        padf = sb("s_padf", [P, TYPES], stack=st)
        zero = sb("s_zero", [P, D], stack=st)
        endt = sb("s_endt", [P, TYPES], stack=st)
        offs = sb("s_offs", [P, TYPES], stack=st)
        slot = sb("s_slot", [P, TYPES], stack=st)
        slotw = sb("s_slotw", [P, TYPES], stack=st)
        slot1 = sb("s_slot1", [P, 1], stack=st)
        row1 = sb("s_row1", [P, 1], stack=st)
        tslot = sb("s_tslot", [P, S], stack=st)
        past = sb("s_past", [1, TYPES - 1, TT], stack=st)
        totile = sb("s_totile", [1, TT], stack=st)
        ps = pb("s_ps", [P, 512], stack=st)
        ps2 = pb("s_ps2", [P, 512], stack=st)
        ps3 = pb("s_ps3", [P, 512], stack=st)
        ps4 = pb("s_ps4", [P, 512], stack=st)
        ld_x, ld_w, ld_t, ld_f, ld_c = (sem(n, st) for n in ("ld_x", "ld_w", "ld_t", "ld_f", "ld_c"))
        cleared, rows_cleared, diag, sums, means, onehot, tabs, ranks, ty1h, step, gbd = (
            sem("s_" + n, st) for n in
            ("cleared", "rows_cleared", "diag", "sums", "means", "onehot", "tabs", "ranks", "ty1h", "step", "gbd"))
        pool_step = sem("s_pool_step", st)
        C_I, C_T, C_1, C_H, C_M, C_P, C_S, C_J = np.cumsum([0, P, P, P, HG, 1, TYPES, S]).tolist()

        with nc.Block() as block:
            @block.sync
            def _(sp):
                sp.dma_start(consts[:], a["consts"]).then_inc(ld_c, 16)
                sp.dma_start(w1[:], a["W1"]).then_inc(ld_w, 16)
                for k, (o, n) in enumerate(KT):
                    sp.dma_start(w2[0:n, k, :], a["W2"][o:o + n, :]).then_inc(ld_w, 16)
                for n, name in enumerate(("w_gate", "w_up", "w_down")):
                    sp.dma_start(ffw[:, n, :], a[name]).then_inc(ld_f, 16)
                sp.wait_ge(cleared, 1)
                for j in range(TT):
                    sp.dma_start(xs_dram[j * P:(j + 1) * P, :], zero[:]).then_inc(rows_cleared, 16)
                sp.wait_ge(rows_cleared, 16 * TT)
                sp.wait_ge(ld_x, 16 * 4)

            @block.scalar
            def _(act):
                act.dma_start(ty[:], a["types"]).then_inc(ld_t, 16)
                act.dma_start(ids[:], a["langs"].to_broadcast([2 * LO, B])).then_inc(ld_t, 16)
                act.wait_ge(cleared, 2)
                for r in (0, LO):
                    act.dma_start(braw[r:r + LANG, :], a["b1"].to_broadcast([LANG, LA])).then_inc(ld_t, 16)
                    act.dma_start(traw[r:r + LANG, :, :], a["tab"]).then_inc(ld_t, 16)
                for q in range(4):
                    act.dma_start(x1[:, q * 8:(q + 1) * 8, :], a["x"][:, q * 8:(q + 1) * 8, :]).then_inc(ld_x, 16)

            @block.gpsimd
            def _(pool):
                pool.memset(zero[:], 0.0).then_inc(cleared, 1)
                pool.memset(braw[:], 0.0)
                pool.memset(traw[:], 0.0).then_inc(cleared, 1)
                pool.wait_ge(ld_t, 16 * 6)
                for n, r in enumerate((0, LO)):
                    v = braw[r:r + LO, :].rearrange("p (l c) -> p l c", l=LANG)
                    pool.affine_select(out=v, in_=v, compare_op=ALU.is_equal, fill=OFF if n == 0 else 0.0, base=0,
                                       pattern=[[-1, LANG], [0, AD]], channel_multiplier=1).then_inc(diag, 1)
                    pool.wait_ge(diag, n + 1)
                pool.wait_ge(ld_w, 16 * 4)
                pool.tensor_copy(w1h[:], w1[:]).then_inc(pool_step, 1)
                pool.wait_ge(pool_step, 1)
                pool.tensor_tensor(w1l[:], w1[:], w1h[:].bitcast(F32), ALU.subtract).then_inc(pool_step, 1)
                pool.wait_ge(pool_step, 2)
                for k, (o, n) in enumerate(KT):
                    pool.tensor_copy(w2h[0:n, k, :], w2[0:n, k, :]).then_inc(pool_step, 1)
                    pool.wait_ge(pool_step, 2 * k + 3)
                    pool.tensor_tensor(w2l[0:n, k, :], w2[0:n, k, :], w2h[0:n, k, :].bitcast(F32), ALU.subtract)\
                        .then_inc(pool_step, 1)
                    pool.wait_ge(pool_step, 2 * k + 4)

            @block.vector
            def _(dve):
                done = [0]

                def link(ins):
                    done[0] += 1
                    ins.then_inc(step, 1)
                    dve.wait_ge(step, done[0])

                dve.wait_ge(ld_c, 16)
                nc.vector.tensor_copy(ident[:], consts[:, C_I:C_T])
                nc.vector.tensor_copy(tri[:], consts[:, C_T:C_1])
                nc.vector.tensor_copy(hmask[:], consts[:, C_H:C_M])
                link(nc.vector.tensor_copy(ones[:], consts[:, C_1:C_H]))
                dve.wait_ge(ld_t, 16 * 6)
                link(nc.vector.tensor_copy(tyf[:], ty[:]))
                link(nc.vector.tensor_scalar(t1h[:], consts[:, C_P:C_S], tyf[:, 0:1], None, ALU.is_equal))
                nc.vector.memset(endt[:], 0.0).then_inc(ty1h, 1)
                link(nc.vector.tensor_copy(idf[:], ids[:]))
                nc.vector.tensor_scalar(lang1h[:], idf[:], consts[0:2 * LO, C_M:C_P], None, ALU.is_equal)
                nc.vector.tensor_copy(thi[:], traw[:])
                dve.wait_ge(diag, 2)
                link(nc.vector.tensor_copy(bhi[:], braw[:]))
                nc.vector.tensor_copy(tab[0:LO], thi[0:LO].bitcast(F32))
                nc.vector.tensor_copy(bias1[0:LO, :], bhi[0:LO, :].bitcast(F32))
                nc.vector.tensor_tensor(tab[LO:2 * LO], traw[LO:2 * LO], thi[LO:2 * LO].bitcast(F32), ALU.subtract)
                nc.vector.tensor_tensor(bias1[LO:2 * LO, :], braw[LO:2 * LO, :], bhi[LO:2 * LO, :].bitcast(F32),
                                        ALU.subtract).then_inc(tabs, 1)
                dve.wait_ge(ld_f, 16 * 3)
                nc.vector.tensor_reduce(tot[:], ffw[:], AX, ALU.add, apply_absolute_value=True).then_inc(sums, 1)
                dve.wait_ge(means, 1)
                link(nc.vector.tensor_scalar(msc[:], ps[:, 0:3], 1.0 / (D * INNER), 1e-5, ALU.mult, ALU.max))
                link(nc.vector.tensor_scalar(wsc[:], msc[:], 1.0 / 127.0, None, ALU.mult))
                link(nc.vector.reciprocal(inv[:], msc[:]))
                for n in range(3):
                    link(nc.vector.tensor_scalar(rnd[:, n, :], ffw[:, n, :], inv[:, n:n + 1], MAGIC, ALU.mult, ALU.add))
                link(nc.vector.tensor_scalar(rnd[:], rnd[:], MAGIC - 1.0, MAGIC + 1.0, ALU.max, ALU.min))
                for n, q in enumerate((wgq[:], wuq[:], wdq[:].rearrange("p k d -> p (k d)"))):
                    link(nc.vector.tensor_scalar(q, rnd[:, n, :], MAGIC, None, ALU.subtract))
                dve.wait_ge(ranks, 1)
                link(nc.vector.tensor_scalar(cnt[:], ps2[:, 0:TYPES], float(BT - 1), None, ALU.add))
                link(nc.vector.tensor_copy(cnti[:], cnt[:]))
                link(nc.vector.tensor_scalar(cnts[:], cnti[:], 2, 2, ALU.logical_shift_right, ALU.logical_shift_left))
                link(nc.vector.tensor_copy(padf[:], cnts[:]))
                link(nc.vector.tensor_copy(endt[:, 0:1], padf[:, 0:1]))
                for n in range(1, TYPES):
                    link(nc.vector.tensor_tensor(endt[:, n:n + 1], endt[:, n - 1:n], padf[:, n:n + 1], ALU.add))
                link(nc.vector.tensor_tensor(offs[:], endt[:], padf[:], ALU.subtract))
                link(nc.vector.tensor_tensor(slot[:], offs[:], ps3[:, 0:TYPES], ALU.add))
                link(nc.vector.tensor_tensor(slotw[:], slot[:], t1h[:], ALU.mult))
                link(nc.vector.tensor_reduce(slot1[:], slotw[:], AX, ALU.add))
                link(nc.vector.tensor_scalar(row1[:], slot1[:], float(S), None, ALU.mult))
                link(nc.vector.tensor_scalar(tslot[:], consts[:, C_S:C_J], row1[:, 0:1], None, ALU.add))
                nc.vector.tensor_copy(type_slot[:], tslot[:])
                for n in range(TYPES - 1):
                    link(nc.vector.tensor_scalar(past[0:1, n, :], consts[0:1, C_J:C_J + TT], endt[0:1, n:n + 1], None,
                                                 ALU.is_ge))
                link(nc.vector.tensor_reduce(totile[0:1, :], past[0:1, :, :].rearrange("p n j -> p j n"), AX, ALU.add))
                link(nc.vector.tensor_copy(type_of_tile[0:1, :], totile[0:1, :]))
                dve.wait_ge(gbd, 1)
                link(nc.vector.tensor_copy(gb[:], ps4[:, 0:2 * D].rearrange("p (n d) -> p n d", n=2)))

            @block.tensor
            def _(pe):
                pe.wait_ge(ty1h, 1)
                nc.tensor.matmul(ps2[:, 0:TYPES], ones[:], t1h[:], start=True, stop=True)
                nc.tensor.matmul(ps3[:, 0:TYPES], tri[:], t1h[:], start=True, stop=True).then_inc(ranks, 1)
                pe.wait_ge(tabs, 1)
                nc.tensor.matmul(ps4[:, 0:2 * D], lang1h[:], tab[:, 0:2, :], start=True, stop=True).then_inc(gbd, 1)
                pe.wait_ge(sums, 1)
                nc.tensor.matmul(ps[:, 0:3], ones[:], tot[:], start=True, stop=True).then_inc(means, 1)


def adapter(nc, a, sb, pb, sem, x1, ident, nrm, w1h, w1l, w2h, w2l, bias1, tab, lang1h, gb, KT):
    with ExitStack() as st:
        xin = sb("a_xin", [P, 2, SB, D], stack=st)
        xh = sb("a_xh", [P, W], F32R, st)
        xl = sb("a_xl", [P, W], F32R, st)
        hh = sb("a_hh", [P, 3, W], F32R, st)
        hl = sb("a_hl", [P, 3, W], F32R, st)
        y = sb("a_y", [P, SB, D], stack=st)
        bs = sb("a_bs", [P, SB, 6], stack=st)
        mv = sb("a_mv", [P, SB, 2], stack=st)
        ve = sb("a_ve", [P, SB], stack=st)
        rs = sb("a_rs", [P, SB], stack=st)
        half = sb("a_half", [P, SB], stack=st)
        nm = sb("a_nm", [P, SB, D], stack=st)
        ng = sb("a_ng", [P, SB, D], stack=st)
        pT = pb("a_pT", [P, W], stack=st)
        pz = [pb(f"a_pz{k}", [P, W], stack=st) for k in range(3)]
        pa = pb("a_pa", [P, SB, D], stack=st)
        x_turned, xh_made, xl_made, z_made, hh_made, hl_made, a_made, y_made, mv_made, ve_made, rs_made, nm_made, \
            ng_made, out_made, stats = (sem("a_" + n, st) for n in (
                "x_turned", "xh_made", "xl_made", "z_made", "hh_made", "hl_made", "a_made", "y_made", "mv_made",
                "ve_made", "rs_made", "nm_made", "ng_made", "out_made", "stats"))
        halfed = sem("a_halfed", st)
        x_loaded = [sem(f"a_x_loaded{q}", st) for q in range(2)]

        with nc.Block() as block:
            @block.tensor
            def _(pe):
                def block_of(j, i, q):
                    pe.wait_ge(x_loaded[q], 16 * j + 16)
                    pe.wait_ge(xl_made, i)
                    for u in range(SB):
                        last = nc.tensor.transpose(pT[:, u * D:(u + 1) * D], xin[:, q, u, :], ident[:])
                    last.then_inc(x_turned, 1)
                    pe.wait_ge(xh_made, i + 1)
                    pe.wait_ge(xl_made, i + 1)
                    for k, (o, n) in enumerate(KT):
                        pe.wait_ge(hl_made, 3 * i)
                        nc.tensor.matmul(pz[k][0:n, :], w1h[:, o:o + n], xh[:], start=True, stop=False)
                        nc.tensor.matmul(pz[k][0:n, :], w1h[:, o:o + n], xl[:], start=False, stop=False)
                        nc.tensor.matmul(pz[k][0:n, :], w1l[:, o:o + n], xh[:], start=False, stop=False)
                        nc.tensor.matmul(pz[k][0:n, :], bias1[:, o:o + n],
                                         lang1h[:, None, :].to_broadcast([2 * LO, SB, B]),
                                         start=False, stop=True).then_inc(z_made, 1)
                    pe.wait_ge(hh_made, 3 * i + 3)
                    pe.wait_ge(hl_made, 3 * i + 3)
                    pe.wait_ge(y_made, i)
                    for u in range(SB):
                        c = slice(u * D, (u + 1) * D)
                        for k, (o, n) in enumerate(KT):
                            nc.tensor.matmul(pa[:, u, :], hh[0:n, k, c], w2h[0:n, k, :], start=(k == 0), stop=False)
                            nc.tensor.matmul(pa[:, u, :], hl[0:n, k, c], w2h[0:n, k, :], start=False, stop=False)
                            nc.tensor.matmul(pa[:, u, :], hh[0:n, k, c], w2l[0:n, k, :], start=False, stop=False)
                        last = nc.tensor.matmul(pa[:, u, :], lang1h[:], tab[:, 2, :], start=False, stop=True)
                    last.then_inc(a_made, 1)

                with pe.Fori(0, NB // 2) as j:
                    for q in range(2):
                        block_of(j, 2 * j + q, q)

            @block.sync
            def _(sp):
                for q in range(2):
                    sp.dma_start(xin[:, q], a["x"][:, q * SB:(q + 1) * SB, :]).then_inc(x_loaded[q], 16)
                with sp.Fori(1, NB // 2) as j:
                    for q in range(2):
                        sp.wait_ge(x_turned, 2 * j + q - 1)
                        sp.dma_start(xin[:, q], a["x"][:, bass.ds((2 * j + q) * SB, SB), :]).then_inc(x_loaded[q], 16)

            @block.scalar
            def _(act):
                with act.Fori(0, NB) as i:
                    act.wait_ge(x_turned, i + 1)
                    act.wait_ge(z_made, 3 * i)
                    nc.scalar.activation(xh[:], pT[:], ACT.Copy).then_inc(xh_made, 1)
                    act.wait_ge(a_made, i)
                    for k, (o, n) in enumerate(KT):
                        act.wait_ge(z_made, 3 * i + k + 1)
                        nc.scalar.activation(hh[0:n, k, :], pz[k][0:n, :], ACT.Relu).then_inc(hh_made, 1)

            @block.gpsimd
            def _(pool):
                pool.memset(half[:], -0.5).then_inc(halfed, 1)
                pool.wait_ge(halfed, 1)
                with pool.Fori(0, NB) as i:
                    pool.wait_ge(ve_made, i + 1)
                    pool.wait_ge(nm_made, i)
                    pool.tensor_tensor(rs[:], ve[:], half[:], ALU.pow).then_inc(rs_made, 1)
                    pool.wait_ge(nm_made, i + 1)
                    pool.tensor_tensor(ng[:], nm[:], gb[:, 0:1, :].to_broadcast([P, SB, D]), ALU.mult).then_inc(ng_made, 1)
                    pool.wait_ge(ng_made, i + 1)
                    pool.tensor_tensor(nrm[:, bass.ds(i * SB, SB), :], ng[:], gb[:, 1:2, :].to_broadcast([P, SB, D]),
                                       ALU.add).then_inc(out_made, 1)

            @block.vector
            def _(dve):
                def products(i):
                    dve.wait_ge(xh_made, i + 1)
                    nc.vector.tensor_tensor(xl[:], pT[:], xh[:].bitcast(F32), ALU.subtract).then_inc(xl_made, 1)
                    for k, (o, n) in enumerate(KT):
                        dve.wait_ge(hh_made, 3 * i + k + 1)
                        nc.vector.scalar_tensor_tensor(hl[0:n, k, :], pz[k][0:n, :], 0.0, hh[0:n, k, :].bitcast(F32),
                                                       ALU.max, ALU.subtract).then_inc(hl_made, 1)

                def statistics(i):
                    dve.wait_ge(a_made, i + 1)
                    nc.vector.tensor_tensor(y[:], pa[:], x1[:, bass.ds(i * SB, SB), :], ALU.add).then_inc(y_made, 1)
                    carry(dve, a_made)
                    dve.wait_ge(y_made, i + 1)
                    for u in range(SB):
                        last = nc.vector.bn_stats(bs[:, u, :], y[:, u, :])
                    last.then_inc(stats, 1)
                    carry(dve, y_made)
                    dve.wait_ge(stats, i + 1)
                    for u in range(SB):
                        last = nc.vector.bn_aggr(mv[:, u, :], bs[:, u, :])
                    last.then_inc(mv_made, 1)
                    dve.wait_ge(mv_made, i + 1)
                    dve.wait_ge(rs_made, i)
                    nc.vector.tensor_scalar(ve[:], mv[:, :, 1], EPS, None, ALU.add).then_inc(ve_made, 1)

                def normalise(i):
                    dve.wait_ge(rs_made, i + 1)
                    dve.wait_ge(ng_made, i)
                    for u in range(SB):
                        last = nc.vector.tensor_scalar(nm[:, u, :], y[:, u, :], mv[:, u, 0:1],
                                                       rs[:, u:u + 1], ALU.subtract, ALU.mult)
                    last.then_inc(nm_made, 1)

                with dve.Fori(0, NB) as i:
                    products(i)
                    statistics(i)
                    normalise(i)


def quantised_ffn(nc, a, sb, pb, sem, x1, ident, nrm, wgq, wuq, wdq, wsc, type_slot, xs_dram, cwp):
    with ExitStack() as st:
        amx = sb("b_amx", [P, S], stack=st)
        sc = sb("b_sc", [P, S], stack=st)
        qs = sb("b_qs", [P, S], stack=st)
        sg = sb("b_sg", [P, S], stack=st)
        su = sb("b_su", [P, S], stack=st)
        xq = sb("b_xq", [P, SB, D], stack=st)
        xqT = sb("b_xqT", [P, 2, W], BF16, st)
        g = sb("b_g", [P, 2, INNER], stack=st)
        m = sb("b_m", [P, 2, 2, INNER], stack=st)
        mq = sb("b_mq", [P, 2, INNER], stack=st)
        mqT = sb("b_mqT", [P, 2, INNER], BF16, st)
        magic = sb("b_magic", [P, 1], stack=st)
        raw = sb("b_raw", [P, 2, CHB, D], stack=st)
        raw_loaded = [sem(f"b_raw_loaded{q}", st) for q in range(2)]
        parted = sem("b_parted", st)
        am2 = sb("b_am2", [P, 2], stack=st)
        sc2 = sb("b_sc2", [P, 2], stack=st)
        qs2 = sb("b_qs2", [P, 2, 2], stack=st)
        sd = sb("b_sd", [P, 2, 2], stack=st)
        pT = pb("b_pT", [P, SB, D], stack=st)
        pg = pb("b_pg", [P, 2, INNER], stack=st)
        pu = pb("b_pu", [P, 2, INNER], stack=st)
        pm = [pb(f"b_pm{u}", [P, INNER], stack=st) for u in range(2)]
        po = pb("b_po", [P, 2, D], stack=st)
        xq_made, xq_turned, xqT_made, g_prod, u_prod, g_made, m_made, am_made, qs_made, mq_made, mqc_made, m_turned, \
            mqT_made, o_made, x1_made, step, sent = (sem("b_" + n, st) for n in (
                "xq_made", "xq_turned", "xqT_made", "g_prod", "u_prod", "g_made", "m_made", "am_made", "qs_made",
                "mq_made", "mqc_made", "m_turned", "mqT_made", "o_made", "x1_made", "step", "sent"))
        xq_raw = sem("b_xq_raw", st)
        NP2 = S // 2

        with nc.Block() as block:
            @block.tensor
            def _(pe):
                def turn(i):
                    pe.wait_ge(xq_made, i + 1)
                    pe.wait_ge(xqT_made, i)
                    for u in range(SB):
                        last = nc.tensor.transpose(pT[:, u, :], xq[:, u, :], ident[:])
                    last.then_inc(xq_turned, 1)

                def up(p, b2, h):
                    for n in range(2):
                        c = slice((2 * h + n) * D, (2 * h + n + 1) * D)
                        if n == 0:
                            pe.wait_ge(g_made, 2 * p)
                        nc.tensor.matmul(pg[:, n, :], xqT[:, b2, c], wgq[:], start=True, stop=True).then_inc(g_prod, 1)
                        if n == 0:
                            pe.wait_ge(m_made, 2 * p)
                        nc.tensor.matmul(pu[:, n, :], xqT[:, b2, c], wuq[:], start=True, stop=True).then_inc(u_prod, 1)

                def down(p):
                    for n in range(2):
                        pe.wait_ge(mqc_made, p + 1)
                        pe.wait_ge(mqT_made, 2 * p + n)
                        if n == 0:
                            pe.wait_ge(mqT_made, 2 * p)
                        for k in range(KF):
                            last = nc.tensor.transpose(pm[n][:, k * P:(k + 1) * P], mq[:, n, k * P:(k + 1) * P], ident[:])
                        last.then_inc(m_turned, 1)
                    pe.wait_ge(x1_made, p)
                    for n in range(2):
                        pe.wait_ge(mqT_made, 2 * p + n + 1)
                        for k in range(KF):
                            last = nc.tensor.matmul(po[:, n, :], mqT[:, n, k * P:(k + 1) * P], wdq[:, k, :],
                                                    start=(k == 0), stop=(k == KF - 1))
                    last.then_inc(o_made, 1)

                turn(0)
                pe.wait_ge(xqT_made, 1)
                up(0, 0, 0)
                with pe.Fori(0, NB - 1) as i:
                    up(2 * i + 1, i % 2, 1)
                    down(2 * i)
                    turn(i + 1)
                    pe.wait_ge(xqT_made, i + 2)
                    up(2 * i + 2, (i + 1) % 2, 0)
                    down(2 * i + 1)
                up(NP2 - 1, (NB - 1) % 2, 1)
                down(NP2 - 2)
                down(NP2 - 1)

            @block.scalar
            def _(act):
                def turned(i):
                    act.wait_ge(xq_turned, i + 1)
                    act.activation(xqT[:, i % 2, :], pT[:].rearrange("p u d -> p (u d)"), ACT.Copy, bias=-MAGIC)\
                       .then_inc(xqT_made, 1)

                def gate(p, b2, h):
                    for n in range(2):
                        act.wait_ge(g_prod, 2 * p + n + 1)
                        act.wait_ge(m_made, 2 * p + n)
                        if n == 0:
                            act.wait_ge(m_made, 2 * p)
                        act.activation(g[:, n, :], pg[:, n, :], ACT.Silu, scale=sg[:, bass.ds(2 * p + n, 1)])\
                           .then_inc(g_made, 1)

                def quantise(p):
                    act.wait_ge(qs_made, p + 1)
                    act.wait_ge(m_turned, 2 * p)
                    for n in range(2):
                        act.activation(mq[:, n, :], m[:, p % 2, n, :], ACT.Identity, bias=magic[:],
                                       scale=qs2[:, p % 2, n:n + 1]).then_inc(mq_made, 1)

                def turned_back(p):
                    for n in range(2):
                        act.wait_ge(m_turned, 2 * p + n + 1)
                        if n == 0:
                            act.wait_ge(o_made, p)
                        act.activation(mqT[:, n, :], pm[n][:], ACT.Copy, bias=-MAGIC).then_inc(mqT_made, 1)

                turned(0)
                gate(0, 0, 0)
                with act.Fori(0, NB - 1) as i:
                    quantise(2 * i)
                    gate(2 * i + 1, i % 2, 1)
                    turned_back(2 * i)
                    turned(i + 1)
                    quantise(2 * i + 1)
                    gate(2 * i + 2, (i + 1) % 2, 0)
                    turned_back(2 * i + 1)
                quantise(NP2 - 2)
                gate(NP2 - 1, (NB - 1) % 2, 1)
                turned_back(NP2 - 2)
                quantise(NP2 - 1)
                turned_back(NP2 - 1)

            @block.vector
            def _(dve):
                def link(ins, n):
                    ins.then_inc(step, 1)
                    dve.wait_ge(step, n)

                link(nc.vector.memset(magic[:], MAGIC), 1)
                link(nc.vector.tensor_reduce(amx[:], nrm[:], AX, ALU.max, apply_absolute_value=True), 2)
                link(nc.vector.tensor_scalar(sc[:], amx[:], 1e-5, 1.0 / 127.0, ALU.max, ALU.mult), 3)
                link(nc.vector.reciprocal(qs[:], sc[:]), 4)
                nc.vector.tensor_scalar(sg[:], sc[:], wsc[:, 0:1], 127.0, ALU.mult, ALU.mult)
                link(nc.vector.tensor_scalar(su[:], sc[:], wsc[:, 1:2], 127.0, ALU.mult, ALU.mult), 5)

                def rows(i):
                    dve.wait_ge(xq_turned, i)
                    for u in range(SB):
                        last = nc.vector.tensor_scalar(xq[:, u, :], nrm[:, i * SB + u, :],
                                                       qs[:, bass.ds(i * SB + u, 1)], MAGIC, ALU.mult, ALU.add)
                    last.then_inc(xq_raw, 1)
                    dve.wait_ge(xq_raw, i + 1)
                    nc.vector.tensor_scalar(xq[:], xq[:], MAGIC - 128.0, MAGIC + 127.0,
                                            ALU.max, ALU.min).then_inc(xq_made, 1)

                def inner(p):
                    for n in range(2):
                        dve.wait_ge(g_made, 2 * p + n + 1)
                        dve.wait_ge(u_prod, 2 * p + n + 1)
                        nc.vector.scalar_tensor_tensor(m[:, p % 2, n, :], pu[:, n, :], su[:, bass.ds(2 * p + n, 1)],
                                                       g[:, n, :], ALU.mult, ALU.mult).then_inc(m_made, 1)
                    dve.wait_ge(m_made, 2 * p + 2)
                    nc.vector.tensor_reduce(am2[:], m[:, p % 2], AX, ALU.max, apply_absolute_value=True).then_inc(am_made, 1)
                    dve.wait_ge(am_made, 3 * p + 1)
                    nc.vector.tensor_scalar(sc2[:], am2[:], 1e-5, 1.0 / 127.0, ALU.max, ALU.mult).then_inc(am_made, 1)
                    dve.wait_ge(am_made, 3 * p + 2)
                    nc.vector.reciprocal(qs2[:, p % 2, :], sc2[:]).then_inc(qs_made, 1)
                    nc.vector.tensor_scalar(sd[:, p % 2, :], sc2[:], wsc[:, 2:3], 127.0, ALU.mult, ALU.mult)\
                        .then_inc(am_made, 1)

                def clamp(p):
                    dve.wait_ge(mq_made, 2 * p + 2)
                    nc.vector.tensor_scalar(mq[:], mq[:], MAGIC - 128.0, MAGIC + 127.0, ALU.max, ALU.min)\
                        .then_inc(mqc_made, 1)

                def residual(p):
                    dve.wait_ge(o_made, p + 1)
                    dve.wait_ge(am_made, 3 * p + 3)
                    for n in range(2):
                        v = x1[:, 2 * p + n, :]
                        last = nc.vector.scalar_tensor_tensor(v, po[:, n, :], sd[:, p % 2, n:n + 1], v, ALU.mult, ALU.add)
                    last.then_inc(x1_made, 1)

                rows(0)
                inner(0)
                with dve.Fori(0, NB - 1) as i:
                    clamp(2 * i)
                    rows(i + 1)
                    inner(2 * i + 1)
                    residual(2 * i)
                    clamp(2 * i + 1)
                    inner(2 * i + 2)
                    residual(2 * i + 1)
                clamp(NP2 - 2)
                inner(NP2 - 1)
                residual(NP2 - 2)
                clamp(NP2 - 1)
                residual(NP2 - 1)

            @block.sync
            def _(sp):
                for n in range(CB // CHB):
                    if n >= 2:
                        sp.wait_ge(parted, 2 * n - 2)
                    sp.dma_start(raw[:, n % 2, :], a["cw"][:, n * CHB:(n + 1) * CHB, :]).then_inc(raw_loaded[n % 2], 16)

            @block.gpsimd
            def _(pool):
                def part(n):
                    c = slice(n * CHB, (n + 1) * CHB)
                    pool.wait_ge(raw_loaded[n % 2], 16 * (n // 2 + 1))
                    pool.tensor_copy(cwp[:, c, 0], raw[:, n % 2]).then_inc(parted, 1)
                    pool.wait_ge(parted, 2 * n + 1)
                    pool.tensor_tensor(cwp[:, c, 1], raw[:, n % 2], cwp[:, c, 0].bitcast(F32), ALU.subtract)\
                        .then_inc(parted, 1)
                    pool.wait_ge(parted, 2 * n + 2)

                for s in range(S):
                    if s % 4 == 0 and s // 4 < CB // CHB:
                        part(s // 4)
                    pool.wait_ge(x1_made, s // 2 + 1)
                    pool.indirect_dma_start(xs_dram, bass.IndirectOffsetOnAxis(ap=type_slot[:, s:s + 1], axis=0),
                                            x1[:, s, :], None).then_inc(sent, 16)
                pool.wait_ge(sent, 16 * S)


def carry(eng, signal):
    eng.wait_ge(signal, 1)


def after(eng, signal, value):
    if not (isinstance(value, int) and value <= 0):
        eng.wait_ge(signal, value)


def rolled(eng, step, tiles, unroll, drain):
    for c in range(unroll):
        step(0, c, c)
    last = tiles // unroll - 1
    with eng.Fori(1, last) as n:
        for c in range(unroll):
            step(n, unroll * n + c, c)
    for c in range(unroll + drain):
        step(last + c // unroll, tiles - unroll + c, c % unroll)


def behind(n, t, c, lag, unroll):
    return n + (c - lag) // unroll, t - lag, (c - lag) % unroll


def within(t, tiles):
    return not isinstance(t, int) or 0 <= t < tiles


def typed_experts(nc, sb, pb, sem, ident, type_of_tile, xs_dram, eo_dram, cwp):
    U, R = TILE_UNROLL, 3
    with ExitStack() as st:
        xs = sb("e_xs", [P, U, D], stack=st)
        xh = sb("e_xh", [P, 2, P], F32R, st)
        xl = sb("e_xl", [P, 2, P], F32R, st)
        r = sb("e_r", [P, 2, FF], stack=st)
        hh = sb("e_hh", [P, 2, FF], F32R, st)
        hl = sb("e_hl", [P, 2, FF], F32R, st)
        yl = sb("e_yl", [P, 2, D], stack=st)
        y = sb("e_y", [P, R, D], stack=st)
        pT = [pb(f"e_pT{q}", [P, 512], stack=st) for q in range(2)]
        pz = [pb(f"e_pz{q}", [P, FF], stack=st) for q in range(2)]
        pt = [pb(f"e_pt{q}", [P, FF], stack=st) for q in range(2)]
        py = [pb(f"e_py{q}", [P, 4, D], stack=st) for q in range(2)]
        w1, w2 = (cwp[:, n * B_WO:(n + 1) * B_WO].rearrange("p (e k) w d -> p e k w d", e=TYPES) for n in range(2))
        loaded = [sem(f"e_loaded{q}", st) for q in range(U)]
        stored = [sem(f"e_stored{q}", st) for q in range(R)]
        x_turned, xh_made, xl_made, z_made, r_made, r_turned, hh_made, hl_made, y_summed, yl_made, y_made = (
            sem("e_" + n, st) for n in ("x_turned", "xh_made", "xl_made", "z_made", "r_made", "r_turned", "hh_made",
                                        "hl_made", "y_summed", "yl_made", "y_made"))

        with nc.Block() as block:
            @block.sync
            def _(sp):
                for q in range(U):
                    sp.dma_start(xs[:, q], xs_dram[q * P:(q + 1) * P, :]).then_inc(loaded[q], 16)

                def step(n, t, c):
                    if within(t + U, TT):
                        sp.wait_ge(x_turned, t + 1)
                        sp.dma_start(xs[:, c], xs_dram[bass.ds((t + U) * P, P), :]).then_inc(loaded[c], 16)
                    if within(t - 3, TT):
                        sp.wait_ge(y_made, t - 2)
                        sp.dma_start(eo_dram[bass.ds((t - 3) * P, P), :], y[:, (c - 3) % R]).then_inc(stored[(c - 3) % R], 16)

                rolled(sp, step, TT, U, 3)
                for q in range(R):
                    sp.wait_ge(stored[q], 16 * (TT // R))

            @block.tensor
            def _(pe):
                held = {}

                def weights_of(t, place):
                    if place not in held:
                        held[place] = pe.value_load(type_of_tile[0:1, bass.ds(t, 1)], min_val=0, max_val=TYPES - 1)
                    return held[place]

                def turn(n, t, c):
                    q = c % 2
                    pe.wait_ge(loaded[c], 16 * n + 16)
                    nc.tensor.transpose(pT[q][:, 0:P], xs[:, c], ident[:]).then_inc(x_turned, 1)

                def first(n, t, c):
                    q = c % 2
                    e = weights_of(t, c)
                    pe.wait_ge(xl_made, t + 1)
                    wh, wl = (w1[:, bass.ds(e, 1), :, n_, :].rearrange("p o k d -> p (o k) d") for n_ in range(2))
                    nc.tensor.matmul(pz[q][:], xh[:, q], wh, start=True, stop=False)
                    nc.tensor.matmul(pz[q][:], xh[:, q], wl, start=False, stop=False)
                    nc.tensor.matmul(pz[q][:], xl[:, q], wh, start=False, stop=True).then_inc(z_made, 1)

                def turn_hidden(n, t, c):
                    q = c % 2
                    pe.wait_ge(r_made, t + 1)
                    for k in range(KF):
                        last = nc.tensor.transpose(pt[q][:, k * P:(k + 1) * P], r[:, q, k * P:(k + 1) * P], ident[:])
                    last.then_inc(r_turned, 1)

                def second(n, t, c, place):
                    q = c % 2
                    e = weights_of(t, place)
                    pe.wait_ge(hl_made, t + 1)
                    after(pe, y_made, t - 1)
                    for k in range(KF):
                        w = w2[:, bass.ds(e, 1), k]
                        h = slice(k * P, (k + 1) * P)
                        nc.tensor.matmul(py[q][:, 0:2, :], hh[:, q, h], w.rearrange("p o w d -> p (o w) d"),
                                         start=(k == 0), stop=False)
                        last = nc.tensor.matmul(py[q][:, 0, :], hl[:, q, h], w[:, :, 0], start=False,
                                                stop=(k == KF - 1))
                    last.then_inc(y_summed, 1)

                turn(0, 0, 0)
                turn(0, 1, 1)

                def step(n, t, c):
                    if c == 0:
                        held.clear()
                    if within(t, TT):
                        first(n, t, c)
                    if within(t - 1, TT):
                        turn_hidden(*behind(n, t, c, 1, U))
                    if within(t + 2, TT):
                        turn(*behind(n, t, c, -2, U))
                    if within(t - 2, TT):
                        second(*behind(n, t, c, 2, U), c - 2)

                rolled(pe, step, TT, U, 2)

            @block.scalar
            def _(act):
                def high(n, t, c):
                    q = c % 2
                    act.wait_ge(x_turned, t + 1)
                    act.activation(xh[:, q], pT[q][:, 0:P], ACT.Copy).then_inc(xh_made, 1)

                def hidden(n, t, c):
                    q = c % 2
                    act.wait_ge(z_made, t + 1)
                    act.activation(r[:, q], pz[q][:], ACT.Relu).then_inc(r_made, 1)

                def hidden_high(n, t, c):
                    q = c % 2
                    act.wait_ge(r_turned, t + 1)
                    act.activation(hh[:, q], pt[q][:], ACT.Copy).then_inc(hh_made, 1)

                def low_sums(n, t, c):
                    q = c % 2
                    act.wait_ge(y_summed, t + 1)
                    after(act, y_made, t - 1)
                    act.activation(yl[:, q], py[q][:, 1, :], ACT.Copy).then_inc(yl_made, 1)

                high(0, 0, 0)
                high(0, 1, 1)

                def step(n, t, c):
                    if within(t, TT):
                        hidden(n, t, c)
                    if within(t - 1, TT):
                        hidden_high(*behind(n, t, c, 1, U))
                    if within(t + 2, TT):
                        high(*behind(n, t, c, -2, U))
                    if within(t - 2, TT):
                        low_sums(*behind(n, t, c, 2, U))

                rolled(act, step, TT, U, 2)

            @block.vector
            def _(dve):
                def low(n, t, c):
                    q = c % 2
                    dve.wait_ge(xh_made, t + 1)
                    nc.vector.tensor_tensor(xl[:, q], pT[q][:, 0:P], xh[:, q].bitcast(F32), ALU.subtract)\
                        .then_inc(xl_made, 1)

                def hidden_low(n, t, c):
                    q = c % 2
                    dve.wait_ge(hh_made, t + 1)
                    nc.vector.tensor_tensor(hl[:, q], pt[q][:], hh[:, q].bitcast(F32), ALU.subtract).then_inc(hl_made, 1)

                def result(n, t, c):
                    q = c % 2
                    dve.wait_ge(yl_made, t + 1)
                    after(dve, stored[c % R], 16 * (U // R * n + c // R))
                    nc.vector.tensor_tensor(y[:, c % R], py[q][:, 0, :], yl[:, q], ALU.add).then_inc(y_made, 1)

                low(0, 0, 0)
                low(0, 1, 1)

                def step(n, t, c):
                    if within(t - 1, TT):
                        hidden_low(*behind(n, t, c, 1, U))
                    if within(t + 2, TT):
                        low(*behind(n, t, c, -2, U))
                    if within(t - 2, TT):
                        result(*behind(n, t, c, 2, U))

                rolled(dve, step, TT, U, 2)


def shared_experts(nc, a, sb, pb, sem, x1, ident, type_slot, eo_dram, qkv_dram, cwp, cres):
    NF = NSH * KF
    with ExitStack() as st:
        wraw = sb("c_wraw", [P, 3 * D], stack=st)
        wgm = sb("c_wgm", [P, 3 * D], stack=st)
        wh = sb("c_wh", [P, 3 * D], F32R, st)
        wl = sb("c_wl", [P, 3 * D], F32R, st)
        lng = sb("c_lng", [P, 1], stack=st)
        lnb = sb("c_lnb", [P, 1], stack=st)
        braw = sb("c_braw", [2, 3 * D], stack=st)
        bsum = sb("c_bsum", [2, 3 * D], stack=st)
        bhi = sb("c_bhi", [2, 3 * D], F32R, st)
        bmul = sb("c_bmul", [2, 3 * D], stack=st)
        bias = sb("c_bias", [2, 3 * D], F32R, st)
        lnb2 = sb("c_lnb2", [P, 2], stack=st)
        sgn = sb("c_sgn", [2, 2], stack=st)
        onesf = sb("c_onesf", [2, P], stack=st)
        onesr = sb("c_onesr", [2, P], F32R, st)
        g1 = sb("c_g1", [P, 3, D], stack=st)
        g2 = sb("c_g2", [P, 3], stack=st)
        gin = sb("c_gin", [P, 3, D], stack=st)
        gT = sb("c_gT", [P, 3, B], stack=st)
        gr = sb("c_gr", [P, B], stack=st)
        gmx = sb("c_gmx", [P, 1], stack=st)
        gx = sb("c_gx", [P, 3], stack=st)
        ge = sb("c_ge", [P, 3], stack=st)
        gs = sb("c_gs", [P, 1], stack=st)
        gi = sb("c_gi", [P, 1], stack=st)
        wgt = sb("c_wgt", [P, 3], stack=st)
        xb = sb("c_xb", [P, SB, D], stack=st)
        xh = sb("c_xh", [P, W], F32R, st)
        xl = sb("c_xl", [P, W], F32R, st)
        hh = sb("c_hh", [P, NF, W], F32R, st)
        hl = sb("c_hl", [P, NF, W], F32R, st)
        rows = sb("c_rows", [P, SB], I32, st)
        rows_made = sem("c_rows_made", st)
        bias_step = sem("c_bias_step", st)
        eo = sb("c_eo", [P, SB, D], stack=st)
        t0 = sb("c_t0", [P, SB, D], stack=st)
        t1 = sb("c_t1", [P, SB, D], stack=st)
        bs = sb("c_bs", [P, SB, 6], stack=st)
        mv = sb("c_mv", [P, SB, 2], stack=st)
        ve = sb("c_ve", [P, SB], stack=st)
        rs = sb("c_rs", [P, SB], stack=st)
        half = sb("c_half", [P, SB], stack=st)
        nm = sb("c_nm", [P, SB, D], stack=st)
        nh = sb("c_nh", [P, W], F32R, st)
        nl = sb("c_nl", [P, W], F32R, st)
        qkv = sb("c_qkv", [P, SB, 3 * D], stack=st)
        pT = pb("c_pT", [P, W], stack=st)
        pz = [pb(f"c_pz{k}", [P, W], stack=st) for k in range(3)]
        py = [pb(f"c_py{n}", [P, SB, D], stack=st) for n in range(NSH)]
        pq = [pb(f"c_pq{n}", [P, W], stack=st) for n in range(2)]
        names = ("w_loaded wg_made wh_made wl_made bias_summed xb_made x_turned xh_made xl_made z_made hh_made hl_made "
                 "y_summed eo_loaded t0_made t1_made c_made stats mv_made ve_made rs_made nm_made n_turned nh_made "
                 "nl_made qkv_summed qkv_made qkv_stored bias_made gin_made g_turned gT_made g_first gr_made g_second "
                 "gate_step ge_made halfed").split()
        s_ = {n: sem("c_" + n, st) for n in names}
        (w_loaded, wg_made, wh_made, wl_made, bias_summed, xb_made, x_turned, xh_made, xl_made, z_made, hh_made, hl_made,
         y_summed, eo_loaded, t0_made, t1_made, c_made, stats, mv_made, ve_made, rs_made, nm_made, n_turned, nh_made,
         nl_made, qkv_summed, qkv_made, qkv_stored, bias_made, gin_made, g_turned, gT_made, g_first, gr_made,
         g_second, gate_step, ge_made, halfed) = (s_[n] for n in names)

        with nc.Block() as block:
            @block.sync
            def _(sp):
                for dst, name in ((wraw[:], "w_qkv"), (lng[:], "ln1_g"), (lnb[:], "ln1_b"), (sgn[:], "signs"),
                                  (g1[:], "g1"), (g2[:], "g2")):
                    sp.dma_start(dst, a[name]).then_inc(w_loaded, 16)
                sp.dma_start(braw[:], a["b_qkv"].to_broadcast([2, 3 * D])).then_inc(w_loaded, 16)
                with sp.Fori(0, NB) as i:
                    sp.wait_ge(qkv_made, SB * i + SB)
                    sp.dma_start(qkv_dram[:, bass.ds(i * SB, SB), :], qkv[:]).then_inc(qkv_stored, 16)
                sp.wait_ge(qkv_stored, 16 * NB)

            @block.gpsimd
            def _(pool):
                pool.memset(half[:], -0.5).then_inc(halfed, 1)
                pool.wait_ge(halfed, 1)

                def fetch(i):
                    after(pool, x_turned, i)
                    pool.tensor_copy(xb[:], x1[:, bass.ds(i * SB, SB), :]).then_inc(xb_made, 1)
                    after(pool, eo_loaded, 16 * SB * i)
                    pool.wait_ge(xb_made, i + 1)
                    pool.tensor_copy(rows[:], type_slot[:, bass.ds(i * SB, SB)]).then_inc(rows_made, 1)
                    carry(pool, xb_made)
                    pool.wait_ge(rows_made, i + 1)
                    after(pool, t0_made, i)
                    for u in range(SB):
                        pool.indirect_dma_start(eo[:, u, :], None, eo_dram,
                                                bass.IndirectOffsetOnAxis(ap=rows[:, u:u + 1], axis=0))\
                            .then_inc(eo_loaded, 16)

                def root(i):
                    pool.wait_ge(ve_made, i + 1)
                    after(pool, nm_made, i)
                    pool.tensor_tensor(rs[:], ve[:], half[:], ALU.pow).then_inc(rs_made, 1)

                fetch(0)
                with pool.Fori(0, NB - 1) as i:
                    fetch(i + 1)
                    root(i)
                root(NB - 1)

            @block.tensor
            def _(pe):
                pe.wait_ge(bias_made, 1)
                nc.tensor.matmul(pz[0][0:2, 0:3 * D], lnb2[:], wraw[:], start=True, stop=True).then_inc(bias_summed, 1)
                pe.wait_ge(wl_made, 1)
                pe.wait_ge(bias_made, 2)

                def turn(i):
                    pe.wait_ge(xb_made, i + 1)
                    after(pe, nl_made, i - 1)
                    for u in range(SB):
                        last = nc.tensor.transpose(pT[:, u * D:(u + 1) * D], xb[:, u, :], ident[:])
                    last.then_inc(x_turned, 1)

                def first(i):
                    pe.wait_ge(xl_made, i + 1)
                    for f in range(NF):
                        after(pe, hl_made, NF * i + f - 2)
                        z = pz[f % 3]
                        w = B_SWI + f
                        nc.tensor.matmul(z[:], cwp[:, w, 0], xh[:], start=True, stop=False)
                        nc.tensor.matmul(z[:], cwp[:, w, 0], xl[:], start=False, stop=False)
                        nc.tensor.matmul(z[:], cwp[:, w, 1], xh[:], start=False, stop=True).then_inc(z_made, 1)

                def second(i, n):
                    pe.wait_ge(hl_made, NF * i + KF * (n + 1))
                    after(pe, c_made, i)
                    for u in range(SB):
                        for k in range(KF):
                            f = n * KF + k
                            w = B_SWO + f
                            t = slice(u * B, (u + 1) * B)
                            nc.tensor.matmul(py[n][:, u, :], hh[:, f, t], cwp[:, w, 0], start=(k == 0), stop=False)
                            nc.tensor.matmul(py[n][:, u, :], hh[:, f, t], cwp[:, w, 1], start=False, stop=False)
                            last = nc.tensor.matmul(py[n][:, u, :], hl[:, f, t], cwp[:, w, 0], start=False,
                                                    stop=(k == KF - 1))
                    last.then_inc(y_summed, 1)

                def gate():
                    pe.wait_ge(gin_made, 1)
                    for n in range(3):
                        last = nc.tensor.transpose(pq[0][:, n * B:(n + 1) * B], gin[:, n, :], ident[:])
                    last.then_inc(g_turned, 1)
                    pe.wait_ge(gT_made, 1)
                    for n in range(3):
                        last = nc.tensor.matmul(pq[1][:, 0:B], g1[:, n, :], gT[:, n, :], start=(n == 0), stop=(n == 2))
                    last.then_inc(g_first, 1)
                    pe.wait_ge(gr_made, 1)
                    nc.tensor.matmul(pq[0][:, 0:3], gr[:], g2[:], start=True, stop=True).then_inc(g_second, 1)

                def turn_normed(i):
                    pe.wait_ge(nm_made, i + 1)
                    after(pe, xl_made, i + 1)
                    for u in range(SB):
                        last = nc.tensor.transpose(pT[:, u * D:(u + 1) * D], nm[:, u, :], ident[:])
                    last.then_inc(n_turned, 1)

                def project(i):
                    pe.wait_ge(nl_made, i + 1)
                    for u in range(SB):
                        t = slice(u * B, (u + 1) * B)
                        o = pq[u % 2][:, 0:3 * D]
                        after(pe, qkv_made, SB * i + u - 1)
                        nc.tensor.matmul(o, onesr[:], bias[:], start=True, stop=False)
                        nc.tensor.matmul(o, nh[:, t], wh[:], start=False, stop=False)
                        nc.tensor.matmul(o, nh[:, t], wl[:], start=False, stop=False)
                        nc.tensor.matmul(o, nl[:, t], wh[:], start=False, stop=True).then_inc(qkv_summed, 1)

                turn(0)
                first(0)
                second(0, 0)
                turn(1)
                second(0, 1)
                gate()

                def rest(i, more):
                    first(i)
                    turn_normed(i - 1)
                    second(i, 0)
                    project(i - 1)
                    if more:
                        turn(i + 1)
                    second(i, 1)

                rest(1, True)
                with pe.Fori(2, NB - 1) as i:
                    rest(i, True)
                rest(NB - 1, False)
                turn_normed(NB - 1)
                project(NB - 1)

            @block.scalar
            def _(act):
                act.wait_ge(wg_made, 1)
                act.activation(wh[:], wgm[:], ACT.Copy).then_inc(wh_made, 1)

                def high(i):
                    act.wait_ge(x_turned, i + 1)
                    after(act, z_made, NF * i)
                    act.activation(xh[:], pT[:], ACT.Copy).then_inc(xh_made, 1)

                def hidden(i):
                    for f in range(NF):
                        after(act, y_summed, NSH * (i - 1) + f // KF + 1)
                        act.wait_ge(z_made, NF * i + f + 1)
                        act.activation(hh[:, f, :], pz[f % 3][:], ACT.Relu).then_inc(hh_made, 1)

                def gate():
                    act.wait_ge(g_turned, 1)
                    act.activation(gT[:].rearrange("p n b -> p (n b)"), pq[0][:, 0:3 * B], ACT.Copy).then_inc(gT_made, 1)
                    act.wait_ge(g_first, 1)
                    act.activation(gr[:], pq[1][:, 0:B], ACT.Relu).then_inc(gr_made, 1)
                    act.wait_ge(gate_step, 2)
                    act.activation(ge[:], gx[:], ACT.Exp).then_inc(ge_made, 1)

                def normed(i):
                    act.wait_ge(n_turned, i + 1)
                    after(act, qkv_summed, SB * i)
                    act.activation(nh[:], pT[:], ACT.Copy).then_inc(nh_made, 1)

                def project(i):
                    after(act, qkv_stored, 16 * i)
                    for u in range(SB):
                        act.wait_ge(qkv_summed, SB * i + u + 1)
                        act.activation(qkv[:, u, :], pq[u % 2][:, 0:3 * D], ACT.Copy).then_inc(qkv_made, 1)

                def scaled(i):
                    act.wait_ge(eo_loaded, 16 * SB * (i + 1))
                    after(act, t1_made, i)
                    act.activation(t0[:], eo[:], ACT.Copy, scale=wgt[:, 0:1]).then_inc(t0_made, 1)

                high(0)
                hidden(0)
                high(1)
                gate()
                act.wait_ge(gate_step, 6)
                scaled(0)

                def rest(i, more):
                    hidden(i)
                    normed(i - 1)
                    project(i - 1)
                    if more:
                        high(i + 1)
                    scaled(i)

                rest(1, True)
                with act.Fori(2, NB - 1) as i:
                    rest(i, True)
                rest(NB - 1, False)
                normed(NB - 1)
                project(NB - 1)

            @block.vector
            def _(dve):
                dve.wait_ge(w_loaded, 16 * 7)
                nc.vector.tensor_copy(lnb2[:], lnb[:].to_broadcast([P, 2])).then_inc(bias_made, 1)
                nc.vector.tensor_scalar(wgm[:], wraw[:], lng[:, 0:1], None, ALU.mult).then_inc(wg_made, 1)
                dve.wait_ge(wh_made, 1)
                nc.vector.tensor_tensor(wl[:], wgm[:], wh[:].bitcast(F32), ALU.subtract).then_inc(wl_made, 1)

                def link(ins, n):
                    ins.then_inc(bias_step, 1)
                    dve.wait_ge(bias_step, n)

                dve.wait_ge(bias_summed, 1)
                nc.vector.memset(onesf[:], 1.0)
                link(nc.vector.tensor_tensor(bsum[:], pz[0][0:2, 0:3 * D], braw[:], ALU.add), 1)
                nc.vector.tensor_copy(onesr[:], onesf[:])
                link(nc.vector.tensor_copy(bhi[:], bsum[:]), 2)
                link(nc.vector.tensor_scalar(bmul[:], bsum[:], sgn[:, 0:1], None, ALU.mult), 3)
                nc.vector.scalar_tensor_tensor(bias[:], bhi[:].bitcast(F32), sgn[:, 1:2], bmul[:], ALU.mult, ALU.add)\
                    .then_inc(bias_made, 1)

                def low(i):
                    dve.wait_ge(xh_made, i + 1)
                    nc.vector.tensor_tensor(xl[:], pT[:], xh[:].bitcast(F32), ALU.subtract).then_inc(xl_made, 1)

                def hidden(i):
                    for f in range(NF):
                        dve.wait_ge(hh_made, NF * i + f + 1)
                        nc.vector.scalar_tensor_tensor(hl[:, f, :], pz[f % 3][:], 0.0, hh[:, f, :].bitcast(F32),
                                                       ALU.max, ALU.subtract).then_inc(hl_made, 1)

                def gate():
                    def link(ins, n):
                        ins.then_inc(gate_step, 1)
                        dve.wait_ge(gate_step, n)

                    dve.wait_ge(eo_loaded, 16 * SB)
                    dve.wait_ge(y_summed, NSH)
                    nc.vector.tensor_copy(gin[:, 0, :], eo[:, 0, :])
                    for n in range(NSH):
                        last = nc.vector.tensor_copy(gin[:, n + 1, :], py[n][:, 0, :])
                    last.then_inc(gin_made, 1)
                    dve.wait_ge(g_second, 1)
                    link(nc.vector.tensor_reduce(gmx[:], pq[0][:, 0:3], AX, ALU.max), 1)
                    link(nc.vector.tensor_scalar(gx[:], pq[0][:, 0:3], gmx[:, 0:1], None, ALU.subtract), 2)
                    dve.wait_ge(ge_made, 1)
                    link(nc.vector.tensor_reduce(gs[:], ge[:], AX, ALU.add), 3)
                    link(nc.vector.reciprocal(gi[:], gs[:]), 4)
                    link(nc.vector.tensor_scalar(wgt[:], ge[:], gi[:, 0:1], None, ALU.mult), 5)
                    link(nc.vector.memset(gs[:], 0.0), 6)

                def mix(i):
                    dve.wait_ge(t0_made, i + 1)
                    dve.wait_ge(y_summed, NSH * (i + 1))
                    nc.vector.scalar_tensor_tensor(t1[:], py[0][:], wgt[:, 1:2], t0[:], ALU.mult, ALU.add).then_inc(t1_made, 1)
                    dve.wait_ge(t1_made, i + 1)
                    c = cres[:, bass.ds(i * SB, SB), :]
                    nc.vector.scalar_tensor_tensor(c, py[1][:], wgt[:, 2:3], t1[:], ALU.mult, ALU.add).then_inc(c_made, 1)
                    carry(dve, t1_made)
                    dve.wait_ge(c_made, i + 1)
                    for u in range(SB):
                        last = nc.vector.bn_stats(bs[:, u, :], cres[:, i * SB + u, :])
                    last.then_inc(stats, 1)
                    carry(dve, c_made)
                    dve.wait_ge(stats, i + 1)
                    for u in range(SB):
                        last = nc.vector.bn_aggr(mv[:, u, :], bs[:, u, :])
                    last.then_inc(mv_made, 1)
                    dve.wait_ge(mv_made, i + 1)
                    nc.vector.tensor_scalar(ve[:], mv[:, :, 1], EPS, None, ALU.add).then_inc(ve_made, 1)
                    dve.wait_ge(rs_made, i + 1)
                    after(dve, n_turned, i)
                    for u in range(SB):
                        last = nc.vector.tensor_scalar(nm[:, u, :], cres[:, i * SB + u, :], mv[:, u, 0:1],
                                                       rs[:, u:u + 1], ALU.subtract, ALU.mult)
                    last.then_inc(nm_made, 1)

                def normed(i):
                    dve.wait_ge(nh_made, i + 1)
                    nc.vector.tensor_tensor(nl[:], pT[:], nh[:].bitcast(F32), ALU.subtract).then_inc(nl_made, 1)

                low(0)
                hidden(0)
                low(1)
                gate()
                mix(0)

                def rest(i, more):
                    hidden(i)
                    normed(i - 1)
                    if more:
                        low(i + 1)
                    mix(i)

                rest(1, True)
                with dve.Fori(2, NB - 1) as i:
                    rest(i, True)
                rest(NB - 1, False)
                normed(NB - 1)


def attention(nc, a, sb, pb, sem, ident, hmask, qkv_dram, att_dram, mwp):
    SC = 1.0 / float(np.sqrt(DK))
    NQ = B // BT
    C4 = P // S
    NS = NQ // C4
    GW = D // HG
    MC = MB // NQ
    with ExitStack() as st:
        quad = sb("t_quad", [P, BT], stack=st)
        qk = sb("t_qk", [P, BT, 2, HG, GW], stack=st)
        qkg = sb("t_qkg", [P, 2, HG, BT, GW], stack=st)
        vt = sb("t_vt", [P, C4, BT, D], stack=st)
        vs = sb("t_vs", [P, 2, BT, HG, GW], stack=st)
        qs = sb("t_qs", [P, 2, HG, BT, S], stack=st)
        ks = sb("t_ks", [P, 2, HG, HG, S], stack=st)
        sm = sb("t_sm", [P, H, S], stack=st)
        p = sb("t_p", [P, 2, H, S], stack=st)
        pn = sb("t_pn", [P, 2, H, S], stack=st)
        ptT = sb("t_ptT", [P, 2, HG, P], stack=st)
        oT = sb("t_oT", [P, 2, P], stack=st)
        mx = sb("t_mx", [P, H], stack=st)
        su = sb("t_su", [P, H], stack=st)
        ri = sb("t_ri", [P, H], stack=st)
        wo = sb("t_wo", [P, D], stack=st)
        bo = sb("t_bo", [P, D], stack=st)
        att = sb("t_att", [P, 2, D], stack=st)
        raw = sb("t_raw", [P, 2, MC, D], stack=st)
        pq = pb("t_pq", [P, HG, P], stack=st)
        pk = pb("t_pk", [P, HG, P], stack=st)
        ps = [pb(f"t_ps{n}", [P, H, S], stack=st) for n in range(2)]
        pt = [pb(f"t_pt{n}", [P, HG, P], stack=st) for n in range(2)]
        po = pb("t_po", [P, 512], stack=st)
        pj = pb("t_pj", [P, 512], stack=st)
        names = ("w_loaded qk_loaded grouped turned qs_made ks_made scored mx_made sub_made p_made su_made ri_made "
                 "pn_made p_turned ptT_made vs_made o_summed oT_made w_summed att_made high low").split()
        s_ = {n: sem("t_" + n, st) for n in names}
        (w_loaded, qk_loaded, grouped, turned, qs_made, ks_made, scored, mx_made, sub_made, p_made, su_made, ri_made,
         pn_made, p_turned, ptT_made, vs_made, o_summed, oT_made, w_summed, att_made, high, low) = (s_[n] for n in names)
        v_loaded = [sem(f"t_v_loaded{c}", st) for c in range(C4)]
        att_stored = [sem(f"t_att_stored{c}", st) for c in range(2)]
        raw_loaded = [sem(f"t_raw_loaded{c}", st) for c in range(2)]
        qk_rows = qkv_dram[:, :, 0:2 * D].rearrange("(n c b) s (w g d) -> n c s b w g d", n=NS, c=C4, w=2, g=HG)
        v_rows = qkv_dram[:, :, 2 * D:].rearrange("(n b) s d -> n s b d", n=NQ)
        att_rows = att_dram.rearrange("(n b) s d -> n (b s) d", n=NQ)

        def quartets(eng, step, drain):
            rolled(eng, step, NQ, C4, drain)

        def has(t, back=0):
            return within(t - back, NQ)

        with nc.Block() as block:
            @block.sync
            def _(sp):
                sp.dma_start(wo[:], a["w_o"]).then_inc(w_loaded, 16)
                sp.dma_start(bo[:], a["b_o"].to_broadcast([P, D])).then_inc(w_loaded, 16)
                sp.dma_start(quad[:], a["quad"]).then_inc(w_loaded, 16)

                def load_qk(n):
                    for c in range(C4):
                        src = qk_rows[n, c] if isinstance(n, int) else \
                            qk_rows[bass.ds(n, 1), c].rearrange("o s b w g d -> (o s) b w g d")
                        sp.dma_start(qk[c * S:(c + 1) * S].rearrange("s b w g d -> s b (w g d)"),
                                     src.rearrange("s b w g d -> s b (w g d)")).then_inc(qk_loaded, 16)

                def load_v(t, c):
                    src = v_rows[t] if isinstance(t, int) else v_rows[bass.ds(t, 1)].rearrange("o s b d -> (o s) b d")
                    for j in range(HG):
                        sp.dma_start(vt[j * S:(j + 1) * S, c], src).then_inc(v_loaded[c], 16)

                def load_raw(t, c):
                    cols = slice(t * MC, (t + 1) * MC) if isinstance(t, int) else bass.ds(t * MC, MC)
                    sp.dma_start(raw[:, c % 2], a["mw"][:, cols, :]).then_inc(raw_loaded[c % 2], 16)

                load_qk(0)
                for c in range(2):
                    load_raw(c, c)
                for c in range(C4):
                    load_v(c, c)

                def step(n, t, c):
                    if c == 1 and within(n + 1, NS):
                        sp.wait_ge(grouped, n + 1)
                        load_qk(n + 1)
                    if has(t, -2):
                        sp.wait_ge(low, t + 1)
                        load_raw(t + 2, c)
                    if has(t, -C4):
                        sp.wait_ge(vs_made, t + 1)
                        load_v(t + C4, c)
                    if has(t, 3):
                        sp.wait_ge(att_made, t - 2)
                        q = (c - 3) % 2
                        dst = att_rows[t - 3] if isinstance(t, int) else \
                            att_rows[bass.ds(t - 3, 1)].rearrange("o p d -> (o p) d")
                        sp.dma_start(dst, att[:, q]).then_inc(att_stored[q], 16)

                quartets(sp, step, 3)
                for q in range(2):
                    sp.wait_ge(att_stored[q], 16 * (NQ // 2))

            @block.gpsimd
            def _(pool):
                pool.wait_ge(w_loaded, 48)

                def values(n, t, c):
                    pool.wait_ge(v_loaded[c], 16 * HG * n + 16 * HG)
                    after(pool, o_summed, t - 1)
                    pool.tensor_tensor(vs[:, c % 2].rearrange("p b g (j d) -> p (b g) j d", j=HG),
                                       vt[:, c].rearrange("p b (g j d) -> p (b g) j d", g=HG, j=HG),
                                       quad[:, None, :, None].to_broadcast([P, BT * HG, HG, DK]),
                                       ALU.mult).then_inc(vs_made, 1)

                def step(n, t, c):
                    values(n, t, c)
                    cols = slice(t * MC, (t + 1) * MC) if isinstance(t, int) else bass.ds(t * MC, MC)
                    pool.wait_ge(raw_loaded[c % 2], 32 * n + 16 * (c // 2) + 16)
                    pool.tensor_copy(mwp[:, cols, 0], raw[:, c % 2]).then_inc(high, 1)
                    pool.wait_ge(high, t + 1)
                    pool.tensor_tensor(mwp[:, cols, 1], raw[:, c % 2], mwp[:, cols, 0].bitcast(F32), ALU.subtract)\
                        .then_inc(low, 1)

                quartets(pool, step, 0)

            @block.tensor
            def _(pe):
                def turn_qk(n):
                    pe.wait_ge(grouped, n + 1)
                    after(pe, qs_made, C4 * n)
                    after(pe, ks_made, C4 * n)
                    for w, dst in enumerate((pq, pk)):
                        for g in range(HG):
                            last = nc.tensor.transpose(dst[:, g, :], qkg[:, w, g].rearrange("p b d -> p (b d)"), ident[:])
                    last.then_inc(turned, 1)

                def scores(t, q):
                    pe.wait_ge(qs_made, t + 1)
                    pe.wait_ge(ks_made, t + 1)
                    after(pe, sub_made, t - 1)
                    for g in range(HG):
                        last = nc.tensor.matmul(ps[q][:, g * HG:(g + 1) * HG, :], qs[:, q, g].rearrange("p b s -> p (b s)"),
                                                ks[:, q, g], start=True, stop=True)
                    last.then_inc(scored, 1)

                def turn_p(t, q):
                    pe.wait_ge(pn_made, t + 1)
                    after(pe, ptT_made, t - 1)
                    for g in range(HG):
                        last = nc.tensor.transpose(pt[q][:, g, :],
                                                   pn[:, q, g * HG:(g + 1) * HG].rearrange("p j k -> p (j k)"), ident[:])
                    last.then_inc(p_turned, 1)

                def values(t, q):
                    pe.wait_ge(ptT_made, t + 1)
                    pe.wait_ge(vs_made, t + 1)
                    after(pe, oT_made, t)
                    for b in range(BT):
                        for g in range(HG):
                            last = nc.tensor.matmul(po[g * GW:(g + 1) * GW, b * S:(b + 1) * S], vs[:, q, b, g],
                                                    ptT[:, q, g, b * S:(b + 1) * S], start=True, stop=True)
                    last.then_inc(o_summed, 1)

                def project(t, q):
                    pe.wait_ge(oT_made, t + 1)
                    after(pe, att_made, t)
                    nc.tensor.matmul(pj[:, 0:D], oT[:, q], wo[:], start=True, stop=True).then_inc(w_summed, 1)

                pe.wait_ge(w_loaded, 48)
                turn_qk(0)

                def step(n, t, c):
                    if has(t):
                        scores(t, c % 2)
                    if has(t, 2):
                        turn_p(t - 2, c % 2)
                    if has(t, 3):
                        project(t - 3, (c - 3) % 2)
                    if has(t, 2):
                        values(t - 2, c % 2)
                    if c == 2 and within(n + 1, NS):
                        turn_qk(n + 1)

                quartets(pe, step, 3)

            @block.scalar
            def _(act):
                def group(n):
                    act.wait_ge(qk_loaded, 16 * C4 * n + 16 * C4)
                    after(act, turned, n)
                    for w in range(2):
                        last = act.activation(qkg[:, w], qk[:, :, w].rearrange("p b g d -> p g b d"), ACT.Copy)
                    last.then_inc(grouped, 1)

                def keys(n, t, c):
                    act.wait_ge(turned, n + 1)
                    after(act, scored, t - 1)
                    for j in range(HG):
                        last = act.activation(ks[:, c % 2, :, j, :], pk[:, :, c * S:(c + 1) * S], ACT.Copy,
                                              scale=hmask[:, j:j + 1])
                    last.then_inc(ks_made, 1)

                def exps(t, q):
                    act.wait_ge(sub_made, t + 1)
                    after(act, pn_made, t - 1)
                    act.activation(p[:, q], sm[:], ACT.Exp, scale=SC).then_inc(p_made, 1)

                def probs(t, q):
                    act.wait_ge(p_turned, t + 1)
                    after(act, o_summed, t - 1)
                    act.activation(ptT[:, q], pt[q][:], ACT.Copy).then_inc(ptT_made, 1)

                def outs(t, q):
                    act.wait_ge(o_summed, t + 1)
                    after(act, w_summed, t - 1)
                    act.activation(oT[:, q], po[:, 0:P], ACT.Copy).then_inc(oT_made, 1)

                group(0)
                keys(0, 0, 0)

                def step(n, t, c):
                    if has(t, 2):
                        probs(t - 2, c % 2)
                    if has(t, -1):
                        keys(n if c + 1 < C4 else n + 1, t + 1, (c + 1) % C4)
                    if has(t):
                        exps(t, c % 2)
                    if has(t, 2):
                        outs(t - 2, c % 2)
                    if c == 1 and within(n + 1, NS):
                        group(n + 1)

                quartets(act, step, 2)

            @block.vector
            def _(dve):
                def queries(n, t, c):
                    dve.wait_ge(turned, n + 1)
                    after(dve, scored, t - 1)
                    nc.vector.tensor_tensor(qs[:, c % 2], pq[:, :, None, c * S:(c + 1) * S].to_broadcast([P, HG, BT, S]),
                                            quad[:, None, :, None].to_broadcast([P, HG, BT, S]), ALU.mult)\
                        .then_inc(qs_made, 1)

                def maxima(t, q):
                    dve.wait_ge(scored, t + 1)
                    after(dve, sub_made, t)
                    nc.vector.tensor_reduce(mx[:], ps[q][:], AX, ALU.max).then_inc(mx_made, 1)
                    dve.wait_ge(mx_made, t + 1)
                    after(dve, p_made, t)
                    nc.vector.tensor_tensor(sm[:], ps[q][:], mx[:, :, None].to_broadcast([P, H, S]), ALU.subtract)\
                        .then_inc(sub_made, 1)

                def normalised(t, q):
                    dve.wait_ge(p_made, t + 1)
                    nc.vector.tensor_reduce(su[:], p[:, q], AX, ALU.add).then_inc(su_made, 1)
                    dve.wait_ge(su_made, t + 1)
                    after(dve, pn_made, t)
                    nc.vector.reciprocal(ri[:], su[:]).then_inc(ri_made, 1)
                    dve.wait_ge(ri_made, t + 1)
                    after(dve, p_turned, t - 1)
                    nc.vector.tensor_tensor(pn[:, q], p[:, q], ri[:, :, None].to_broadcast([P, H, S]), ALU.mult)\
                        .then_inc(pn_made, 1)

                def result(n, t, c):
                    dve.wait_ge(w_summed, t + 1)
                    after(dve, att_stored[c % 2], 16 * (2 * n + c // 2))
                    nc.vector.tensor_tensor(att[:, c % 2], pj[:, 0:D], bo[:], ALU.add).then_inc(att_made, 1)

                dve.wait_ge(w_loaded, 48)
                queries(0, 0, 0)

                def step(n, t, c):
                    if has(t, -1):
                        queries(n if c + 1 < C4 else n + 1, t + 1, (c + 1) % C4)
                    if has(t):
                        maxima(t, c % 2)
                    if has(t, 1):
                        normalised(t - 1, (c - 1) % 2)
                    if has(t, 3):
                        result(n - 1 + (c + 1) // C4, t - 3, (c + 1) % C4)

                quartets(dve, step, 3)


def second_norm(nc, a, sb, pb, sem, ident, x1, cres, att_dram, h2, logits, ms_dram):
    with ExitStack() as st:
        att = sb("d_att", [P, SB, D], stack=st)
        x2 = sb("d_x2", [P, SB, D], stack=st)
        bs = sb("d_bs", [P, SB, 6], stack=st)
        mv = sb("d_mv", [P, SB, 2], stack=st)
        ve = sb("d_ve", [P, SB], stack=st)
        rs = sb("d_rs", [P, SB], stack=st)
        half = sb("d_half", [P, SB], stack=st)
        nm = sb("d_nm", [P, SB, D], stack=st)
        ng = sb("d_ng", [P, SB, D], stack=st)
        hb = sb("d_hb", [P, SB, D], stack=st)
        hT = sb("d_hT", [P, W], stack=st)
        gbt = sb("d_gbt", [P, 2, D], stack=st)
        gw = sb("d_gw", [P, E], stack=st)
        gbias = sb("d_gbias", [P, E], stack=st)
        pT = pb("d_pT", [P, W], stack=st)
        pl = pb("d_pl", [P, 512], stack=st)
        names = ("w_loaded att_loaded x2_made x1_made stats mv_made ve_made rs_made nm_made ng_made hb_made h_turned "
                 "hT_made h2_made summed l_made halfed").split()
        s_ = {n: sem("d_" + n, st) for n in names}
        (w_loaded, att_loaded, x2_made, x1_made, stats, mv_made, ve_made, rs_made, nm_made, ng_made, hb_made, h_turned,
         hT_made, h2_made, summed, l_made, halfed) = (s_[n] for n in names)

        with nc.Block() as block:
            @block.sync
            def _(sp):
                sp.dma_start(gbt[:], a["ln2"].to_broadcast([P, 2 * D]).rearrange("p (n d) -> p n d", n=2)).then_inc(w_loaded, 16)
                sp.dma_start(gw[:], a["gate_w"]).then_inc(w_loaded, 16)
                sp.dma_start(gbias[:], a["gate_b"].to_broadcast([P, E])).then_inc(w_loaded, 16)
                sp.dma_start(att[:], att_dram[:, 0:SB, :]).then_inc(att_loaded, 16)
                with sp.Fori(0, NB - 1) as i:
                    sp.wait_ge(x2_made, i + 1)
                    sp.dma_start(att[:], att_dram[:, bass.ds((i + 1) * SB, SB), :]).then_inc(att_loaded, 16)

            @block.gpsimd
            def _(pool):
                pool.memset(half[:], -0.5).then_inc(halfed, 1)
                pool.wait_ge(halfed, 1)
                pool.wait_ge(w_loaded, 48)
                with pool.Fori(0, NB) as i:
                    pool.wait_ge(ve_made, i + 1)
                    pool.wait_ge(nm_made, i)
                    pool.tensor_tensor(rs[:], ve[:], half[:], ALU.pow).then_inc(rs_made, 1)
                    pool.wait_ge(x2_made, i + 1)
                    pool.wait_ge(x1_made, i)
                    v = x1[:, bass.ds(i * SB, SB), :]
                    pool.tensor_tensor(v, v, x2[:], ALU.add).then_inc(x1_made, 1)
                    pool.wait_ge(nm_made, i + 1)
                    pool.tensor_tensor(ng[:], nm[:], gbt[:, 0:1, :].to_broadcast([P, SB, D]), ALU.mult).then_inc(ng_made, 1)
                    pool.wait_ge(ng_made, i + 1)
                    pool.wait_ge(h2_made, i)
                    pool.wait_ge(h_turned, i)
                    pool.tensor_tensor(hb[:], ng[:], gbt[:, 1:2, :].to_broadcast([P, SB, D]), ALU.add).then_inc(hb_made, 1)

            @block.tensor
            def _(pe):
                pe.wait_ge(w_loaded, 48)
                with pe.Fori(0, NB) as i:
                    pe.wait_ge(hb_made, i + 1)
                    pe.wait_ge(hT_made, i)
                    for u in range(SB):
                        last = nc.tensor.transpose(pT[:, u * D:(u + 1) * D], hb[:, u, :], ident[:])
                    last.then_inc(h_turned, 1)
                    pe.wait_ge(hT_made, i + 1)
                    pe.wait_ge(l_made, i)
                    for u in range(SB):
                        last = nc.tensor.matmul(pl[:, u * E:(u + 1) * E], hT[:, u * B:(u + 1) * B], gw[:], start=True, stop=True)
                    last.then_inc(summed, 1)

            @block.scalar
            def _(act):
                with act.Fori(0, NB) as i:
                    act.wait_ge(hb_made, i + 1)
                    act.activation(h2[:, bass.ds(i * SB, SB), 0:D], hb[:], ACT.Copy).then_inc(h2_made, 1)
                    act.wait_ge(h_turned, i + 1)
                    act.wait_ge(summed, i)
                    act.activation(hT[:], pT[:], ACT.Copy).then_inc(hT_made, 1)

            @block.vector
            def _(dve):
                dve.wait_ge(w_loaded, 48)
                with dve.Fori(0, NB) as i:
                    dve.wait_ge(att_loaded, 16 * i + 16)
                    dve.wait_ge(x1_made, i)
                    nc.vector.tensor_tensor(x2[:], cres[:, bass.ds(i * SB, SB), :], att[:], ALU.add).then_inc(x2_made, 1)
                    dve.wait_ge(x2_made, i + 1)
                    for u in range(SB):
                        last = nc.vector.bn_stats(bs[:, u, :], x2[:, u, :])
                    last.then_inc(stats, 1)
                    carry(dve, x2_made)
                    dve.wait_ge(stats, i + 1)
                    for u in range(SB):
                        last = nc.vector.bn_aggr(mv[:, u, :], bs[:, u, :])
                    last.then_inc(mv_made, 1)
                    dve.wait_ge(mv_made, i + 1)
                    nc.vector.tensor_scalar(ve[:], mv[:, :, 1], EPS, None, ALU.add).then_inc(ve_made, 1)
                    dve.wait_ge(rs_made, i + 1)
                    dve.wait_ge(ng_made, i)
                    for u in range(SB):
                        last = nc.vector.tensor_scalar(nm[:, u, :], x2[:, u, :], mv[:, u, 0:1], rs[:, u:u + 1],
                                                       ALU.subtract, ALU.mult)
                    last.then_inc(nm_made, 1)
                    dve.wait_ge(summed, i + 1)
                    nc.vector.tensor_tensor(logits[:, bass.ds(i * SB, SB), :],
                                            pl[:, 0:SB * E].rearrange("p (u e) -> p u e", e=E),
                                            gbias[:, None, :].to_broadcast([P, SB, E]), ALU.add).then_inc(l_made, 1)


def route(nc, a, sb, pb, sem, ones, tri, h2, logits, expert_of_tile, ms_dram):
    SE = [P, S, E]
    with ExitStack() as st:
        c = sb("r_c", [P, 2 * E + S + ET + 2], stack=st)
        padr = sb("r_padr", [P, ROW], stack=st)
        padi = sb("r_padi", [P, ET], I32, st)
        zero = sb("r_zero", [P, ET, ROW], stack=st)
        m1, m2, r1, r2, dl, ex, ex1, w1, w2, sf = (sb("r_" + n, [P, S], stack=st) for n in
                                                  ("m1", "m2", "r1", "r2", "dl", "ex", "ex1", "w1", "w2", "sf"))
        eq, ew, k1, k2, l2, both, inc, exc, rank, pick = (sb("r_" + n, SE, stack=st) for n in
                                                          ("eq", "ew", "k1", "k2", "l2", "both", "inc", "exc", "rank", "pick"))
        tot, cnt, padf, endt, offs, base = (sb("r_" + n, [P, E], stack=st) for n in
                                            ("tot", "cnt", "padf", "endt", "offs", "base"))
        cnti = sb("r_cnti", [P, E], I32, st)
        cnts = sb("r_cnts", [P, E], I32, st)
        past = sb("r_past", [1, E - 1, ET], stack=st)
        totile = sb("r_totile", [1, ET], stack=st)
        slots = [sb(f"r_slots{k}", [P, S], I32, st) for k in range(2)]
        dests = [sb(f"r_dests{k}", [P, S], I32, st) for k in range(2)]
        rows = sb("r_rows", [P, SB], I32, st)
        pc = pb("r_pc", [P, 512], stack=st)
        pp = pb("r_pp", [P, 512], stack=st)
        c_loaded, pad_loaded, pad_made, pad_stored, step, totals, prefix, ex_made, dl_made, slots_made, sent, tagged, \
            zeroed, rows_made = (sem("r_" + n, st) for n in (
                "c_loaded", "pad_loaded", "pad_made", "pad_stored", "step", "totals", "prefix", "ex_made", "dl_made",
                "slots_made", "sent", "tagged", "zeroed", "rows_made"))
        C_W, C_1, C_T, C_Q, C_D = np.cumsum([0, E, E, ET, S]).tolist()

        with nc.Block() as block:
            @block.sync
            def _(sp):
                sp.dma_start(c[:, 0:E + E + ET + S], a["rconsts"]).then_inc(c_loaded, 16)
                sp.dma_start(padi[:], a["pads"]).then_inc(pad_loaded, 16)
                sp.wait_ge(pad_made, 1)
                sp.dma_start(ms_dram.rearrange("(j p) c -> p j c", p=P), zero[:]).then_inc(pad_stored, 16)

            @block.gpsimd
            def _(pool):
                pool.memset(zero[:], 0.0).then_inc(zeroed, 1)
                pool.wait_ge(zeroed, 1)
                pool.wait_ge(pad_loaded, 16)
                pool.tensor_copy(zero[:, :, D:D + 1].bitcast(I32), padi[:, :, None]).then_inc(pad_made, 1)
                pool.wait_ge(pad_stored, 16)
                for k in range(2):
                    pool.wait_ge(tagged, k + 1)
                    for s in range(S):
                        pool.indirect_dma_start(ms_dram, bass.IndirectOffsetOnAxis(ap=slots[k][:, s:s + 1], axis=0),
                                                h2[:, s, :], None).then_inc(sent, 16)
                    pool.wait_ge(sent, 16 * S * (k + 1))

            @block.tensor
            def _(pe):
                pe.wait_ge(totals, 1)
                nc.tensor.matmul(pc[:, 0:E], ones[:], tot[:], start=True, stop=True)
                nc.tensor.matmul(pp[:, 0:E], tri[:], tot[:], start=True, stop=True).then_inc(prefix, 1)

            @block.scalar
            def _(act):
                act.wait_ge(dl_made, 1)
                act.activation(ex[:], dl[:], ACT.Exp).then_inc(ex_made, 1)

            @block.vector
            def _(dve):
                done = [0]

                def link(ins):
                    done[0] += 1
                    ins.then_inc(step, 1)
                    dve.wait_ge(step, done[0])

                order = c[:, None, C_W:C_1].to_broadcast(SE)
                wide = lambda t: t[:, :, None].to_broadcast(SE)
                dve.wait_ge(c_loaded, 16)

                def best(values, m, r, k):
                    link(nc.vector.tensor_reduce(m[:], values, AX, ALU.max))
                    link(nc.vector.tensor_tensor(eq[:], values, wide(m), ALU.is_equal))
                    link(nc.vector.tensor_tensor(ew[:], eq[:], order, ALU.mult))
                    link(nc.vector.tensor_reduce(r[:], ew[:], AX, ALU.max))
                    link(nc.vector.tensor_tensor(k[:], order, wide(r), ALU.is_equal))

                best(logits[:], m1, r1, k1)
                link(nc.vector.scalar_tensor_tensor(l2[:], k1[:], -3.0e38, logits[:], ALU.mult, ALU.add))
                best(l2[:], m2, r2, k2)
                nc.vector.tensor_tensor(dl[:], m2[:], m1[:], ALU.subtract).then_inc(dl_made, 1)
                link(nc.vector.tensor_tensor(both[:], k1[:], k2[:], ALU.add))
                for e in range(E):
                    link(nc.vector.tensor_tensor_scan(inc[:, :, e], ones[:, 0:S], both[:, :, e], 0.0, ALU.mult, ALU.add))
                nc.vector.tensor_copy(tot[:], inc[:, S - 1, :]).then_inc(totals, 1)
                link(nc.vector.tensor_tensor(exc[:], inc[:], both[:], ALU.subtract))
                dve.wait_ge(prefix, 1)
                link(nc.vector.tensor_scalar(cnt[:], pc[:, 0:E], float(P - 1), None, ALU.add))
                link(nc.vector.tensor_copy(cnti[:], cnt[:]))
                link(nc.vector.tensor_scalar(cnts[:], cnti[:], 7, 7, ALU.logical_shift_right, ALU.logical_shift_left))
                link(nc.vector.tensor_copy(padf[:], cnts[:]))
                link(nc.vector.tensor_tensor_scan(endt[:], ones[:, 0:E], padf[:], 0.0, ALU.mult, ALU.add))
                link(nc.vector.tensor_tensor(offs[:], endt[:], padf[:], ALU.subtract))
                link(nc.vector.tensor_tensor(base[:], pp[:, 0:E], offs[:], ALU.add))
                link(nc.vector.tensor_tensor(rank[:], exc[:], base[:, None, :].to_broadcast(SE), ALU.add))
                for k, one in enumerate((k1, k2)):
                    link(nc.vector.tensor_tensor(pick[:], rank[:], one[:], ALU.mult))
                    link(nc.vector.tensor_reduce(sf[:], pick[:], AX, ALU.add))
                    link(nc.vector.tensor_copy(slots[k][:], sf[:]))
                    link(nc.vector.tensor_scalar(dests[k][:], c[:, C_Q:C_D], float(k * T), None, ALU.add))
                dve.wait_ge(ex_made, 1)
                link(nc.vector.tensor_scalar(ex1[:], ex[:], 1.0, None, ALU.add))
                link(nc.vector.reciprocal(w1[:], ex1[:]))
                link(nc.vector.tensor_tensor(w2[:], ex[:], w1[:], ALU.mult))
                for k, wk in enumerate((w1, w2)):
                    if k:
                        dve.wait_ge(sent, 16 * S)
                    link(nc.vector.tensor_copy(h2[:, :, D:D + 1].bitcast(I32), dests[k][:, :, None]))
                    nc.vector.tensor_copy(h2[:, :, D + 1:D + 2], wk[:, :, None]).then_inc(tagged, 1)
                for n in range(E - 1):
                    link(nc.vector.tensor_scalar(past[0:1, n, :], c[0:1, C_T:C_T + ET], endt[0:1, n:n + 1], None, ALU.is_ge))
                link(nc.vector.tensor_reduce(totile[0:1, :], past[0:1, :, :].rearrange("p n j -> p j n"), AX, ALU.add))
                link(nc.vector.tensor_copy(expert_of_tile[0:1, :], totile[0:1, :]))


def experts(nc, a, sb, pb, sem, ident, expert_of_tile, ms_dram, y_dram, mwp):
    U, R = TILE_UNROLL, 3
    with ExitStack() as st:
        b1 = sb("x_b1", [P, E * FF], stack=st)
        b2r = sb("x_b2r", [2, E * D], stack=st)
        b2h = sb("x_b2h", [2, E * D], F32R, st)
        b2m = sb("x_b2m", [2, E * D], stack=st)
        b2 = sb("x_b2", [2, E * D], F32R, st)
        sgn = sb("x_sgn", [2, 2], stack=st)
        onesf = sb("x_onesf", [2, P], stack=st)
        onesr = sb("x_onesr", [2, P], F32R, st)
        xs = [sb(f"x_xs{q}", [P, ROW], stack=st) for q in range(U)]
        none = sb("x_none", [P, 1], I32, st)
        idx = [sb(f"x_idx{q}", [P, 1], I32, st) for q in range(R)]
        xh = sb("x_xh", [P, 2, P], F32R, st)
        xl = sb("x_xl", [P, 2, P], F32R, st)
        r = sb("x_r", [P, 2, FF], stack=st)
        hh = sb("x_hh", [P, 2, FF], F32R, st)
        hl = sb("x_hl", [P, 2, FF], F32R, st)
        yl = sb("x_yl", [P, 2, D], stack=st)
        y = sb("x_y", [P, R, D], stack=st)
        pT = [pb(f"x_pT{q}", [P, 512], stack=st) for q in range(2)]
        pz = [pb(f"x_pz{q}", [P, FF], stack=st) for q in range(2)]
        pt = [pb(f"x_pt{q}", [P, FF], stack=st) for q in range(2)]
        py = [pb(f"x_py{q}", [P, 4, D], stack=st) for q in range(2)]
        w1, w2 = (mwp[:, n * E * KF:(n + 1) * E * KF].rearrange("p (e k) w d -> p e k w d", e=E) for n in range(2))
        loaded = [sem(f"x_loaded{q}", st) for q in range(U)]
        sent = [sem(f"x_sent{q}", st) for q in range(R)]
        names = ("x_turned xh_made xl_made z_made r_made r_turned hh_made hl_made y_summed yl_made y_made idx_made "
                 "b_loaded step none_made").split()
        (x_turned, xh_made, xl_made, z_made, r_made, r_turned, hh_made, hl_made, y_summed, yl_made, y_made, idx_made,
         b_loaded, step_, none_made) = (sem("x_" + n, st) for n in names)

        with nc.Block() as block:
            @block.sync
            def _(sp):
                for q in range(U):
                    sp.dma_start(xs[q][:], ms_dram[q * P:(q + 1) * P, :]).then_inc(loaded[q], 16)
                sp.dma_start(b1[:], a["m_b1"].to_broadcast([P, E * FF])).then_inc(b_loaded, 16)
                sp.dma_start(b2r[:], a["m_b2"].to_broadcast([2, E * D])).then_inc(b_loaded, 16)
                sp.dma_start(sgn[:], a["signs"]).then_inc(b_loaded, 16)

                def step(n, t, c):
                    if within(t + U, ET):
                        sp.wait_ge(x_turned, t + 1)
                        sp.wait_ge(y_made, t + 1)
                        sp.wait_ge(idx_made, t + 1)
                        sp.dma_start(xs[c][:], ms_dram[bass.ds((t + U) * P, P), :]).then_inc(loaded[c], 16)

                rolled(sp, step, ET, U, 0)

            @block.gpsimd
            def _(pool):
                pool.memset(none[:], 0).then_inc(none_made, 1)
                pool.wait_ge(none_made, 1)

                def step(n, t, c):
                    q = c % R
                    pool.wait_ge(y_made, t + 1)
                    pool.wait_ge(loaded[c], 16 * n + 16)
                    after(pool, sent[q], 16 * (U // R * n + c // R))
                    pool.tensor_tensor(idx[q][:], xs[c][:, D:D + 1].bitcast(I32), none[:], ALU.add).then_inc(idx_made, 1)
                    carry(pool, none_made)
                    pool.wait_ge(idx_made, t + 1)
                    pool.indirect_dma_start(y_dram, bass.IndirectOffsetOnAxis(ap=idx[q][:, 0:1], axis=0),
                                            y[:, q, :], None).then_inc(sent[q], 16)

                rolled(pool, step, ET, U, 0)
                for q in range(R):
                    pool.wait_ge(sent[q], 16 * (ET // R))

            @block.tensor
            def _(pe):
                held = {}

                def weights_of(t, place):
                    if place not in held:
                        held[place] = pe.value_load(expert_of_tile[0:1, bass.ds(t, 1)], min_val=0, max_val=E - 1)
                    return held[place]

                def turn(n, t, c):
                    q = c % 2
                    pe.wait_ge(loaded[c], 16 * n + 16)
                    nc.tensor.transpose(pT[q][:, 0:P], xs[c][:, 0:D], ident[:]).then_inc(x_turned, 1)

                def first(n, t, c):
                    q = c % 2
                    e = weights_of(t, c)
                    pe.wait_ge(xl_made, t + 1)
                    wh, wl = (w1[:, bass.ds(e, 1), :, n_, :].rearrange("p o k d -> p (o k) d") for n_ in range(2))
                    nc.tensor.matmul(pz[q][:], xh[:, q], wh, start=True, stop=False)
                    nc.tensor.matmul(pz[q][:], xh[:, q], wl, start=False, stop=False)
                    nc.tensor.matmul(pz[q][:], xl[:, q], wh, start=False, stop=True).then_inc(z_made, 1)

                def turn_hidden(n, t, c):
                    q = c % 2
                    pe.wait_ge(r_made, t + 1)
                    for k in range(KF):
                        last = nc.tensor.transpose(pt[q][:, k * P:(k + 1) * P], r[:, q, k * P:(k + 1) * P], ident[:])
                    last.then_inc(r_turned, 1)

                def second(n, t, c, place):
                    q = c % 2
                    e = weights_of(t, place)
                    pe.wait_ge(hl_made, t + 1)
                    after(pe, y_made, t - 1)
                    for k in range(KF):
                        w = w2[:, bass.ds(e, 1), k]
                        h = slice(k * P, (k + 1) * P)
                        nc.tensor.matmul(py[q][:, 0:2, :], hh[:, q, h], w.rearrange("p o w d -> p (o w) d"),
                                         start=(k == 0), stop=False)
                        nc.tensor.matmul(py[q][:, 0, :], hl[:, q, h], w[:, :, 0], start=False, stop=False)
                    nc.tensor.matmul(py[q][:, 0, :], onesr[:], b2[:, bass.ds(e * D, D)], start=False, stop=True)\
                        .then_inc(y_summed, 1)

                pe.wait_ge(step_, 5)
                turn(0, 0, 0)
                turn(0, 1, 1)

                def step(n, t, c):
                    if c == 0:
                        held.clear()
                    if within(t, ET):
                        first(n, t, c)
                    if within(t - 1, ET):
                        turn_hidden(*behind(n, t, c, 1, U))
                    if within(t + 2, ET):
                        turn(*behind(n, t, c, -2, U))
                    if within(t - 2, ET):
                        second(*behind(n, t, c, 2, U), c - 2)

                rolled(pe, step, ET, U, 2)

            @block.scalar
            def _(act):
                def high(n, t, c):
                    q = c % 2
                    act.wait_ge(x_turned, t + 1)
                    act.activation(xh[:, q], pT[q][:, 0:P], ACT.Copy).then_inc(xh_made, 1)

                def hidden_high(n, t, c):
                    q = c % 2
                    act.wait_ge(r_turned, t + 1)
                    act.activation(hh[:, q], pt[q][:], ACT.Relu).then_inc(hh_made, 1)

                def low_sums(n, t, c):
                    q = c % 2
                    act.wait_ge(y_summed, t + 1)
                    after(act, y_made, t - 1)
                    act.activation(yl[:, q], py[q][:, 1, :], ACT.Copy, scale=xs[c][:, D + 1:D + 2]).then_inc(yl_made, 1)

                high(0, 0, 0)
                high(0, 1, 1)

                def step(n, t, c):
                    if within(t - 1, ET):
                        hidden_high(*behind(n, t, c, 1, U))
                    if within(t + 2, ET):
                        high(*behind(n, t, c, -2, U))
                    if within(t - 2, ET):
                        low_sums(*behind(n, t, c, 2, U))

                rolled(act, step, ET, U, 2)

            @block.vector
            def _(dve):
                def link(ins, n):
                    ins.then_inc(step_, 1)
                    dve.wait_ge(step_, n)

                dve.wait_ge(b_loaded, 48)
                link(nc.vector.memset(onesf[:], 1.0), 1)
                nc.vector.tensor_copy(onesr[:], onesf[:])
                link(nc.vector.tensor_copy(b2h[:], b2r[:]), 2)
                link(nc.vector.tensor_scalar(b2m[:], b2r[:], sgn[:, 0:1], None, ALU.mult), 3)
                link(nc.vector.scalar_tensor_tensor(b2[:], b2h[:].bitcast(F32), sgn[:, 1:2], b2m[:], ALU.mult, ALU.add), 4)
                link(nc.vector.memset(onesf[:], 1.0), 5)

                def low(n, t, c):
                    q = c % 2
                    dve.wait_ge(xh_made, t + 1)
                    nc.vector.tensor_tensor(xl[:, q], pT[q][:, 0:P], xh[:, q].bitcast(F32), ALU.subtract)\
                        .then_inc(xl_made, 1)

                def hidden(n, t, c):
                    q = c % 2
                    e = dve.value_load(expert_of_tile[0:1, bass.ds(t, 1)], min_val=0, max_val=E - 1)
                    dve.wait_ge(z_made, t + 1)
                    nc.vector.tensor_tensor(r[:, q], pz[q][:], b1[:, bass.ds(e * FF, FF)], ALU.add).then_inc(r_made, 1)

                def hidden_low(n, t, c):
                    q = c % 2
                    dve.wait_ge(hh_made, t + 1)
                    nc.vector.scalar_tensor_tensor(hl[:, q], pt[q][:], 0.0, hh[:, q].bitcast(F32), ALU.max, ALU.subtract)\
                        .then_inc(hl_made, 1)

                def result(n, t, c):
                    q = c % 2
                    dve.wait_ge(yl_made, t + 1)
                    after(dve, sent[c % R], 16 * (U // R * n + c // R))
                    nc.vector.scalar_tensor_tensor(y[:, c % R], py[q][:, 0, :], xs[c][:, D + 1:D + 2], yl[:, q],
                                                   ALU.mult, ALU.add).then_inc(y_made, 1)

                low(0, 0, 0)
                low(0, 1, 1)

                def step(n, t, c):
                    if within(t, ET):
                        hidden(n, t, c)
                    if within(t - 1, ET):
                        hidden_low(*behind(n, t, c, 1, U))
                    if within(t + 2, ET):
                        low(*behind(n, t, c, -2, U))
                    if within(t - 2, ET):
                        result(*behind(n, t, c, 2, U))

                rolled(dve, step, ET, U, 2)


def combine(nc, sb, pb, sem, x1, y_dram, out):
    with ExitStack() as st:
        y = sb("f_y", [P, 2, 2, SB, D], stack=st)
        t = sb("f_t", [P, 2, SB, D], stack=st)
        o = sb("f_o", [P, 2, SB, D], stack=st)
        loaded = [sem(f"f_loaded{q}", st) for q in range(2)]
        stored = [sem(f"f_stored{q}", st) for q in range(2)]
        t_made = sem("f_t_made", st)
        o_made = sem("f_o_made", st)
        y_view = y_dram[0:2 * T, :].rearrange("(k b s) d -> b k s d", k=2, b=B)

        with nc.Block() as block:
            @block.sync
            def _(sp):
                for i in range(2):
                    for k in range(2):
                        sp.dma_start(y[:, i, k], y_view[:, k, i * SB:(i + 1) * SB, :]).then_inc(loaded[i], 16)
                with sp.Fori(1, NB // 2) as j:
                    for q in range(2):
                        sp.wait_ge(o_made, 2 * j + q - 1)
                        for k in range(2):
                            sp.dma_start(y[:, q, k], y_view[:, k, bass.ds((2 * j + q) * SB, SB), :]).then_inc(loaded[q], 16)

            @block.scalar
            def _(act):
                with act.Fori(0, NB // 2) as j:
                    for q in range(2):
                        act.wait_ge(o_made, 2 * j + q + 1)
                        act.dma_start(out[:, bass.ds((2 * j + q) * SB, SB), :], o[:, q]).then_inc(stored[q], 16)
                for q in range(2):
                    act.wait_ge(stored[q], 16 * (NB // 2))

            @block.vector
            def _(dve):
                with dve.Fori(0, NB // 2) as j:
                    for q in range(2):
                        dve.wait_ge(loaded[q], 32 * j + 32)
                        nc.vector.tensor_tensor(t[:, q], y[:, q, 0], y[:, q, 1], ALU.add).then_inc(t_made, 1)
                        dve.wait_ge(t_made, 2 * j + q + 1)
                        dve.wait_ge(stored[q], 16 * j)
                        nc.vector.tensor_tensor(o[:, q], t[:, q], x1[:, bass.ds((2 * j + q) * SB, SB), :], ALU.add)\
                            .then_inc(o_made, 1)


def constants():
    p = np.arange(P)
    f = np.float32
    parts = [np.eye(P, dtype=f), (p[:, None] < p[None, :]).astype(f), np.ones((P, P), f),
             ((p[:, None] // DK) % HG == np.arange(HG)[None, :]).astype(f), (p[:, None] % LO).astype(f),
             np.tile(np.arange(TYPES, dtype=f), (P, 1)), np.tile(np.arange(S, dtype=f), (P, 1)),
             np.tile(BT * np.arange(TT, dtype=f), (P, 1))]
    return np.ascontiguousarray(np.concatenate(parts, axis=1))


def route_constants():
    p = np.arange(P)
    f = np.float32
    parts = [np.tile(E - np.arange(E, dtype=f), (P, 1)), np.ones((P, E), f), np.tile(P * np.arange(ET, dtype=f), (P, 1)),
             (p[:, None] * S + np.arange(S)[None, :]).astype(f)]
    return np.ascontiguousarray(np.concatenate(parts, axis=1))


def arrays_of(inputs):
    g = {k: np.asarray(v) for k, v in inputs.items()}
    c = np.ascontiguousarray
    L0, C1, F1 = "L0_cond_", "L1_cond_", "L1_ffn_"
    return {
        "x": c(g["x"]),
        "langs": c(g["itok_B_0_8"].reshape(1, B)),
        "types": c(g["itok_B_0_2"].reshape(B, 1)),
        "consts": constants(),
        "W1": c(g[L0 + "W1"].transpose(1, 0, 2).reshape(D, LA)),
        "b1": c(g[L0 + "b1"].reshape(1, LA)),
        "W2": c(g[L0 + "W2"].reshape(LA, D)),
        "tab": c(np.stack([g[L0 + "gamma"], g[L0 + "beta"], g[L0 + "b2"]], axis=1)),
        "w_gate": c(g["L0_ffn_w_gate"].T),
        "w_up": c(g["L0_ffn_w_up"].T),
        "cw": c(np.concatenate(
            [g[C1 + "wi"].transpose(1, 0, 2).reshape(D, -1),
             g[C1 + "wo"].reshape(TYPES, KF, P, D).transpose(2, 0, 1, 3).reshape(P, -1),
             g[C1 + "swi"].transpose(1, 0, 2).reshape(D, -1),
             g[C1 + "swo"].reshape(NSH, KF, P, D).transpose(2, 0, 1, 3).reshape(P, -1)], axis=1).reshape(P, CB, D)),
        "mw": c(np.concatenate(
            [g[F1 + "W1"].transpose(1, 0, 2).reshape(D, -1),
             g[F1 + "W2"].reshape(E, KF, P, D).transpose(2, 0, 1, 3).reshape(P, -1)], axis=1).reshape(P, MB, D)),
        "m_b1": c(g[F1 + "b1"].reshape(1, -1)),
        "m_b2": c(g[F1 + "b2"].reshape(1, -1)),
        "signs": np.array([[0, 1], [1, -1]], np.float32),
        "quad": (np.arange(P)[:, None] // S == np.arange(BT)[None, :]).astype(np.float32),
        "rconsts": route_constants(),
        "pads": np.ascontiguousarray((2 * T + np.arange(ET * P, dtype=np.int32)).reshape(ET, P).T),
        "w_o": c(g[F1 + "w_o"]),
        "b_o": c(g[F1 + "b_o"].reshape(1, D)),
        "ln2": c(np.concatenate([g[F1 + "ln2_g"], g[F1 + "ln2_b"]]).reshape(1, 2 * D)),
        "gate_w": c(g[F1 + "gate_w"]),
        "gate_b": c(g[F1 + "gate_b"].reshape(1, E)),
        "g1": c(g[C1 + "g1"].reshape(3, D, D).transpose(1, 0, 2)),
        "g2": c(g[C1 + "g2"]),
        "w_qkv": c(g[F1 + "w_qkv"]),
        "b_qkv": c(g[F1 + "b_qkv"].reshape(1, 3 * D)),
        "ln1_g": c(g[F1 + "ln1_g"].reshape(D, 1)),
        "ln1_b": c(g[F1 + "ln1_b"].reshape(D, 1)),
        "w_down": c(g["L0_ffn_w_down"].T.reshape(KF, P, D).transpose(1, 0, 2).reshape(P, KF * D)),
    }


def kernel(**inputs):
    import concourse.bacc as bacc
    from concourse.bass_utils import run_bass_kernel_spmd

    nc = bacc.Bacc("TRN2", target_bir_lowering=False, num_devices=1)
    arrays = {f"in_{n}": v for n, v in arrays_of(inputs).items()}
    a = {n[3:]: nc.dram_tensor(n, v.shape, mybir.dt.from_np(v.dtype), kind="ExternalInput").ap()
         for n, v in arrays.items()}
    out = nc.dram_tensor("out_dram", (B, S, D), F32, kind="ExternalOutput").ap()
    adaln_ffn_moe_kernel(nc, a, out)
    r = run_bass_kernel_spmd(nc, [arrays], core_ids=[0])
    return r.results[0]["out_dram"]
```

```python
from contextlib import ExitStack

import numpy as np
import concourse.bass as bass
from concourse import mybir

F32 = mybir.dt.float32
F32R = mybir.dt.float32r
BF16 = mybir.dt.bfloat16
I32 = mybir.dt.int32
ALU = mybir.AluOpType
ACT = mybir.ActivationFunctionType
AX = mybir.AxisListType.X

P = 128
B, S, D = 128, 32, 128
T = B * S
LANG, AD = 10, 32
LA = LANG * AD
INNER = 512
TYPES, NSH = 5, 2
H, DK = 16, 8
E = 8
FF = 512
KF = FF // P
SB = 4
NB = S // SB
W = SB * D
BT = P // S
TT = (B + TYPES * (BT - 1)) // BT
TILE_UNROLL = 6
TT += -TT % TILE_UNROLL
ET = (2 * T + E * (P - 1)) // P
EXPERT_UNROLL = 12
ET += -ET % EXPERT_UNROLL
TAG_ROWS = E * T + E * P
TAG = 4
CB = (TYPES + NSH) * 2 * KF
B_WO = TYPES * KF
B_SWI = 2 * TYPES * KF
B_SWO = B_SWI + NSH * KF
MB = 2 * E * KF
CHB = 8
MAGIC = 1.5 * 2.0 ** 23
OFF = -1.0e30
EPS = 1e-5
HG = H // 4
LO = 32


def adaln_ffn_moe_kernel(nc, a, out):
    ctx = ExitStack()

    def sb(name, shape, dt=F32, stack=None):
        return (stack or ctx).enter_context(nc.sbuf_tensor(name, shape, dt))

    def pb(name, shape, dt=F32, stack=None):
        return (stack or ctx).enter_context(nc.psum_tensor(name, shape, dt))

    def sem(name, stack=None):
        if name in kept:
            return kept[name]
        handle = sems[-1].enter_context(nc.semaphore(name))
        numbers.append(handle.num)
        return handle

    def reuse_semaphores():
        nc.all_engine_barrier(sems_to_clear=range(min(numbers), max(numbers) + 1))
        sems.pop().close()
        sems.append(ctx.enter_context(ExitStack()))
        numbers.clear()

    with ctx:
        kept = {n: ctx.enter_context(nc.semaphore(n)) for n in ("b_sent", "c_eo_loaded")}
        sems, numbers = [ctx.enter_context(ExitStack())], []
        x1 = sb("x1", [P, S, D])
        ident = sb("ident", [P, P])
        tri = sb("tri", [P, P])
        ones = sb("ones", [P, P])
        hmask = sb("hmask", [P, HG])
        type_slot = sb("type_slot", [P, S], I32)
        type_of_tile = sb("type_of_tile", [1, TT], I32)
        xs_dram = nc.dram_tensor("xs_dram", (TT * P, D), F32, kind="Internal").ap()
        eo_dram = nc.dram_tensor("eo_dram", (TT * P, D), F32, kind="Internal").ap()
        qkv_dram = nc.dram_tensor("qkv_dram", (B, S, 3 * D), F32, kind="Internal").ap()
        att_dram = nc.dram_tensor("att_dram", (B, S, D), F32, kind="Internal").ap()

        cres = sb("cres", [P, S, D])
        with ExitStack() as cond:
            cwp = sb("cwp", [P, CB, 2, D], F32R, cond)
            with ExitStack() as layer0:
                nrm = sb("nrm", [P, S, D], stack=layer0)
                w1h = sb("w1h", [P, LA], F32R, layer0)
                w1l = sb("w1l", [P, LA], F32R, layer0)
                w2h = sb("w2h", [P, 3, D], F32R, layer0)
                w2l = sb("w2l", [P, 3, D], F32R, layer0)
                bias1 = sb("bias1", [2 * LO, LA], F32R, layer0)
                tab = sb("tab", [2 * LO, 3, D], F32R, layer0)
                lang1h = sb("lang1h", [2 * LO, B], F32R, layer0)
                gb = sb("gb", [P, 2, D], stack=layer0)
                amx = sb("amx", [P, S], stack=layer0)
                wgq = sb("wgq", [P, INNER], BF16, layer0)
                wuq = sb("wuq", [P, INNER], BF16, layer0)
                wdq = sb("wdq", [P, KF, D], BF16, layer0)
                wsc = sb("wsc", [P, 3], stack=layer0)

                KT = [(0, P), (P, P), (2 * P, LA - 2 * P)]
                xin = sb("xin", [P, 2, SB, D], stack=layer0)
                zero = sb("zero", [P, D], stack=layer0)
                x_loaded = [sem(f"x_loaded{q}") for q in range(2)]
                x1_loaded, rows_cleared = sem("x1_loaded"), sem("rows_cleared")
                setup(nc, a, sb, pb, sem, x1, ident, tri, ones, hmask, type_slot, type_of_tile, xs_dram,
                      w1h, w1l, w2h, w2l, bias1, tab, lang1h, gb, wgq, wuq, wdq, wsc, KT, xin, zero,
                      x_loaded, x1_loaded, rows_cleared)
                adapter(nc, a, sb, pb, sem, x1, ident, nrm, amx, w1h, w1l, w2h, w2l, bias1, tab, lang1h, gb, KT,
                        xin, x_loaded, x1_loaded)
                quantised_ffn(nc, a, sb, pb, sem, x1, ident, nrm, amx, wgq, wuq, wdq, wsc, type_slot, xs_dram, cwp,
                              rows_cleared)
            typed_experts(nc, sb, pb, sem, ident, type_of_tile, xs_dram, eo_dram, cwp)
            shared_experts(nc, a, sb, pb, sem, x1, ident, type_slot, eo_dram, qkv_dram, cwp, cres)
        reuse_semaphores()
        h_dram = nc.dram_tensor("h_dram", (B, S, D), F32, kind="Internal").ap()
        tags_dram = nc.dram_tensor("tags_dram", (TAG_ROWS, TAG), I32, kind="Internal").ap()
        y_dram = nc.dram_tensor("y_dram", (2 * T + TAG_ROWS, D), F32, kind="Internal").ap()
        mwp = sb("mwp", [P, MB, 2, D], F32R)
        attention(nc, a, sb, pb, sem, ident, hmask, qkv_dram, att_dram, mwp)
        biases = (sb("b1", [P, E * FF]), sb("b2", [2, E * D], F32R), sb("onesr", [2, P], F32R), sb("ln2", [P, 2]))
        expert_of_tile = sb("expert_of_tile", [1, ET], I32)
        row_of_tile = sb("row_of_tile", [1, ET], I32)
        second_norm(nc, a, sb, pb, sem, ident, ones, tri, x1, cres, att_dram, h_dram, tags_dram, expert_of_tile,
                    row_of_tile, biases)
        experts(nc, sb, pb, sem, ident, expert_of_tile, row_of_tile, h_dram, tags_dram, y_dram, mwp,
                biases)
        combine(nc, sb, sem, x1, y_dram, out)


def carry(eng, signal):
    eng.wait_ge(signal, 1)


def after(eng, signal, value):
    if not (isinstance(value, int) and value <= 0):
        eng.wait_ge(signal, value)


def rolled(eng, step, tiles, unroll, drain, tail=1, head=1):
    for t in range(head * unroll):
        step(t // unroll, t, t % unroll)
    rounds = tiles // unroll
    with eng.Fori(head, rounds - tail) as n:
        for c in range(unroll):
            step(n, unroll * n + c, c)
    for t in range(tiles - tail * unroll, tiles + drain):
        step(t // unroll, t, t % unroll)


def behind(n, t, c, lag, unroll):
    return n + (c - lag) // unroll, t - lag, (c - lag) % unroll


def within(t, tiles):
    return not isinstance(t, int) or 0 <= t < tiles


def setup(nc, a, sb, pb, sem, x1, ident, tri, ones, hmask, type_slot, type_of_tile, xs_dram,
          w1h, w1l, w2h, w2l, bias1, tab, lang1h, gb, wgq, wuq, wdq, wsc, KT, xin, zero,
          x_loaded, x1_loaded, rows_cleared):
    with ExitStack() as st:
        w1 = sb("s_w1", [P, LA], stack=st)
        w2 = sb("s_w2", [P, 3, D], stack=st)
        braw = sb("s_braw", [2 * LO, LA], stack=st)
        traw = sb("s_traw", [2 * LO, 3, D], stack=st)
        bhi = sb("s_bhi", [2 * LO, LA], F32R, st)
        thi = sb("s_thi", [2 * LO, 3, D], F32R, st)
        ids = sb("s_ids", [2 * LO, B], I32, st)
        idf = sb("s_idf", [2 * LO, B], stack=st)
        ty = sb("s_ty", [P, 1], I32, st)
        tyf = sb("s_tyf", [P, 1], stack=st)
        consts = sb("s_consts", [P, 3 * P + HG + 1 + TYPES + S + TT], stack=st)
        ffw = sb("s_ffw", [P, 3, INNER], stack=st)
        tot = sb("s_tot", [P, 3], stack=st)
        msc = sb("s_msc", [P, 3], stack=st)
        inv = sb("s_inv", [P, 3], stack=st)
        rnd = sb("s_rnd", [P, 3, INNER], stack=st)
        t1h = sb("s_t1h", [P, TYPES], stack=st)
        cnt = sb("s_cnt", [P, TYPES], stack=st)
        cnti = sb("s_cnti", [P, TYPES], I32, st)
        cnts = sb("s_cnts", [P, TYPES], I32, st)
        padf = sb("s_padf", [P, TYPES], stack=st)
        endt = sb("s_endt", [P, TYPES], stack=st)
        offs = sb("s_offs", [P, TYPES], stack=st)
        slot = sb("s_slot", [P, TYPES], stack=st)
        slotw = sb("s_slotw", [P, TYPES], stack=st)
        slot1 = sb("s_slot1", [P, 1], stack=st)
        row1 = sb("s_row1", [P, 1], stack=st)
        tslot = sb("s_tslot", [P, S], stack=st)
        past = sb("s_past", [1, TYPES - 1, TT], stack=st)
        totile = sb("s_totile", [1, TT], stack=st)
        ps = pb("s_ps", [P, 512], stack=st)
        ps2 = pb("s_ps2", [P, 512], stack=st)
        ps3 = pb("s_ps3", [P, 512], stack=st)
        ps4 = pb("s_ps4", [P, 512], stack=st)
        ld_ty = sem("ld_ty", st)
        ld_w, ld_t, ld_f, ld_c = (sem(n, st) for n in ("ld_w", "ld_t", "ld_f", "ld_c"))
        cleared, diag, sums, means, tabs, ranks, ty1h, step, gbd = (
            sem("s_" + n, st) for n in
            ("cleared", "diag", "sums", "means", "tabs", "ranks", "ty1h", "step", "gbd"))
        pool_step = sem("s_pool_step", st)
        C_I, C_T, C_1, C_H, C_M, C_P, C_S, C_J = np.cumsum([0, P, P, P, HG, 1, TYPES, S]).tolist()

        with nc.Block() as block:
            @block.sync
            def _(sp):
                sp.dma_start(consts[:], a["consts"]).then_inc(ld_c, 16)
                sp.dma_start(w1[:], a["W1"]).then_inc(ld_w, 16)
                for k, (o, n) in enumerate(KT):
                    sp.dma_start(w2[0:n, k, :], a["W2"][o:o + n, :]).then_inc(ld_w, 16)
                for n, name in enumerate(("w_gate", "w_up", "w_down")):
                    sp.dma_start(ffw[:, n, :], a[name]).then_inc(ld_f, 16)
                sp.wait_ge(cleared, 1)
                sp.dma_start(xs_dram.rearrange("(p j) d -> p j d", p=P), zero[:, None, :].to_broadcast([P, TT, D]))\
                    .then_inc(rows_cleared, 16)

            @block.scalar
            def _(act):
                act.dma_start(ty[:], a["types"]).then_inc(ld_ty, 16)
                act.dma_start(ids[:], a["langs"].to_broadcast([2 * LO, B])).then_inc(ld_t, 16)
                act.wait_ge(cleared, 2)
                for r in (0, LO):
                    act.dma_start(braw[r:r + LANG, :], a["b1"].to_broadcast([LANG, LA])).then_inc(ld_t, 16)
                    act.dma_start(traw[r:r + LANG, :, :], a["tab"]).then_inc(ld_t, 16)
                for q in range(2):
                    act.dma_start(xin[:, q], a["x"][:, q * SB:(q + 1) * SB, :]).then_inc(x_loaded[q], 16)
                for q in range(4):
                    act.dma_start(x1[:, q * 8:(q + 1) * 8, :], a["x"][:, q * 8:(q + 1) * 8, :]).then_inc(x1_loaded, 16)

            @block.gpsimd
            def _(pool):
                pool.memset(zero[:], 0.0).then_inc(cleared, 1)
                pool.memset(braw[:], 0.0)
                pool.memset(traw[:], 0.0).then_inc(cleared, 1)
                pool.wait_ge(ld_t, 16 * 5)
                for n, r in enumerate((0, LO)):
                    v = braw[r:r + LO, :].rearrange("p (l c) -> p l c", l=LANG)
                    pool.affine_select(out=v, in_=v, compare_op=ALU.is_equal, fill=OFF if n == 0 else 0.0, base=0,
                                       pattern=[[-1, LANG], [0, AD]], channel_multiplier=1).then_inc(diag, 1)
                    pool.wait_ge(diag, n + 1)
                pool.wait_ge(ld_w, 16 * 4)
                pool.tensor_copy(w1h[:], w1[:]).then_inc(pool_step, 1)
                pool.wait_ge(pool_step, 1)
                pool.tensor_tensor(w1l[:], w1[:], w1h[:].bitcast(F32), ALU.subtract).then_inc(pool_step, 1)
                pool.wait_ge(pool_step, 2)
                for k, (o, n) in enumerate(KT):
                    pool.tensor_copy(w2h[0:n, k, :], w2[0:n, k, :]).then_inc(pool_step, 1)
                    pool.wait_ge(pool_step, 2 * k + 3)
                    pool.tensor_tensor(w2l[0:n, k, :], w2[0:n, k, :], w2h[0:n, k, :].bitcast(F32), ALU.subtract)\
                        .then_inc(pool_step, 1)
                    pool.wait_ge(pool_step, 2 * k + 4)

            @block.vector
            def _(dve):
                done = [0]

                def link(ins):
                    done[0] += 1
                    ins.then_inc(step, 1)
                    dve.wait_ge(step, done[0])

                dve.wait_ge(ld_c, 16)
                nc.vector.tensor_copy(ident[:], consts[:, C_I:C_T])
                nc.vector.tensor_copy(tri[:], consts[:, C_T:C_1])
                nc.vector.tensor_copy(hmask[:], consts[:, C_H:C_M])
                link(nc.vector.tensor_copy(ones[:], consts[:, C_1:C_H]))
                dve.wait_ge(ld_ty, 16)
                link(nc.vector.tensor_copy(tyf[:], ty[:]))
                nc.vector.tensor_scalar(t1h[:], consts[:, C_P:C_S], tyf[:, 0:1], None, ALU.is_equal).then_inc(ty1h, 1)
                dve.wait_ge(ranks, 1)
                link(nc.vector.tensor_scalar(cnt[:], ps2[:, 0:TYPES], float(BT - 1), None, ALU.add))
                link(nc.vector.tensor_copy(cnti[:], cnt[:]))
                link(nc.vector.tensor_scalar(cnts[:], cnti[:], 2, 2, ALU.logical_shift_right, ALU.logical_shift_left))
                link(nc.vector.tensor_copy(padf[:], cnts[:]))
                link(nc.vector.tensor_copy(endt[:, 0:1], padf[:, 0:1]))
                for n in range(1, TYPES):
                    link(nc.vector.tensor_tensor(endt[:, n:n + 1], endt[:, n - 1:n], padf[:, n:n + 1], ALU.add))
                link(nc.vector.tensor_tensor(offs[:], endt[:], padf[:], ALU.subtract))
                link(nc.vector.tensor_tensor(slot[:], offs[:], ps3[:, 0:TYPES], ALU.add))
                link(nc.vector.tensor_tensor(slotw[:], slot[:], t1h[:], ALU.mult))
                link(nc.vector.tensor_reduce(slot1[:], slotw[:], AX, ALU.add))
                link(nc.vector.tensor_scalar(row1[:], slot1[:], float(S), None, ALU.mult))
                link(nc.vector.tensor_scalar(tslot[:], consts[:, C_S:C_J], row1[:, 0:1], None, ALU.add))
                nc.vector.tensor_copy(type_slot[:], tslot[:])
                lines = [1, TYPES - 1, TT]
                link(nc.vector.tensor_tensor(past[:], consts[0:1, None, C_J:C_J + TT].to_broadcast(lines),
                                             endt[0:1, 0:TYPES - 1, None].to_broadcast(lines), ALU.is_ge))
                link(nc.vector.tensor_reduce(totile[0:1, :], past[0:1, :, :].rearrange("p n j -> p j n"), AX, ALU.add))
                link(nc.vector.tensor_copy(type_of_tile[0:1, :], totile[0:1, :]))
                dve.wait_ge(ld_t, 16 * 5)
                link(nc.vector.tensor_copy(idf[:], ids[:]))
                nc.vector.tensor_scalar(lang1h[:], idf[:], consts[0:2 * LO, C_M:C_P], None, ALU.is_equal)
                nc.vector.tensor_copy(thi[:], traw[:])
                dve.wait_ge(diag, 2)
                link(nc.vector.tensor_copy(bhi[:], braw[:]))
                nc.vector.tensor_copy(tab[0:LO], thi[0:LO].bitcast(F32))
                nc.vector.tensor_copy(bias1[0:LO, :], bhi[0:LO, :].bitcast(F32))
                nc.vector.tensor_tensor(tab[LO:2 * LO], traw[LO:2 * LO], thi[LO:2 * LO].bitcast(F32), ALU.subtract)
                nc.vector.tensor_tensor(bias1[LO:2 * LO, :], braw[LO:2 * LO, :], bhi[LO:2 * LO, :].bitcast(F32),
                                        ALU.subtract).then_inc(tabs, 1)
                dve.wait_ge(ld_f, 16 * 3)
                nc.vector.tensor_reduce(tot[:], ffw[:], AX, ALU.add, apply_absolute_value=True).then_inc(sums, 1)
                dve.wait_ge(means, 1)
                link(nc.vector.tensor_scalar(msc[:], ps[:, 0:3], 1.0 / (D * INNER), 1e-5, ALU.mult, ALU.max))
                link(nc.vector.tensor_scalar(wsc[:], msc[:], 1.0 / 127.0, None, ALU.mult))
                link(nc.vector.reciprocal(inv[:], msc[:]))
                for n in range(3):
                    link(nc.vector.tensor_scalar(rnd[:, n, :], ffw[:, n, :], inv[:, n:n + 1], MAGIC, ALU.mult, ALU.add))
                link(nc.vector.tensor_scalar(rnd[:], rnd[:], MAGIC - 1.0, MAGIC + 1.0, ALU.max, ALU.min))
                for n, q in enumerate((wgq[:], wuq[:], wdq[:].rearrange("p k d -> p (k d)"))):
                    link(nc.vector.tensor_scalar(q, rnd[:, n, :], MAGIC, None, ALU.subtract))
                dve.wait_ge(gbd, 1)
                link(nc.vector.tensor_copy(gb[:], ps4[:, 0:2 * D].rearrange("p (n d) -> p n d", n=2)))

            @block.tensor
            def _(pe):
                pe.wait_ge(ty1h, 1)
                nc.tensor.matmul(ps2[:, 0:TYPES], ones[:], t1h[:], start=True, stop=True)
                nc.tensor.matmul(ps3[:, 0:TYPES], tri[:], t1h[:], start=True, stop=True).then_inc(ranks, 1)
                pe.wait_ge(tabs, 1)
                nc.tensor.matmul(ps4[:, 0:2 * D], lang1h[:], tab[:, 0:2, :], start=True, stop=True).then_inc(gbd, 1)
                pe.wait_ge(sums, 1)
                nc.tensor.matmul(ps[:, 0:3], ones[:], tot[:], start=True, stop=True).then_inc(means, 1)


def adapter(nc, a, sb, pb, sem, x1, ident, nrm, amx, w1h, w1l, w2h, w2l, bias1, tab, lang1h, gb, KT,
            xin, x_loaded, x1_loaded):
    with ExitStack() as st:
        xh = sb("a_xh", [P, W], F32R, st)
        xl = sb("a_xl", [P, W], F32R, st)
        hh = sb("a_hh", [P, 2, 3, W], F32R, st)
        hl = sb("a_hl", [P, 2, 3, W], F32R, st)
        aT = sb("a_aT", [P, W], stack=st)
        y = sb("a_y", [P, SB, D], stack=st)
        bs = sb("a_bs", [P, SB, 6], stack=st)
        mv = sb("a_mv", [P, SB, 2], stack=st)
        ve = sb("a_ve", [P, SB], stack=st)
        rs = sb("a_rs", [P, SB], stack=st)
        half = sb("a_half", [P, SB], stack=st)
        nm = sb("a_nm", [P, SB, D], stack=st)
        ng = sb("a_ng", [P, SB, D], stack=st)
        pT = pb("a_pT", [P, W], stack=st)
        pz = [pb(f"a_pz{k}", [P, W], stack=st) for k in range(3)]
        pa = pb("a_pa", [P, W], stack=st)
        pt = pb("a_pt", [P, SB, D], stack=st)
        x_turned, xh_made, xl_made, z_made, hh_made, hl_made, a_made, aT_made, a_turned, y_made, stats, mv_made, \
            ve_made, rs_made, nm_made, ng_made, out_made, halfed = (sem("a_" + n, st) for n in (
                "x_turned", "xh_made", "xl_made", "z_made", "hh_made", "hl_made", "a_made", "aT_made", "a_turned",
                "y_made", "stats", "mv_made", "ve_made", "rs_made", "nm_made", "ng_made", "out_made", "halfed"))
        NK = len(KT)

        with nc.Block() as block:
            @block.tensor
            def _(pe):
                def turn(n, i, c):
                    pe.wait_ge(x_loaded[c], 16 * n + 16)
                    for u in range(SB):
                        last = nc.tensor.transpose(pT[:, u * D:(u + 1) * D], xin[:, c, u, :], ident[:])
                    last.then_inc(x_turned, 1)

                def first(n, i, c):
                    pe.wait_ge(xl_made, i + 1)
                    for k, (o, m) in enumerate(KT):
                        after(pe, hl_made, NK * (i - 1) + k + 1)
                        nc.tensor.matmul(pz[k][0:m, :], w1h[:, o:o + m], xh[:], start=True, stop=False)
                        nc.tensor.matmul(pz[k][0:m, :], w1h[:, o:o + m], xl[:], start=False, stop=False)
                        nc.tensor.matmul(pz[k][0:m, :], w1l[:, o:o + m], xh[:], start=False, stop=False)
                        nc.tensor.matmul(pz[k][0:m, :], bias1[:, o:o + m],
                                         lang1h[:, None, :].to_broadcast([2 * LO, SB, B]),
                                         start=False, stop=True).then_inc(z_made, 1)

                def second(n, i, c):
                    pe.wait_ge(hl_made, NK * i + NK)
                    after(pe, aT_made, i)
                    nc.tensor.matmul(pa[:], tab[:, 2, :], lang1h[:, None, :].to_broadcast([2 * LO, SB, B]),
                                     start=True, stop=False)
                    for k, (o, m) in enumerate(KT):
                        nc.tensor.matmul(pa[:], w2h[0:m, k, :], hh[0:m, c, k, :], start=False, stop=False)
                        nc.tensor.matmul(pa[:], w2h[0:m, k, :], hl[0:m, c, k, :], start=False, stop=False)
                        last = nc.tensor.matmul(pa[:], w2l[0:m, k, :], hh[0:m, c, k, :], start=False, stop=(k == NK - 1))
                    last.then_inc(a_made, 1)

                def turn_back(n, i, c):
                    pe.wait_ge(aT_made, i + 1)
                    after(pe, y_made, i)
                    for u in range(SB):
                        last = nc.tensor.transpose(pt[:, u, :], aT[:, u * D:(u + 1) * D], ident[:])
                    last.then_inc(a_turned, 1)

                turn(0, 0, 0)

                def step(n, i, c):
                    if within(i, NB):
                        first(n, i, c)
                    if within(i - 2, NB):
                        turn_back(*behind(n, i, c, 2, 2))
                    if within(i + 1, NB):
                        turn(*behind(n, i, c, -1, 2))
                    if within(i - 1, NB):
                        second(*behind(n, i, c, 1, 2))

                rolled(pe, step, NB, 2, 2, head=2)

            @block.sync
            def _(sp):
                def step(n, i, c):
                    if within(i + 2, NB):
                        sp.wait_ge(x_turned, i + 1)
                        sp.dma_start(xin[:, c], a["x"][:, bass.ds((i + 2) * SB, SB), :]).then_inc(x_loaded[c], 16)

                rolled(sp, step, NB, 2, 0)

            @block.scalar
            def _(act):
                def high(n, i, c):
                    act.wait_ge(x_turned, i + 1)
                    nc.scalar.activation(xh[:], pT[:], ACT.Copy).then_inc(xh_made, 1)

                def hidden(n, i, c):
                    for k, (o, m) in enumerate(KT):
                        act.wait_ge(z_made, NK * i + k + 1)
                        if k == 0:
                            after(act, a_made, i - 1)
                        nc.scalar.activation(hh[0:m, c, k, :], pz[k][0:m, :], ACT.Relu).then_inc(hh_made, 1)

                def sums(n, i, c):
                    act.wait_ge(a_made, i + 1)
                    after(act, a_turned, i)
                    nc.scalar.activation(aT[:], pa[:], ACT.Copy).then_inc(aT_made, 1)

                high(0, 0, 0)

                def step(n, i, c):
                    if within(i, NB):
                        hidden(n, i, c)
                    if within(i + 1, NB):
                        high(*behind(n, i, c, -1, 2))
                    if within(i - 1, NB):
                        sums(*behind(n, i, c, 1, 2))

                rolled(act, step, NB, 2, 1)

            @block.gpsimd
            def _(pool):
                pool.memset(half[:], -0.5).then_inc(halfed, 1)
                pool.wait_ge(halfed, 1)

                def scale(n, i, c):
                    pool.wait_ge(ve_made, i + 1)
                    pool.tensor_tensor(rs[:], ve[:], half[:], ALU.pow).then_inc(rs_made, 1)
                    pool.wait_ge(nm_made, i + 1)
                    pool.tensor_tensor(ng[:], nm[:], gb[:, 0:1, :].to_broadcast([P, SB, D]), ALU.mult).then_inc(ng_made, 1)
                    pool.wait_ge(ng_made, i + 1)
                    pool.tensor_tensor(nrm[:, bass.ds(i * SB, SB), :], ng[:], gb[:, 1:2, :].to_broadcast([P, SB, D]),
                                       ALU.add).then_inc(out_made, 1)

                rolled(pool, scale, NB, 2, 0)

            @block.vector
            def _(dve):
                def low(n, i, c):
                    dve.wait_ge(xh_made, i + 1)
                    nc.vector.tensor_tensor(xl[:], pT[:], xh[:].bitcast(F32), ALU.subtract).then_inc(xl_made, 1)

                def hidden(n, i, c):
                    for k, (o, m) in enumerate(KT):
                        dve.wait_ge(hh_made, NK * i + k + 1)
                        nc.vector.scalar_tensor_tensor(hl[0:m, c, k, :], pz[k][0:m, :], 0.0,
                                                       hh[0:m, c, k, :].bitcast(F32), ALU.max, ALU.subtract)\
                            .then_inc(hl_made, 1)

                def residual(n, i, c):
                    dve.wait_ge(a_turned, i + 1)
                    after(dve, nm_made, i)
                    nc.vector.tensor_tensor(y[:], pt[:], x1[:, bass.ds(i * SB, SB), :], ALU.add).then_inc(y_made, 1)

                def statistics(n, i, c):
                    carry(dve, x_turned)
                    dve.wait_ge(y_made, i + 1)
                    for u in range(SB):
                        last = nc.vector.bn_stats(bs[:, u, :], y[:, u, :])
                    last.then_inc(stats, 1)
                    carry(dve, x_turned)
                    dve.wait_ge(stats, i + 1)
                    for u in range(SB):
                        last = nc.vector.bn_aggr(mv[:, u, :], bs[:, u, :])
                    last.then_inc(mv_made, 1)
                    dve.wait_ge(mv_made, i + 1)
                    nc.vector.tensor_scalar(ve[:], mv[:, :, 1], EPS, None, ALU.add).then_inc(ve_made, 1)

                def normalise(n, i, c):
                    dve.wait_ge(rs_made, i + 1)
                    after(dve, ng_made, i)
                    for u in range(SB):
                        last = nc.vector.tensor_scalar(nm[:, u, :], y[:, u, :], mv[:, u, 0:1],
                                                       rs[:, u:u + 1], ALU.subtract, ALU.mult)
                    last.then_inc(nm_made, 1)

                def largest(i):
                    dve.wait_ge(out_made, i + 1)
                    nc.vector.tensor_reduce(amx[:, bass.ds(i * SB, SB)], nrm[:, bass.ds(i * SB, SB), :], AX, ALU.max,
                                            apply_absolute_value=True)

                low(0, 0, 0)
                dve.wait_ge(x1_loaded, 16 * 4)

                def step(n, i, c):
                    if within(i, NB):
                        hidden(n, i, c)
                    if within(i + 1, NB):
                        low(*behind(n, i, c, -1, 2))
                    if within(i - 2, NB):
                        residual(*behind(n, i, c, 2, 2))
                        statistics(*behind(n, i, c, 2, 2))
                    if within(i - 3, NB):
                        largest(i - 3)
                    if within(i - 2, NB):
                        normalise(*behind(n, i, c, 2, 2))

                rolled(dve, step, NB, 2, 3, head=2)


def quantised_ffn(nc, a, sb, pb, sem, x1, ident, nrm, amx, wgq, wuq, wdq, wsc, type_slot, xs_dram, cwp,
                  rows_cleared):
    with ExitStack() as st:
        sc = sb("b_sc", [P, S], stack=st)
        qs = sb("b_qs", [P, S], stack=st)
        sg = sb("b_sg", [P, S], stack=st)
        su = sb("b_su", [P, S], stack=st)
        xq = sb("b_xq", [P, SB, D], stack=st)
        xqT = sb("b_xqT", [P, 2, W], BF16, st)
        g = sb("b_g", [P, 2, INNER], stack=st)
        m = sb("b_m", [P, 2, 2, INNER], stack=st)
        mq = sb("b_mq", [P, 2, INNER], stack=st)
        mqT = sb("b_mqT", [P, 2, INNER], BF16, st)
        magic = sb("b_magic", [P, 1], stack=st)
        raw = sb("b_raw", [P, 2, CHB, D], stack=st)
        raw_loaded = [sem(f"b_raw_loaded{q}", st) for q in range(2)]
        parted = sem("b_parted", st)
        am2 = sb("b_am2", [P, 2], stack=st)
        sc2 = sb("b_sc2", [P, 2], stack=st)
        qs2 = sb("b_qs2", [P, 2, 2], stack=st)
        sd = sb("b_sd", [P, 2, 2], stack=st)
        pT = pb("b_pT", [P, SB, D], stack=st)
        pg = pb("b_pg", [P, 2, INNER], stack=st)
        pu = pb("b_pu", [P, 2, INNER], stack=st)
        pm = [pb(f"b_pm{u}", [P, INNER], stack=st) for u in range(2)]
        po = pb("b_po", [P, 2, D], stack=st)
        xq_made, xq_turned, xqT_made, g_prod, u_prod, g_made, m_made, am_made, qs_made, mq_made, mqc_made, m_turned, \
            mqT_made, o_made, x1_made, step, sent = (sem("b_" + n, st) for n in (
                "xq_made", "xq_turned", "xqT_made", "g_prod", "u_prod", "g_made", "m_made", "am_made", "qs_made",
                "mq_made", "mqc_made", "m_turned", "mqT_made", "o_made", "x1_made", "step", "sent"))
        xq_raw = sem("b_xq_raw", st)
        NP2 = S // 2

        with nc.Block() as block:
            @block.tensor
            def _(pe):
                def turn(i):
                    pe.wait_ge(xq_made, i + 1)
                    after(pe, xqT_made, i)
                    for u in range(SB):
                        last = nc.tensor.transpose(pT[:, u, :], xq[:, u, :], ident[:])
                    last.then_inc(xq_turned, 1)

                def up(p, b2, h):
                    for n in range(2):
                        c = slice((2 * h + n) * D, (2 * h + n + 1) * D)
                        after(pe, g_made, 2 * p + n - 1)
                        nc.tensor.matmul(pg[:, n, :], xqT[:, b2, c], wgq[:], start=True, stop=True).then_inc(g_prod, 1)
                        after(pe, m_made, 2 * p + n - 1)
                        nc.tensor.matmul(pu[:, n, :], xqT[:, b2, c], wuq[:], start=True, stop=True).then_inc(u_prod, 1)

                def down(p):
                    for n in range(2):
                        pe.wait_ge(mqc_made, p + 1)
                        after(pe, mqT_made, 2 * p + n - 1)
                        for k in range(KF):
                            last = nc.tensor.transpose(pm[n][:, k * P:(k + 1) * P], mq[:, n, k * P:(k + 1) * P], ident[:])
                        last.then_inc(m_turned, 1)
                    after(pe, x1_made, p)
                    for n in range(2):
                        pe.wait_ge(mqT_made, 2 * p + n + 1)
                        for k in range(KF):
                            last = nc.tensor.matmul(po[:, n, :], mqT[:, n, k * P:(k + 1) * P], wdq[:, k, :],
                                                    start=(k == 0), stop=(k == KF - 1))
                    last.then_inc(o_made, 1)

                turn(0)
                pe.wait_ge(xqT_made, 1)
                up(0, 0, 0)

                def body(i):
                    up(2 * i + 1, i % 2, 1)
                    turn(i + 1)
                    down(2 * i)
                    pe.wait_ge(xqT_made, i + 2)
                    up(2 * i + 2, (i + 1) % 2, 0)
                    down(2 * i + 1)

                body(0)
                with pe.Fori(1, NB - 1) as i:
                    body(i)
                up(NP2 - 1, (NB - 1) % 2, 1)
                down(NP2 - 2)
                down(NP2 - 1)

            @block.scalar
            def _(act):
                def turned(i):
                    act.wait_ge(xq_turned, i + 1)
                    act.activation(xqT[:, i % 2, :], pT[:].rearrange("p u d -> p (u d)"), ACT.Copy, bias=-MAGIC)\
                       .then_inc(xqT_made, 1)

                def gate(p, b2, h):
                    for n in range(2):
                        act.wait_ge(g_prod, 2 * p + n + 1)
                        after(act, m_made, 2 * p + n - 1)
                        act.activation(g[:, n, :], pg[:, n, :], ACT.Silu, scale=sg[:, bass.ds(2 * p + n, 1)])\
                           .then_inc(g_made, 1)

                def quantise(p):
                    act.wait_ge(qs_made, p + 1)
                    after(act, m_turned, 2 * p)
                    for n in range(2):
                        act.activation(mq[:, n, :], m[:, p % 2, n, :], ACT.Identity, bias=magic[:],
                                       scale=qs2[:, p % 2, n:n + 1]).then_inc(mq_made, 1)

                def turned_back(p):
                    for n in range(2):
                        act.wait_ge(m_turned, 2 * p + n + 1)
                        if n == 0:
                            after(act, o_made, p)
                        act.activation(mqT[:, n, :], pm[n][:], ACT.Copy, bias=-MAGIC).then_inc(mqT_made, 1)

                turned(0)
                gate(0, 0, 0)

                def body(i):
                    quantise(2 * i)
                    gate(2 * i + 1, i % 2, 1)
                    turned(i + 1)
                    turned_back(2 * i)
                    quantise(2 * i + 1)
                    gate(2 * i + 2, (i + 1) % 2, 0)
                    turned_back(2 * i + 1)

                body(0)
                with act.Fori(1, NB - 1) as i:
                    body(i)
                quantise(NP2 - 2)
                gate(NP2 - 1, (NB - 1) % 2, 1)
                turned_back(NP2 - 2)
                quantise(NP2 - 1)
                turned_back(NP2 - 1)

            @block.vector
            def _(dve):
                def link(ins, n):
                    ins.then_inc(step, 1)
                    dve.wait_ge(step, n)

                nc.vector.memset(magic[:], MAGIC).then_inc(step, 1)
                link(nc.vector.tensor_scalar(sc[:], amx[:], 1e-5, 1.0 / 127.0, ALU.max, ALU.mult), 2)
                link(nc.vector.reciprocal(qs[:], sc[:]), 3)
                nc.vector.tensor_scalar(sg[:], sc[:], wsc[:, 0:1], 127.0, ALU.mult, ALU.mult)
                link(nc.vector.tensor_scalar(su[:], sc[:], wsc[:, 1:2], 127.0, ALU.mult, ALU.mult), 4)

                def rows(i):
                    after(dve, xq_turned, i)
                    for u in range(SB):
                        last = nc.vector.tensor_scalar(xq[:, u, :], nrm[:, i * SB + u, :],
                                                       qs[:, bass.ds(i * SB + u, 1)], MAGIC, ALU.mult, ALU.add)
                    last.then_inc(xq_raw, 1)
                    dve.wait_ge(xq_raw, i + 1)
                    nc.vector.tensor_scalar(xq[:], xq[:], MAGIC - 128.0, MAGIC + 127.0,
                                            ALU.max, ALU.min).then_inc(xq_made, 1)

                def inner(p):
                    for n in range(2):
                        dve.wait_ge(g_made, 2 * p + n + 1)
                        dve.wait_ge(u_prod, 2 * p + n + 1)
                        nc.vector.scalar_tensor_tensor(m[:, p % 2, n, :], pu[:, n, :], su[:, bass.ds(2 * p + n, 1)],
                                                       g[:, n, :], ALU.mult, ALU.mult).then_inc(m_made, 1)
                    dve.wait_ge(m_made, 2 * p + 2)
                    nc.vector.tensor_reduce(am2[:], m[:, p % 2], AX, ALU.max, apply_absolute_value=True).then_inc(am_made, 1)
                    dve.wait_ge(am_made, 3 * p + 1)
                    nc.vector.tensor_scalar(sc2[:], am2[:], 1e-5, 1.0 / 127.0, ALU.max, ALU.mult).then_inc(am_made, 1)
                    dve.wait_ge(am_made, 3 * p + 2)
                    nc.vector.reciprocal(qs2[:, p % 2, :], sc2[:]).then_inc(qs_made, 1)
                    nc.vector.tensor_scalar(sd[:, p % 2, :], sc2[:], wsc[:, 2:3], 127.0, ALU.mult, ALU.mult)\
                        .then_inc(am_made, 1)

                def clamp(p):
                    dve.wait_ge(mq_made, 2 * p + 2)
                    nc.vector.tensor_scalar(mq[:], mq[:], MAGIC - 128.0, MAGIC + 127.0, ALU.max, ALU.min)\
                        .then_inc(mqc_made, 1)

                def residual(p):
                    dve.wait_ge(o_made, p + 1)
                    dve.wait_ge(am_made, 3 * p + 3)
                    for n in range(2):
                        v = x1[:, 2 * p + n, :]
                        last = nc.vector.scalar_tensor_tensor(v, po[:, n, :], sd[:, p % 2, n:n + 1], v, ALU.mult, ALU.add)
                    last.then_inc(x1_made, 1)

                rows(0)
                inner(0)

                def body(i):
                    rows(i + 1)
                    clamp(2 * i)
                    inner(2 * i + 1)
                    residual(2 * i)
                    clamp(2 * i + 1)
                    inner(2 * i + 2)
                    residual(2 * i + 1)

                body(0)
                with dve.Fori(1, NB - 1) as i:
                    body(i)
                clamp(NP2 - 2)
                inner(NP2 - 1)
                residual(NP2 - 2)
                clamp(NP2 - 1)
                residual(NP2 - 1)

            @block.sync
            def _(sp):
                for n in range(CB // CHB):
                    if n >= 2:
                        sp.wait_ge(parted, 2 * n - 2)
                    sp.dma_start(raw[:, n % 2, :], a["cw"][:, n * CHB:(n + 1) * CHB, :]).then_inc(raw_loaded[n % 2], 16)

            @block.gpsimd
            def _(pool):
                def part(n):
                    c = slice(n * CHB, (n + 1) * CHB)
                    pool.wait_ge(raw_loaded[n % 2], 16 * (n // 2 + 1))
                    pool.tensor_copy(cwp[:, c, 0], raw[:, n % 2]).then_inc(parted, 1)
                    pool.wait_ge(parted, 2 * n + 1)
                    pool.tensor_tensor(cwp[:, c, 1], raw[:, n % 2], cwp[:, c, 0].bitcast(F32), ALU.subtract)\
                        .then_inc(parted, 1)
                    pool.wait_ge(parted, 2 * n + 2)

                pool.wait_ge(rows_cleared, 16)
                for s in range(S):
                    if s % 4 == 0 and s // 4 < CB // CHB:
                        part(s // 4)
                    pool.wait_ge(x1_made, s // 2 + 1)
                    pool.indirect_dma_start(xs_dram, bass.IndirectOffsetOnAxis(ap=type_slot[:, s:s + 1], axis=0),
                                            x1[:, s, :], None).then_inc(sent, 16)
                pool.wait_ge(sent, 16 * S)


def typed_experts(nc, sb, pb, sem, ident, type_of_tile, xs_dram, eo_dram, cwp):
    U, R = TILE_UNROLL, 3
    with ExitStack() as st:
        xs = sb("e_xs", [P, U, D], stack=st)
        xh = sb("e_xh", [P, 2, P], F32R, st)
        xl = sb("e_xl", [P, 2, P], F32R, st)
        r = sb("e_r", [P, 2, FF], stack=st)
        hh = sb("e_hh", [P, 2, FF], F32R, st)
        hl = sb("e_hl", [P, 2, FF], F32R, st)
        yl = sb("e_yl", [P, 2, D], stack=st)
        y = sb("e_y", [P, R, D], stack=st)
        pT = [pb(f"e_pT{q}", [P, 512], stack=st) for q in range(2)]
        pz = [pb(f"e_pz{q}", [P, FF], stack=st) for q in range(2)]
        pt = [pb(f"e_pt{q}", [P, FF], stack=st) for q in range(2)]
        py = [pb(f"e_py{q}", [P, 4, D], stack=st) for q in range(2)]
        w1, w2 = (cwp[:, n * B_WO:(n + 1) * B_WO].rearrange("p (e k) w d -> p e k w d", e=TYPES) for n in range(2))
        loaded = [sem(f"e_loaded{q}", st) for q in range(U)]
        stored = [sem(f"e_stored{q}", st) for q in range(R)]
        x_turned, xh_made, xl_made, z_made, r_made, r_turned, hh_made, hl_made, y_summed, yl_made, y_made = (
            sem("e_" + n, st) for n in ("x_turned", "xh_made", "xl_made", "z_made", "r_made", "r_turned", "hh_made",
                                        "hl_made", "y_summed", "yl_made", "y_made"))

        with nc.Block() as block:
            @block.sync
            def _(sp):
                for q in range(U):
                    sp.dma_start(xs[:, q], xs_dram[q * P:(q + 1) * P, :]).then_inc(loaded[q], 16)

                def step(n, t, c):
                    if within(t + U, TT):
                        sp.wait_ge(x_turned, t + 1)
                        sp.dma_start(xs[:, c], xs_dram[bass.ds((t + U) * P, P), :]).then_inc(loaded[c], 16)
                    if within(t - 3, TT):
                        sp.wait_ge(y_made, t - 2)
                        sp.dma_start(eo_dram[bass.ds((t - 3) * P, P), :], y[:, (c - 3) % R]).then_inc(stored[(c - 3) % R], 16)

                rolled(sp, step, TT, U, 3)
                for q in range(R):
                    sp.wait_ge(stored[q], 16 * (TT // R))

            @block.tensor
            def _(pe):
                held = {}

                def weights_of(t, place):
                    if place not in held:
                        held[place] = pe.value_load(type_of_tile[0:1, bass.ds(t, 1)], min_val=0, max_val=TYPES - 1)
                    return held[place]

                def turn(n, t, c):
                    q = c % 2
                    pe.wait_ge(loaded[c], 16 * n + 16)
                    nc.tensor.transpose(pT[q][:, 0:P], xs[:, c], ident[:]).then_inc(x_turned, 1)

                def first(n, t, c):
                    q = c % 2
                    e = weights_of(t, c)
                    pe.wait_ge(xl_made, t + 1)
                    wh, wl = (w1[:, bass.ds(e, 1), :, n_, :].rearrange("p o k d -> p (o k) d") for n_ in range(2))
                    nc.tensor.matmul(pz[q][:], xh[:, q], wh, start=True, stop=False)
                    nc.tensor.matmul(pz[q][:], xh[:, q], wl, start=False, stop=False)
                    nc.tensor.matmul(pz[q][:], xl[:, q], wh, start=False, stop=True).then_inc(z_made, 1)

                def turn_hidden(n, t, c):
                    q = c % 2
                    pe.wait_ge(r_made, t + 1)
                    for k in range(KF):
                        last = nc.tensor.transpose(pt[q][:, k * P:(k + 1) * P], r[:, q, k * P:(k + 1) * P], ident[:])
                    last.then_inc(r_turned, 1)

                def second(n, t, c, place):
                    q = c % 2
                    e = weights_of(t, place)
                    pe.wait_ge(hl_made, t + 1)
                    after(pe, y_made, t - 1)
                    for k in range(KF):
                        w = w2[:, bass.ds(e, 1), k]
                        h = slice(k * P, (k + 1) * P)
                        nc.tensor.matmul(py[q][:, 0:2, :], hh[:, q, h], w.rearrange("p o w d -> p (o w) d"),
                                         start=(k == 0), stop=False)
                        last = nc.tensor.matmul(py[q][:, 0, :], hl[:, q, h], w[:, :, 0], start=False,
                                                stop=(k == KF - 1))
                    last.then_inc(y_summed, 1)

                turn(0, 0, 0)
                turn(0, 1, 1)

                def step(n, t, c):
                    if c == 0:
                        held.clear()
                    if within(t, TT):
                        first(n, t, c)
                    if within(t - 1, TT):
                        turn_hidden(*behind(n, t, c, 1, U))
                    if within(t + 2, TT):
                        turn(*behind(n, t, c, -2, U))
                    if within(t - 2, TT):
                        second(*behind(n, t, c, 2, U), c - 2)

                rolled(pe, step, TT, U, 2)

            @block.scalar
            def _(act):
                def high(n, t, c):
                    q = c % 2
                    act.wait_ge(x_turned, t + 1)
                    act.activation(xh[:, q], pT[q][:, 0:P], ACT.Copy).then_inc(xh_made, 1)

                def hidden(n, t, c):
                    q = c % 2
                    act.wait_ge(z_made, t + 1)
                    act.activation(r[:, q], pz[q][:], ACT.Relu).then_inc(r_made, 1)

                def hidden_high(n, t, c):
                    q = c % 2
                    act.wait_ge(r_turned, t + 1)
                    act.activation(hh[:, q], pt[q][:], ACT.Copy).then_inc(hh_made, 1)

                def low_sums(n, t, c):
                    q = c % 2
                    act.wait_ge(y_summed, t + 1)
                    after(act, y_made, t - 1)
                    act.activation(yl[:, q], py[q][:, 1, :], ACT.Copy).then_inc(yl_made, 1)

                high(0, 0, 0)
                high(0, 1, 1)

                def step(n, t, c):
                    if within(t, TT):
                        hidden(n, t, c)
                    if within(t - 1, TT):
                        hidden_high(*behind(n, t, c, 1, U))
                    if within(t + 2, TT):
                        high(*behind(n, t, c, -2, U))
                    if within(t - 2, TT):
                        low_sums(*behind(n, t, c, 2, U))

                rolled(act, step, TT, U, 2)

            @block.vector
            def _(dve):
                def low(n, t, c):
                    q = c % 2
                    dve.wait_ge(xh_made, t + 1)
                    nc.vector.tensor_tensor(xl[:, q], pT[q][:, 0:P], xh[:, q].bitcast(F32), ALU.subtract)\
                        .then_inc(xl_made, 1)

                def hidden_low(n, t, c):
                    q = c % 2
                    dve.wait_ge(hh_made, t + 1)
                    nc.vector.tensor_tensor(hl[:, q], pt[q][:], hh[:, q].bitcast(F32), ALU.subtract).then_inc(hl_made, 1)

                def result(n, t, c):
                    q = c % 2
                    dve.wait_ge(yl_made, t + 1)
                    after(dve, stored[c % R], 16 * (U // R * n + c // R))
                    nc.vector.tensor_tensor(y[:, c % R], py[q][:, 0, :], yl[:, q], ALU.add).then_inc(y_made, 1)

                low(0, 0, 0)
                low(0, 1, 1)

                def step(n, t, c):
                    if within(t - 1, TT):
                        hidden_low(*behind(n, t, c, 1, U))
                    if within(t + 2, TT):
                        low(*behind(n, t, c, -2, U))
                    if within(t - 2, TT):
                        result(*behind(n, t, c, 2, U))

                rolled(dve, step, TT, U, 2)


def shared_experts(nc, a, sb, pb, sem, x1, ident, type_slot, eo_dram, qkv_dram, cwp, cres):
    with ExitStack() as st:
        wraw = sb("c_wraw", [P, 3 * D], stack=st)
        wgm = sb("c_wgm", [P, 3 * D], stack=st)
        wh = sb("c_wh", [P, 3 * D], F32R, st)
        wl = sb("c_wl", [P, 3 * D], F32R, st)
        lng = sb("c_lng", [P, 1], stack=st)
        lnb = sb("c_lnb", [P, 1], stack=st)
        braw = sb("c_braw", [2, 3 * D], stack=st)
        bsum = sb("c_bsum", [2, 3 * D], stack=st)
        bhi = sb("c_bhi", [2, 3 * D], F32R, st)
        bmul = sb("c_bmul", [2, 3 * D], stack=st)
        bias = sb("c_bias", [2, 3 * D], F32R, st)
        lnb2 = sb("c_lnb2", [P, 2], stack=st)
        sgn = sb("c_sgn", [2, 2], stack=st)
        onesf = sb("c_onesf", [2, P], stack=st)
        onesr = sb("c_onesr", [2, P], F32R, st)
        g1 = sb("c_g1", [P, 3, D], stack=st)
        g2 = sb("c_g2", [P, 3], stack=st)
        gh = sb("c_gh", [P, NSH, KF, B], F32R, st)
        gl = sb("c_gl", [P, NSH, KF, B], F32R, st)
        gT = sb("c_gT", [P, 3, B], stack=st)
        gr = sb("c_gr", [P, B], stack=st)
        gmx = sb("c_gmx", [P, 1], stack=st)
        gx = sb("c_gx", [P, 3], stack=st)
        ge = sb("c_ge", [P, 3], stack=st)
        gs = sb("c_gs", [P, 1], stack=st)
        gi = sb("c_gi", [P, 1], stack=st)
        wgt = sb("c_wgt", [P, 3], stack=st)
        xb = sb("c_xb", [P, NSH, SB, D], stack=st)
        xh = sb("c_xh", [P, W], F32R, st)
        xl = sb("c_xl", [P, W], F32R, st)
        hh = sb("c_hh", [P, NSH, KF, W], F32R, st)
        hl = sb("c_hl", [P, NSH, KF, W], F32R, st)
        yT = sb("c_yT", [P, W], stack=st)
        rows = sb("c_rows", [P, SB], I32, st)
        eo = sb("c_eo", [P, SB, D], stack=st)
        bs = sb("c_bs", [P, SB, 6], stack=st)
        mv = sb("c_mv", [P, SB, 2], stack=st)
        ve = sb("c_ve", [P, SB], stack=st)
        rs = sb("c_rs", [P, SB], stack=st)
        half = sb("c_half", [P, SB], stack=st)
        nm = sb("c_nm", [P, SB, D], stack=st)
        nh = sb("c_nh", [P, W], F32R, st)
        nl = sb("c_nl", [P, W], F32R, st)
        qkv = sb("c_qkv", [P, SB, 3 * D], stack=st)
        pT = pb("c_pT", [P, W], stack=st)
        pz = [pb(f"c_pz{k}", [P, W], stack=st) for k in range(3)]
        py = pb("c_py", [P, W], stack=st)
        pb_ = pb("c_pb", [P, SB, D], stack=st)
        pq = [pb(f"c_pq{n}", [P, W], stack=st) for n in range(2)]
        names = ("w_loaded wg_made wh_made wl_made bias_made bias_step bias_summed xb_made x_turned xh_made xl_made "
                 "z_made hh_made hl_made y_summed yT_made y_turned rows_made eo_loaded c_made stats mv_made ve_made "
                 "rs_made nm_made n_turned nh_made nl_made qkv_summed qkv_made qkv_stored halfed g_turned g_high g_low "
                 "g_z gh_made gl_made g_summed gT_made g_first gr_made g_second gate_step ge_made wgt_made").split()
        s_ = {n: sem("c_" + n, st) for n in names}
        (w_loaded, wg_made, wh_made, wl_made, bias_made, bias_step, bias_summed, xb_made, x_turned, xh_made, xl_made,
         z_made, hh_made, hl_made, y_summed, yT_made, y_turned, rows_made, eo_loaded, c_made, stats, mv_made, ve_made,
         rs_made, nm_made, n_turned, nh_made, nl_made, qkv_summed, qkv_made, qkv_stored, halfed, g_turned, g_high,
         g_low, g_z, gh_made, gl_made, g_summed, gT_made, g_first, gr_made, g_second, gate_step, ge_made,
         wgt_made) = (s_[n] for n in names)
        NT = NSH * NB
        U = 2 * NSH

        def block_of(n, c):
            return 2 * n + c // NSH, c % NSH

        with nc.Block() as block:
            @block.sync
            def _(sp):
                for dst, name in ((wraw[:], "w_qkv"), (lng[:], "ln1_g"), (lnb[:], "ln1_b"), (sgn[:], "signs"),
                                  (g1[:], "g1"), (g2[:], "g2")):
                    sp.dma_start(dst, a[name]).then_inc(w_loaded, 16)
                sp.dma_start(braw[:], a["b_qkv"].to_broadcast([2, 3 * D])).then_inc(w_loaded, 16)
                with sp.Fori(0, NB) as i:
                    sp.wait_ge(qkv_made, SB * i + SB)
                    sp.dma_start(qkv_dram[:, bass.ds(i * SB, SB), :], qkv[:]).then_inc(qkv_stored, 16)
                sp.wait_ge(qkv_stored, 16 * NB)

            @block.gpsimd
            def _(pool):
                def gather(i):
                    after(pool, eo_loaded, 16 * SB * i)
                    if not isinstance(i, int) or i:
                        pool.wait_ge(xb_made, i + 1)
                    pool.tensor_copy(rows[:], type_slot[:, bass.ds(i * SB, SB)]).then_inc(rows_made, 1)
                    carry(pool, halfed)
                    pool.wait_ge(rows_made, i + 1)
                    after(pool, c_made, i)
                    for u in range(SB):
                        pool.indirect_dma_start(eo[:, u, :], None, eo_dram,
                                                bass.IndirectOffsetOnAxis(ap=rows[:, u:u + 1], axis=0))\
                            .then_inc(eo_loaded, 16)

                def root(i):
                    pool.wait_ge(ve_made, i + 1)
                    pool.tensor_tensor(rs[:], ve[:], half[:], ALU.pow).then_inc(rs_made, 1)

                pool.memset(half[:], -0.5).then_inc(halfed, 1)
                gather(0)
                root(0)
                with pool.Fori(1, NB) as i:
                    gather(i)
                    root(i)

            @block.tensor
            def _(pe):
                pe.wait_ge(bias_made, 1)
                nc.tensor.matmul(pz[0][0:2, 0:3 * D], lnb2[:], wraw[:], start=True, stop=True).then_inc(bias_summed, 1)

                def gate():
                    nc.tensor.transpose(pT[:, 0:B], x1[:, 0, :], ident[:]).then_inc(g_turned, 1)
                    pe.wait_ge(g_low, 1)
                    for n in range(NSH):
                        for k in range(KF):
                            w, o = B_SWI + n * KF + k, pz[n + 1][:, k * B:(k + 1) * B]
                            nc.tensor.matmul(o, cwp[:, w, 0], xh[:, 0:B], start=True, stop=False)
                            nc.tensor.matmul(o, cwp[:, w, 0], xl[:, 0:B], start=False, stop=False)
                            last = nc.tensor.matmul(o, cwp[:, w, 1], xh[:, 0:B], start=False, stop=True)
                        last.then_inc(g_z, 1)
                    pe.wait_ge(eo_loaded, 16 * SB)
                    nc.tensor.transpose(pb_[:, 0, :], eo[:, 0, :], ident[:])
                    for n in range(NSH):
                        pe.wait_ge(gl_made, n + 1)
                        for k in range(KF):
                            w, o = B_SWO + n * KF + k, pb_[:, n + 1, :]
                            nc.tensor.matmul(o, cwp[:, w, 0], gh[:, n, k], start=(k == 0), stop=False)
                            nc.tensor.matmul(o, cwp[:, w, 0], gl[:, n, k], start=False, stop=False)
                            last = nc.tensor.matmul(o, cwp[:, w, 1], gh[:, n, k], start=False, stop=(k == KF - 1))
                    last.then_inc(g_summed, 1)
                    pe.wait_ge(gT_made, 1)
                    for n in range(3):
                        last = nc.tensor.matmul(pq[1][:, 0:B], g1[:, n, :], gT[:, n, :], start=(n == 0), stop=(n == 2))
                    last.then_inc(g_first, 1)
                    pe.wait_ge(gr_made, 1)
                    nc.tensor.matmul(pq[0][:, 0:3], gr[:], g2[:], start=True, stop=True).then_inc(g_second, 1)

                def turn(t, m):
                    pe.wait_ge(xb_made, t + 1)
                    for u in range(SB):
                        last = nc.tensor.transpose(pT[:, u * D:(u + 1) * D], xb[:, m, u, :], ident[:])
                    last.then_inc(x_turned, 1)

                def first(t, c):
                    m = c % NSH
                    pe.wait_ge(xl_made, t + 1)
                    for k in range(KF):
                        if k == 3:
                            pe.wait_ge(hl_made, KF * t + 1)
                        w, z = B_SWI + m * KF + k, pz[k % 3]
                        nc.tensor.matmul(z[:], cwp[:, w, 0], xh[:], start=True, stop=False)
                        nc.tensor.matmul(z[:], cwp[:, w, 0], xl[:], start=False, stop=False)
                        nc.tensor.matmul(z[:], cwp[:, w, 1], xh[:], start=False, stop=True).then_inc(z_made, 1)

                def second(t, i, m):
                    pe.wait_ge(hl_made, KF * t + KF)
                    if m == 0:
                        after(pe, yT_made, i)
                    for k in range(KF):
                        w = B_SWO + m * KF + k
                        nc.tensor.matmul(py[:], cwp[:, w, 0], hh[:, m, k], start=(m == 0 and k == 0), stop=False)
                        nc.tensor.matmul(py[:], cwp[:, w, 0], hl[:, m, k], start=False, stop=False)
                        last = nc.tensor.matmul(py[:], cwp[:, w, 1], hh[:, m, k], start=False,
                                                stop=(m == NSH - 1 and k == KF - 1))
                    last.then_inc(y_summed, 1)

                def turn_back(i):
                    pe.wait_ge(yT_made, i + 1)
                    after(pe, nl_made, i)
                    for u in range(SB):
                        last = nc.tensor.transpose(pb_[:, u, :], yT[:, u * B:(u + 1) * B], ident[:])
                    last.then_inc(y_turned, 1)

                def turn_normed(i):
                    pe.wait_ge(nm_made, i + 1)
                    for u in range(SB):
                        last = nc.tensor.transpose(pb_[:, u, :], nm[:, u, :], ident[:])
                    last.then_inc(n_turned, 1)

                def project(i):
                    pe.wait_ge(nl_made, i + 1)
                    for u in range(SB):
                        t = slice(u * B, (u + 1) * B)
                        o = pq[u % 2][:, 0:3 * D]
                        if u >= 2:
                            pe.wait_ge(qkv_made, SB * i + u - 1)
                        nc.tensor.matmul(o, onesr[:], bias[:], start=True, stop=False)
                        nc.tensor.matmul(o, nh[:, t], wh[:], start=False, stop=False)
                        nc.tensor.matmul(o, nh[:, t], wl[:], start=False, stop=False)
                        nc.tensor.matmul(o, nl[:, t], wh[:], start=False, stop=True).then_inc(qkv_summed, 1)

                gate()
                pe.wait_ge(wl_made, 1)
                pe.wait_ge(bias_made, 2)
                turn(0, 0)

                def step(n, t, c):
                    i, m = block_of(n, c)
                    if within(t, NT):
                        first(t, c)
                    if m == 0 and within(t - 2 * NSH, NT):
                        turn_normed(i - 2)
                    if m == 1 and within(t - NSH, NT):
                        turn_back(i - 1)
                    if within(t + 1, NT):
                        turn(t + 1, (m + 1) % NSH)
                    if m == 1 and within(t - 2 * NSH, NT):
                        project(i - 2)
                    if within(t - 1, NT):
                        second(t - 1, i if m else i - 1, (m - 1) % NSH)

                rolled(pe, step, NT, U, 2 * NSH)

            @block.scalar
            def _(act):
                act.wait_ge(wg_made, 1)
                act.activation(wh[:], wgm[:], ACT.Copy).then_inc(wh_made, 1)

                def gate():
                    act.wait_ge(g_turned, 1)
                    act.activation(xh[:, 0:B], pT[:, 0:B], ACT.Copy).then_inc(g_high, 1)
                    for n in range(NSH):
                        act.wait_ge(g_z, n + 1)
                        act.activation(gh[:, n].rearrange("p k b -> p (k b)"), pz[n + 1][:], ACT.Relu).then_inc(gh_made, 1)
                    act.wait_ge(g_summed, 1)
                    act.activation(gT[:], pb_[:, 0:3, :], ACT.Copy).then_inc(gT_made, 1)
                    act.wait_ge(g_first, 1)
                    act.activation(gr[:], pq[1][:, 0:B], ACT.Relu).then_inc(gr_made, 1)
                    act.wait_ge(gate_step, 2)
                    act.activation(ge[:], gx[:], ACT.Exp).then_inc(ge_made, 1)

                def high(t):
                    act.wait_ge(x_turned, t + 1)
                    act.activation(xh[:], pT[:], ACT.Copy).then_inc(xh_made, 1)

                def hidden(t, c):
                    for k in range(KF):
                        if k == 0:
                            after(act, y_summed, t - 1)
                        act.wait_ge(z_made, KF * t + k + 1)
                        act.activation(hh[:, c % NSH, k], pz[k % 3][:], ACT.Relu).then_inc(hh_made, 1)

                def sums(i):
                    act.wait_ge(y_summed, NSH * i + NSH)
                    after(act, y_turned, i)
                    act.activation(yT[:], py[:], ACT.Copy).then_inc(yT_made, 1)

                def normed(i):
                    act.wait_ge(n_turned, i + 1)
                    after(act, qkv_summed, SB * i)
                    act.activation(nh[:], pb_[:].rearrange("p u d -> p (u d)"), ACT.Copy).then_inc(nh_made, 1)

                def project(i):
                    after(act, qkv_stored, 16 * i)
                    for u in range(SB):
                        act.wait_ge(qkv_summed, SB * i + u + 1)
                        act.activation(qkv[:, u, :], pq[u % 2][:, 0:3 * D], ACT.Copy).then_inc(qkv_made, 1)

                def weigh(t, i, m):
                    act.activation(xb[:, m], x1[:, bass.ds(i * SB, SB), :], ACT.Copy, scale=wgt[:, m + 1:m + 2])\
                       .then_inc(xb_made, 1)

                gate()
                act.wait_ge(wgt_made, 1)
                weigh(0, 0, 0)
                weigh(1, 0, 1)
                high(0)

                def step(n, t, c):
                    i, m = block_of(n, c)
                    if within(t, NT):
                        hidden(t, c)
                    if m == 0 and within(t - 2 * NSH, NT):
                        normed(i - 2)
                    if within(t + 1, NT):
                        high(t + 1)
                    if within(t + 2, NT):
                        weigh(t + 2, i + 1, m)
                    if m == 0 and within(t - NSH, NT):
                        sums(i - 1)
                    if m == 1 and within(t - 2 * NSH, NT):
                        project(i - 2)

                rolled(act, step, NT, U, 2 * NSH)

            @block.vector
            def _(dve):
                dve.wait_ge(w_loaded, 16 * 7)
                nc.vector.tensor_copy(lnb2[:], lnb[:].to_broadcast([P, 2])).then_inc(bias_made, 1)
                nc.vector.tensor_scalar(wgm[:], wraw[:], lng[:, 0:1], None, ALU.mult).then_inc(wg_made, 1)
                dve.wait_ge(wh_made, 1)
                nc.vector.tensor_tensor(wl[:], wgm[:], wh[:].bitcast(F32), ALU.subtract).then_inc(wl_made, 1)

                def link(ins, n):
                    ins.then_inc(bias_step, 1)
                    dve.wait_ge(bias_step, n)

                def bias_parts():
                    dve.wait_ge(bias_summed, 1)
                    nc.vector.memset(onesf[:], 1.0)
                    link(nc.vector.tensor_tensor(bsum[:], pz[0][0:2, 0:3 * D], braw[:], ALU.add), 1)
                    nc.vector.tensor_copy(onesr[:], onesf[:])
                    link(nc.vector.tensor_copy(bhi[:], bsum[:]), 2)
                    link(nc.vector.tensor_scalar(bmul[:], bsum[:], sgn[:, 0:1], None, ALU.mult), 3)
                    nc.vector.scalar_tensor_tensor(bias[:], bhi[:].bitcast(F32), sgn[:, 1:2], bmul[:], ALU.mult, ALU.add)\
                        .then_inc(bias_made, 1)

                def gate():
                    def link(ins, n):
                        ins.then_inc(gate_step, 1)
                        dve.wait_ge(gate_step, n)

                    dve.wait_ge(g_high, 1)
                    nc.vector.tensor_tensor(xl[:, 0:B], pT[:, 0:B], xh[:, 0:B].bitcast(F32), ALU.subtract).then_inc(g_low, 1)
                    for n in range(NSH):
                        dve.wait_ge(gh_made, n + 1)
                        nc.vector.scalar_tensor_tensor(gl[:, n].rearrange("p k b -> p (k b)"), pz[n + 1][:], 0.0,
                                                       gh[:, n].rearrange("p k b -> p (k b)").bitcast(F32),
                                                       ALU.max, ALU.subtract).then_inc(gl_made, 1)
                    bias_parts()
                    dve.wait_ge(g_second, 1)
                    link(nc.vector.tensor_reduce(gmx[:], pq[0][:, 0:3], AX, ALU.max), 1)
                    link(nc.vector.tensor_scalar(gx[:], pq[0][:, 0:3], gmx[:, 0:1], None, ALU.subtract), 2)
                    dve.wait_ge(ge_made, 1)
                    link(nc.vector.tensor_reduce(gs[:], ge[:], AX, ALU.add), 3)
                    link(nc.vector.reciprocal(gi[:], gs[:]), 4)
                    nc.vector.tensor_scalar(wgt[:], ge[:], gi[:, 0:1], None, ALU.mult).then_inc(wgt_made, 1)

                def low(t):
                    dve.wait_ge(xh_made, t + 1)
                    nc.vector.tensor_tensor(xl[:], pT[:], xh[:].bitcast(F32), ALU.subtract).then_inc(xl_made, 1)

                def hidden(t, c):
                    for k in range(KF):
                        dve.wait_ge(hh_made, KF * t + k + 1)
                        nc.vector.scalar_tensor_tensor(hl[:, c % NSH, k], pz[k % 3][:], 0.0,
                                                       hh[:, c % NSH, k].bitcast(F32), ALU.max, ALU.subtract)\
                            .then_inc(hl_made, 1)

                def mix(i):
                    dve.wait_ge(eo_loaded, 16 * SB * (i + 1))
                    dve.wait_ge(y_turned, i + 1)
                    nc.vector.scalar_tensor_tensor(cres[:, bass.ds(i * SB, SB), :], eo[:], wgt[:, 0:1], pb_[:],
                                                   ALU.mult, ALU.add).then_inc(c_made, 1)

                def normalise(i):
                    carry(dve, wgt_made)
                    dve.wait_ge(c_made, i + 1)
                    for u in range(SB):
                        last = nc.vector.bn_stats(bs[:, u, :], cres[:, i * SB + u, :])
                    last.then_inc(stats, 1)
                    carry(dve, wgt_made)
                    dve.wait_ge(stats, i + 1)
                    for u in range(SB):
                        last = nc.vector.bn_aggr(mv[:, u, :], bs[:, u, :])
                    last.then_inc(mv_made, 1)
                    dve.wait_ge(mv_made, i + 1)
                    nc.vector.tensor_scalar(ve[:], mv[:, :, 1], EPS, None, ALU.add).then_inc(ve_made, 1)
                    dve.wait_ge(rs_made, i + 1)
                    after(dve, n_turned, i)
                    for u in range(SB):
                        last = nc.vector.tensor_scalar(nm[:, u, :], cres[:, i * SB + u, :], mv[:, u, 0:1],
                                                       rs[:, u:u + 1], ALU.subtract, ALU.mult)
                    last.then_inc(nm_made, 1)

                def normed(i):
                    dve.wait_ge(nh_made, i + 1)
                    nc.vector.tensor_tensor(nl[:], pb_[:].rearrange("p u d -> p (u d)"), nh[:].bitcast(F32), ALU.subtract)\
                        .then_inc(nl_made, 1)

                gate()
                dve.wait_ge(wgt_made, 1)
                low(0)

                def step(n, t, c):
                    i, m = block_of(n, c)
                    if within(t, NT):
                        hidden(t, c)
                    if m == 0 and within(t - 2 * NSH, NT):
                        normed(i - 2)
                    if m == 1 and within(t - NSH, NT):
                        mix(i - 1)
                    if within(t + 1, NT):
                        low(t + 1)
                    if m == 1 and within(t - NSH, NT):
                        normalise(i - 1)

                rolled(dve, step, NT, U, 2 * NSH)


def attention(nc, a, sb, pb, sem, ident, hmask, qkv_dram, att_dram, mwp):
    SC = 1.0 / float(np.sqrt(DK))
    NQ = B // BT
    C4 = P // S
    NS = NQ // C4
    GW = D // HG
    MC = MB // NQ
    with ExitStack() as st:
        quad = sb("t_quad", [P, BT], stack=st)
        qk = sb("t_qk", [P, BT, 2, HG, GW], stack=st)
        qkg = sb("t_qkg", [P, 2, HG, BT, GW], stack=st)
        vt = sb("t_vt", [P, C4, BT, D], stack=st)
        vs = sb("t_vs", [P, 2, BT, HG, GW], stack=st)
        qs = sb("t_qs", [P, 2, HG, BT, S], stack=st)
        ks = sb("t_ks", [P, 2, HG, HG, S], stack=st)
        sm = sb("t_sm", [P, H, S], stack=st)
        p = sb("t_p", [P, 2, H, S], stack=st)
        hones = sb("t_hones", [P, HG, DK], stack=st)
        ptT = sb("t_ptT", [P, 2, HG, P], stack=st)
        oT = sb("t_oT", [P, 2, P], stack=st)
        ri = sb("t_ri", [P, P], stack=st)
        mx = sb("t_mx", [P, H], stack=st)
        wo = sb("t_wo", [P, D], stack=st)
        bo = sb("t_bo", [P, D], stack=st)
        att = sb("t_att", [P, C4, D], stack=st)
        raw = sb("t_raw", [P, 2, MC, D], stack=st)
        pq = pb("t_pq", [P, HG, P], stack=st)
        pk = pb("t_pk", [P, HG, P], stack=st)
        ps = [pb(f"t_ps{n}", [P, H, S], stack=st) for n in range(2)]
        pt = [pb(f"t_pt{n}", [P, HG, P], stack=st) for n in range(2)]
        po = pb("t_po", [P, 2, 2, P], stack=st)
        pj = pb("t_pj", [P, 512], stack=st)
        names = ("w_loaded qk_loaded grouped turned qs_made ks_made scored mx_made sub_made p_made ri_made "
                 "hones_made p_turned ptT_made vs_made o_summed oT_made w_summed att_made high low").split()
        s_ = {n: sem("t_" + n, st) for n in names}
        (w_loaded, qk_loaded, grouped, turned, qs_made, ks_made, scored, mx_made, sub_made, p_made, ri_made,
         hones_made, p_turned, ptT_made, vs_made, o_summed, oT_made, w_summed, att_made, high, low) = (s_[n] for n in names)
        v_loaded = [sem(f"t_v_loaded{c}", st) for c in range(C4)]
        att_stored = [sem(f"t_att_stored{c}", st) for c in range(C4)]
        raw_loaded = [sem(f"t_raw_loaded{c}", st) for c in range(2)]
        qk_rows = qkv_dram[:, :, 0:2 * D].rearrange("(n c b) s (w g d) -> n c s b w g d", n=NS, c=C4, w=2, g=HG)
        v_rows = qkv_dram[:, :, 2 * D:].rearrange("(n b) s d -> n s b d", n=NQ)
        att_rows = att_dram.rearrange("(n b) s d -> n (b s) d", n=NQ)

        def quartets(eng, step, drain, head=1):
            rolled(eng, step, NQ, C4, drain, tail=2, head=head)

        def has(t, back=0):
            return within(t - back, NQ)

        with nc.Block() as block:
            @block.sync
            def _(sp):
                sp.dma_start(wo[:], a["w_o"]).then_inc(w_loaded, 16)
                sp.dma_start(bo[:], a["b_o"].to_broadcast([P, D])).then_inc(w_loaded, 16)
                sp.dma_start(quad[:], a["quad"]).then_inc(w_loaded, 16)

                def load_v(t, c):
                    src = v_rows[t] if isinstance(t, int) else v_rows[bass.ds(t, 1)].rearrange("o s b d -> (o s) b d")
                    for j in range(HG):
                        sp.dma_start(vt[j * S:(j + 1) * S, c], src).then_inc(v_loaded[c], 16)

                def load_raw(t, c):
                    cols = slice(t * MC, (t + 1) * MC) if isinstance(t, int) else bass.ds(t * MC, MC)
                    sp.dma_start(raw[:, c % 2], a["mw"][:, cols, :]).then_inc(raw_loaded[c % 2], 16)

                for c in range(2):
                    load_raw(c, c)
                for c in range(C4):
                    load_v(c, c)

                def step(n, t, c):
                    if has(t, -2):
                        sp.wait_ge(low, t + 1)
                        load_raw(t + 2, c)
                    if has(t, -C4):
                        sp.wait_ge(vs_made, t + 1)
                        load_v(t + C4, c)
                    if has(t, 3):
                        sp.wait_ge(att_made, t - 2)
                        q = (c - 3) % C4
                        dst = att_rows[t - 3] if isinstance(t, int) else \
                            att_rows[bass.ds(t - 3, 1)].rearrange("o p d -> (o p) d")
                        sp.dma_start(dst, att[:, q]).then_inc(att_stored[q], 16)

                quartets(sp, step, 3)
                for q in range(C4):
                    sp.wait_ge(att_stored[q], 16 * NS)

            @block.gpsimd
            def _(pool):
                pool.wait_ge(w_loaded, 48)

                def values(n, t, c):
                    pool.wait_ge(v_loaded[c], 16 * HG * n + 16 * HG)
                    after(pool, o_summed, t - 1)
                    pool.tensor_tensor(vs[:, c % 2].rearrange("p b g (j d) -> p (b g) j d", j=HG),
                                       vt[:, c].rearrange("p b (g j d) -> p (b g) j d", g=HG, j=HG),
                                       quad[:, None, :, None].to_broadcast([P, BT * HG, HG, DK]),
                                       ALU.mult).then_inc(vs_made, 1)

                def step(n, t, c):
                    values(n, t, c)
                    cols = slice(t * MC, (t + 1) * MC) if isinstance(t, int) else bass.ds(t * MC, MC)
                    pool.wait_ge(raw_loaded[c % 2], 32 * n + 16 * (c // 2) + 16)
                    pool.tensor_copy(mwp[:, cols, 0], raw[:, c % 2]).then_inc(high, 1)
                    pool.wait_ge(high, t + 1)
                    pool.tensor_tensor(mwp[:, cols, 1], raw[:, c % 2], mwp[:, cols, 0].bitcast(F32), ALU.subtract)\
                        .then_inc(low, 1)

                quartets(pool, step, 0)

            @block.tensor
            def _(pe):
                def turn_qk(n):
                    pe.wait_ge(grouped, 2 * n + 2)
                    after(pe, qs_made, C4 * n)
                    after(pe, ks_made, C4 * n)
                    for w, dst in enumerate((pq, pk)):
                        for g in range(HG):
                            last = nc.tensor.transpose(dst[:, g, :], qkg[:, w, g].rearrange("p b d -> p (b d)"), ident[:])
                    last.then_inc(turned, 1)

                def scores(t, q):
                    pe.wait_ge(qs_made, t + 1)
                    pe.wait_ge(ks_made, t + 1)
                    after(pe, sub_made, t - 1)
                    for g in range(HG):
                        last = nc.tensor.matmul(ps[q][:, g * HG:(g + 1) * HG, :], qs[:, q, g].rearrange("p b s -> p (b s)"),
                                                ks[:, q, g], start=True, stop=True)
                    last.then_inc(scored, 1)

                def turn_p(t, q):
                    pe.wait_ge(p_made, t + 1)
                    after(pe, ptT_made, t - 1)
                    for g in range(HG):
                        last = nc.tensor.transpose(pt[q][:, g, :],
                                                   p[:, q, g * HG:(g + 1) * HG].rearrange("p j k -> p (j k)"), ident[:])
                    last.then_inc(p_turned, 1)

                def values(t, q):
                    pe.wait_ge(ptT_made, t + 1)
                    pe.wait_ge(vs_made, t + 1)
                    after(pe, oT_made, t - 1)
                    for b in range(BT):
                        for g in range(HG):
                            nc.tensor.matmul(po[g * GW:(g + 1) * GW, q, 0, b * S:(b + 1) * S], vs[:, q, b, g],
                                             ptT[:, q, g, b * S:(b + 1) * S], start=True, stop=True)
                    for g in range(HG):
                        last = nc.tensor.matmul(po[g * GW:(g + 1) * GW, q, 1], hones[:].rearrange("p j d -> p (j d)"),
                                                ptT[:, q, g], start=True, stop=True)
                    last.then_inc(o_summed, 1)

                def project(t, q):
                    pe.wait_ge(oT_made, t + 1)
                    after(pe, att_made, t)
                    nc.tensor.matmul(pj[:, 0:D], oT[:, q], wo[:], start=True, stop=True).then_inc(w_summed, 1)

                pe.wait_ge(w_loaded, 48)
                pe.wait_ge(hones_made, 1)
                turn_qk(0)

                def step(n, t, c):
                    if has(t):
                        scores(t, c % 2)
                    if has(t, 2):
                        turn_p(t - 2, c % 2)
                    if has(t, 3):
                        project(t - 3, (c - 3) % 2)
                    if has(t, 2):
                        values(t - 2, c % 2)
                    if c == 2 and within(n + 1, NS):
                        turn_qk(n + 1)

                quartets(pe, step, 3)

            @block.scalar
            def _(act):
                def load_qk(n, c):
                    src = qk_rows[n, c] if isinstance(n, int) else \
                        qk_rows[bass.ds(n, 1), c].rearrange("o s b w g d -> (o s) b w g d")
                    act.dma_start(qk[c * S:(c + 1) * S].rearrange("s b w g d -> s b (w g d)"),
                                  src.rearrange("s b w g d -> s b (w g d)")).then_inc(qk_loaded, 16)

                def group(n, w):
                    act.wait_ge(qk_loaded, 16 * C4 * n + 16 * C4)
                    after(act, turned, n)
                    act.activation(qkg[:, w], qk[:, :, w].rearrange("p b g d -> p g b d"), ACT.Copy).then_inc(grouped, 1)

                def keys(n, t, c):
                    act.wait_ge(turned, n + 1)
                    after(act, scored, t - 1)
                    for j in range(HG):
                        last = act.activation(ks[:, c % 2, :, j, :], pk[:, :, c * S:(c + 1) * S], ACT.Copy,
                                              scale=hmask[:, j:j + 1])
                    last.then_inc(ks_made, 1)

                def exps(t, q):
                    act.wait_ge(sub_made, t + 1)
                    after(act, p_turned, t - 1)
                    act.activation(p[:, q], sm[:], ACT.Exp, scale=SC).then_inc(p_made, 1)

                def probs(t, q):
                    act.wait_ge(p_turned, t + 1)
                    after(act, o_summed, t - 1)
                    act.activation(ptT[:, q], pt[q][:], ACT.Copy).then_inc(ptT_made, 1)

                for c in range(C4):
                    load_qk(0, c)
                for w in range(2):
                    group(0, w)
                act.wait_ge(grouped, 2)
                for c in range(2):
                    load_qk(1, c)
                keys(0, 0, 0)

                def step(n, t, c):
                    if has(t, 2):
                        probs(t - 2, c % 2)
                    if has(t, -1):
                        keys(n if c + 1 < C4 else n + 1, t + 1, (c + 1) % C4)
                    if has(t):
                        exps(t, c % 2)
                    if c == 1 and within(n + 1, NS):
                        for w in range(2):
                            group(n + 1, w)
                    if c == 0 and within(n + 1, NS):
                        load_qk(n + 1, 2)
                        load_qk(n + 1, 3)
                    if c in (2, 3) and within(n + 2, NS):
                        if c == 2:
                            act.wait_ge(grouped, 2 * n + 4)
                        load_qk(n + 2, c - 2)

                quartets(act, step, 2)

            @block.vector
            def _(dve):
                def queries(n, t, c):
                    dve.wait_ge(turned, n + 1)
                    after(dve, scored, t - 1)
                    nc.vector.tensor_tensor(qs[:, c % 2], pq[:, :, None, c * S:(c + 1) * S].to_broadcast([P, HG, BT, S]),
                                            quad[:, None, :, None].to_broadcast([P, HG, BT, S]), ALU.mult)\
                        .then_inc(qs_made, 1)

                def maxima(t, q):
                    dve.wait_ge(scored, t + 1)
                    after(dve, sub_made, t)
                    nc.vector.tensor_reduce(mx[:], ps[q][:], AX, ALU.max).then_inc(mx_made, 1)
                    dve.wait_ge(mx_made, t + 1)
                    after(dve, p_made, t)
                    nc.vector.tensor_tensor(sm[:], ps[q][:], mx[:, :, None].to_broadcast([P, H, S]), ALU.subtract)\
                        .then_inc(sub_made, 1)

                def divided(t, q):
                    dve.wait_ge(o_summed, t + 1)
                    nc.vector.reciprocal(ri[:], po[:, q, 1]).then_inc(ri_made, 1)
                    dve.wait_ge(ri_made, t + 1)
                    after(dve, w_summed, t - 1)
                    nc.vector.tensor_tensor(oT[:, q], po[:, q, 0], ri[:], ALU.mult).then_inc(oT_made, 1)

                def result(n, t, c):
                    dve.wait_ge(w_summed, t + 1)
                    after(dve, att_stored[c], 16 * n)
                    nc.vector.tensor_tensor(att[:, c], pj[:, 0:D], bo[:], ALU.add).then_inc(att_made, 1)

                dve.wait_ge(w_loaded, 48)
                nc.vector.tensor_copy(hones[:], quad[:, :, None].to_broadcast([P, HG, DK])).then_inc(hones_made, 1)
                queries(0, 0, 0)

                def step(n, t, c):
                    if has(t, -1):
                        queries(n if c + 1 < C4 else n + 1, t + 1, (c + 1) % C4)
                    if has(t, 3):
                        divided(t - 3, (c - 3) % 2)
                    if has(t):
                        maxima(t, c % 2)
                    if has(t, 3):
                        result(n - 1 + (c + 1) // C4, t - 3, (c + 1) % C4)

                quartets(dve, step, 3, head=2)


def second_norm(nc, a, sb, pb, sem, ident, ones, tri, x1, cres, att_dram, h_dram, tags_dram, expert_of_tile,
                row_of_tile, biases):
    SE = [P, SB, E]
    with ExitStack() as st:
        att = sb("d_att", [P, 2, SB, D], stack=st)
        x2 = sb("d_x2", [P, 2, SB, D], stack=st)
        bs = sb("d_bs", [P, SB, 6], stack=st)
        mv = sb("d_mv", [P, SB, 2], stack=st)
        ve = sb("d_ve", [P, SB], stack=st)
        rs = sb("d_rs", [P, SB], stack=st)
        half = sb("d_half", [P, SB], stack=st)
        nm = sb("d_nm", [P, 2, SB, D], stack=st)
        hT = sb("d_hT", [P, W], stack=st)
        b1, b2, onesr, gbc = biases
        b2r = sb("d_b2r", [2, E * D], stack=st)
        b2h = sb("d_b2h", [2, E * D], F32R, st)
        b2m = sb("d_b2m", [2, E * D], stack=st)
        sgn = sb("d_sgn", [2, 2], stack=st)
        offs = sb("d_offs", [P, P], stack=st)
        gw = sb("d_gw", [P, E], stack=st)
        gwm = sb("d_gwm", [P, E], stack=st)
        gbias = sb("d_gbias", [P, E], stack=st)
        gb2 = sb("d_gb2", [P, E], stack=st)
        c = sb("d_c", [P, 2 * E + ET], stack=st)
        lb = sb("d_lb", SE, stack=st)
        ids = sb("d_ids", [P, S, 2, TAG], I32, st)
        tags = sb("d_tags", [P, 2, SB, 2, TAG], I32, st)
        slots = sb("d_slots", [P, 2, 2, SB], I32, st)
        m1, m2, r1, r2, dl, ex, ex1, w1, sf = (sb("d_" + n, [P, SB], stack=st) for n in
                                               ("m1", "m2", "r1", "r2", "dl", "ex", "ex1", "w1", "sf"))
        eq, ew, k1, k2, l2, both, exc, rank, pick = (sb("d_" + n, SE, stack=st) for n in
                                                     ("eq", "ew", "k1", "k2", "l2", "both", "exc", "rank", "pick"))
        tot, run, base, place, lens, endt, gap = (sb("d_" + n, [P, E], stack=st) for n in
                                                  ("tot", "run", "base", "place", "lens", "endt", "gap"))
        cnti = sb("d_cnti", [P, E], I32, st)
        cnts = sb("d_cnts", [P, E], I32, st)
        past = sb("d_past", [1, E - 1, ET], stack=st)
        gaps = sb("d_gaps", [1, E - 1, ET], stack=st)
        totile = sb("d_totile", [1, ET], stack=st)
        gsum = sb("d_gsum", [1, ET], stack=st)
        rowf = sb("d_rowf", [1, ET], stack=st)
        pT = pb("d_pT", [P, W], stack=st)
        pl = pb("d_pl", [P, 512], stack=st)
        pc = pb("d_pc", [P, 512], stack=st)
        pp = pb("d_pp", [P, 512], stack=st)
        names = ("w_loaded x2_made x1_made stats mv_made ve_made rs_made nm_made h_turned hT_made "
                 "summed l_made halfed offs_made bias_summed gate_made dl_made ex_made totals prefix tagged "
                 "tags_set end_step b1_loaded b2_loaded b2_step").split()
        s_ = {n: sem("d_" + n, st) for n in names}
        (w_loaded, x2_made, x1_made, stats, mv_made, ve_made, rs_made, nm_made, h_turned, hT_made, summed, l_made,
         halfed, offs_made, bias_summed, gate_made, dl_made, ex_made, totals, prefix, tagged, tags_set,
         end_step, b1_loaded, b2_loaded, b2_step) = (s_[n] for n in names)
        routed = [sem(f"d_routed{q}", st) for q in range(36)]
        h_stored = [sem(f"d_h_stored{q}", st) for q in range(2)]
        sent = [sem(f"d_sent{q}", st) for q in range(2)]
        C_W, C_O, C_T = 0, E, 2 * E
        att_loaded = [sem(f"d_att_loaded{q}", st) for q in range(2)]

        with nc.Block() as block:
            @block.sync
            def _(sp):
                for q in range(2):
                    sp.dma_start(att[:, q], att_dram[:, q * SB:(q + 1) * SB, :]).then_inc(att_loaded[q], 16)
                for dst, src in ((gbc[:], a["ln2c"]), (gw[:], a["gate_w"]), (gbias[:], a["gate_b"].to_broadcast([P, E])),
                                 (c[:], a["rconsts"]), (ids[:], a["ids"])):
                    sp.dma_start(dst, src).then_inc(w_loaded, 16)
                sp.dma_start(tags_dram, a["tags"]).then_inc(tags_set, 16)
                sp.dma_start(b2r[:], a["m_b2"].to_broadcast([2, E * D])).then_inc(b2_loaded, 16)
                sp.dma_start(sgn[:], a["signs"]).then_inc(b2_loaded, 16)
                sp.dma_start(b1[:], a["m_b1"].to_broadcast([P, E * FF])).then_inc(b1_loaded, 16)

                def step(n, i, c):
                    if within(i + 2, NB):
                        sp.wait_ge(x2_made, i + 1)
                        sp.dma_start(att[:, c], att_dram[:, bass.ds((i + 2) * SB, SB), :]).then_inc(att_loaded[c], 16)

                    sp.wait_ge(nm_made, i + 1)
                    sp.dma_start(h_dram[:, bass.ds(i * SB, SB), :], nm[:, c]).then_inc(h_stored[c], 16)

                rolled(sp, step, NB, 2, 0)
                for q in range(2):
                    sp.wait_ge(h_stored[q], 16 * (NB // 2))
                sp.wait_ge(b1_loaded, 16)

            @block.gpsimd
            def _(pool):
                pool.memset(half[:], -0.5).then_inc(halfed, 1)
                pool.wait_ge(halfed, 1)

                def root(i):
                    pool.wait_ge(ve_made, i + 1)
                    after(pool, rs_made, i - 1)
                    pool.tensor_tensor(rs[:], ve[:], half[:], ALU.pow).then_inc(rs_made, 1)

                def scatter(i, c):
                    carry(pool, halfed)
                    pool.wait_ge(tagged, i + 1)
                    for u in range(SB):
                        for k in range(2):
                            pool.indirect_dma_start(tags_dram,
                                                    bass.IndirectOffsetOnAxis(ap=slots[:, c, k, u:u + 1], axis=0),
                                                    tags[:, c, u, k, :], None).then_inc(sent[c], 16)

                root(0)
                pool.wait_ge(tags_set, 16)

                def step(n, i, c):
                    if within(i + 1, NB):
                        root(i + 1)
                    if within(i - 1, NB):
                        scatter(i - 1, (c - 1) % 2)

                rolled(pool, step, NB, 2, 1)
                for q in range(2):
                    pool.wait_ge(sent[q], 16 * 2 * SB * (NB // 2))

            @block.tensor
            def _(pe):
                pe.wait_ge(offs_made, 1)
                nc.tensor.matmul(pl[:, 0:E], offs[:], gw[:], start=True, stop=True).then_inc(bias_summed, 1)

                def turn(i, c):
                    pe.wait_ge(nm_made, i + 1)
                    after(pe, hT_made, i)
                    for u in range(SB):
                        last = nc.tensor.transpose(pT[:, u * D:(u + 1) * D], nm[:, c, u, :], ident[:])
                    last.then_inc(h_turned, 1)

                def sums(i):
                    pe.wait_ge(hT_made, i + 1)
                    after(pe, l_made, i)
                    for u in range(SB):
                        last = nc.tensor.matmul(pl[:, u * E:(u + 1) * E], hT[:, u * B:(u + 1) * B], gwm[:],
                                                start=True, stop=True)
                    last.then_inc(summed, 1)

                def counts(i):
                    pe.wait_ge(totals, i + 1)
                    nc.tensor.matmul(pc[:, 0:E], ones[:], tot[:], start=True, stop=True)
                    nc.tensor.matmul(pp[:, 0:E], tri[:], tot[:], start=True, stop=True).then_inc(prefix, 1)

                pe.wait_ge(gate_made, 1)

                def step(n, i, c):
                    if within(i, NB):
                        turn(i, c)
                        sums(i)
                    if within(i - 1, NB):
                        counts(i - 1)

                rolled(pe, step, NB, 2, 1)

            @block.scalar
            def _(act):
                def step(n, i, c):
                    if within(i, NB):
                        act.wait_ge(h_turned, i + 1)
                        act.activation(hT[:], pT[:], ACT.Copy).then_inc(hT_made, 1)
                    if within(i - 1, NB):
                        act.wait_ge(dl_made, i)
                        act.activation(ex[:], dl[:], ACT.Exp).then_inc(ex_made, 1)

                rolled(act, step, NB, 2, 1)

            @block.vector
            def _(dve):
                def statistics(n, i, c):
                    dve.wait_ge(att_loaded[c], 16 * n + 16)
                    nc.vector.tensor_tensor(x2[:, c], cres[:, bass.ds(i * SB, SB), :], att[:, c], ALU.add).then_inc(x2_made, 1)
                    carry(dve, gate_made)
                    dve.wait_ge(x2_made, i + 1)
                    for u in range(SB):
                        last = nc.vector.bn_stats(bs[:, u, :], x2[:, c, u, :])
                    last.then_inc(stats, 1)
                    carry(dve, gate_made)
                    dve.wait_ge(stats, i + 1)
                    for u in range(SB):
                        last = nc.vector.bn_aggr(mv[:, u, :], bs[:, u, :])
                    last.then_inc(mv_made, 1)
                    dve.wait_ge(mv_made, i + 1)
                    nc.vector.tensor_scalar(ve[:], mv[:, :, 1], EPS, None, ALU.add).then_inc(ve_made, 1)
                    v = x1[:, bass.ds(i * SB, SB), :]
                    nc.vector.tensor_tensor(v, v, x2[:, c], ALU.add).then_inc(x1_made, 1)

                def normalise(n, i, c):
                    dve.wait_ge(rs_made, i + 1)
                    after(dve, h_stored[c], 16 * n)
                    for u in range(SB):
                        last = nc.vector.tensor_scalar(nm[:, c, u, :], x2[:, c, u, :], mv[:, u, 0:1], rs[:, u:u + 1],
                                                       ALU.subtract, ALU.mult)
                    last.then_inc(nm_made, 1)

                def gate(i):
                    dve.wait_ge(summed, i + 1)
                    nc.vector.tensor_tensor(lb[:],
                                            pl[:, 0:SB * E].rearrange("p (u e) -> p u e", e=E),
                                            gb2[:, None, :].to_broadcast([P, SB, E]), ALU.add).then_inc(l_made, 1)

                order = c[:, None, C_W:C_O].to_broadcast(SE)
                wide = lambda t: t[:, :, None].to_broadcast(SE)

                def route(n, i, q):
                    links = iter(routed)

                    def link(ins):
                        s = next(links)
                        ins.then_inc(s, 1)
                        dve.wait_ge(s, i + 1)

                    def best(values, m, r, k):
                        link(nc.vector.tensor_reduce(m[:], values, AX, ALU.max))
                        link(nc.vector.tensor_tensor(eq[:], values, wide(m), ALU.is_equal))
                        link(nc.vector.tensor_tensor(ew[:], eq[:], order, ALU.mult))
                        link(nc.vector.tensor_reduce(r[:], ew[:], AX, ALU.max))
                        link(nc.vector.tensor_tensor(k[:], order, wide(r), ALU.is_equal))

                    dve.wait_ge(l_made, i + 1)
                    best(lb[:], m1, r1, k1)
                    link(nc.vector.scalar_tensor_tensor(l2[:], k1[:], -3.0e38, lb[:], ALU.mult, ALU.add))
                    best(l2[:], m2, r2, k2)
                    nc.vector.tensor_tensor(dl[:], m2[:], m1[:], ALU.subtract).then_inc(dl_made, 1)
                    link(nc.vector.tensor_tensor(both[:], k1[:], k2[:], ALU.add))
                    link(nc.vector.tensor_copy(exc[:, 1, :], both[:, 0, :]))
                    for u in range(2, SB):
                        link(nc.vector.tensor_tensor(exc[:, u, :], exc[:, u - 1, :], both[:, u - 1, :], ALU.add))
                    nc.vector.tensor_tensor(tot[:], exc[:, SB - 1, :], both[:, SB - 1, :], ALU.add).then_inc(totals, 1)
                    after(dve, sent[q], 16 * 2 * SB * n)
                    link(nc.vector.tensor_copy(tags[:, q], ids[:, bass.ds(i * SB, SB)]))
                    dve.wait_ge(ex_made, i + 1)
                    link(nc.vector.tensor_scalar(ex1[:], ex[:], 1.0, None, ALU.add))
                    link(nc.vector.reciprocal(w1[:], ex1[:]))
                    tf = tags[:, q].bitcast(F32)
                    nc.vector.tensor_copy(tf[:, :, 0, 2], w1[:])
                    link(nc.vector.tensor_tensor(tf[:, :, 1, 2], ex[:], w1[:], ALU.mult))
                    link(nc.vector.tensor_tensor(base[:], run[:], c[:, C_O:C_T], ALU.add))
                    dve.wait_ge(prefix, i + 1)
                    link(nc.vector.tensor_tensor(place[:], pp[:, 0:E], base[:], ALU.add))
                    link(nc.vector.tensor_tensor(run[:], pc[:, 0:E], run[:], ALU.add))
                    link(nc.vector.tensor_tensor(rank[:], exc[:], place[:, None, :].to_broadcast(SE), ALU.add))
                    for k, one in enumerate((k1, k2)):
                        link(nc.vector.tensor_tensor(pick[:], rank[:], one[:], ALU.mult))
                        link(nc.vector.tensor_reduce(sf[:], pick[:], AX, ALU.add))
                        ins = nc.vector.tensor_copy(slots[:, q, k], sf[:])
                        if k == 0:
                            link(ins)
                    ins.then_inc(tagged, 1)

                def deal():
                    done = [0]

                    def link(ins):
                        done[0] += 1
                        ins.then_inc(end_step, 1)
                        dve.wait_ge(end_step, done[0])

                    link(nc.vector.tensor_scalar(lens[:], run[:], float(P - 1), None, ALU.add))
                    link(nc.vector.tensor_copy(cnti[:], lens[:]))
                    link(nc.vector.tensor_scalar(cnts[:], cnti[:], 7, 7, ALU.logical_shift_right, ALU.logical_shift_left))
                    link(nc.vector.tensor_copy(lens[:], cnts[:]))
                    link(nc.vector.tensor_tensor_scan(endt[:], ones[:, 0:E], lens[:], 0.0, ALU.mult, ALU.add))
                    link(nc.vector.tensor_scalar(gap[:], lens[:], -1.0, float(T), ALU.mult, ALU.add))
                    lines = [1, E - 1, ET]
                    link(nc.vector.tensor_tensor(past[:], c[0:1, None, C_T:C_T + ET].to_broadcast(lines),
                                                 endt[0:1, 0:E - 1, None].to_broadcast(lines), ALU.is_ge))
                    link(nc.vector.tensor_tensor(gaps[:], past[:], gap[0:1, 0:E - 1, None].to_broadcast(lines), ALU.mult))
                    link(nc.vector.tensor_reduce(totile[0:1, :], past[0:1, :, :].rearrange("p n j -> p j n"), AX, ALU.add))
                    link(nc.vector.tensor_copy(expert_of_tile[0:1, :], totile[0:1, :]))
                    link(nc.vector.tensor_reduce(gsum[0:1, :], gaps[0:1, :, :].rearrange("p n j -> p j n"), AX, ALU.add))
                    link(nc.vector.tensor_tensor(rowf[0:1, :], gsum[0:1, :], c[0:1, C_T:C_T + ET], ALU.add))
                    link(nc.vector.tensor_copy(row_of_tile[0:1, :], rowf[0:1, :]))

                nc.vector.memset(run[:], 0.0)
                nc.vector.memset(exc[:], 0.0)
                dve.wait_ge(w_loaded, 80)
                nc.vector.tensor_copy(offs[:], gbc[:, 1:2].to_broadcast([P, P])).then_inc(offs_made, 1)
                nc.vector.tensor_scalar(gwm[:], gw[:], gbc[:, 0:1], None, ALU.mult)
                dve.wait_ge(bias_summed, 1)
                nc.vector.tensor_tensor(gb2[:], pl[:, 0:E], gbias[:], ALU.add).then_inc(gate_made, 1)
                dve.wait_ge(gate_made, 1)
                nc.vector.tensor_copy(onesr[:], ones[0:2, :])
                dve.wait_ge(b2_loaded, 32)
                nc.vector.tensor_copy(b2h[:], b2r[:]).then_inc(b2_step, 1)
                nc.vector.tensor_scalar(b2m[:], b2r[:], sgn[:, 0:1], None, ALU.mult).then_inc(b2_step, 1)
                dve.wait_ge(b2_step, 2)
                nc.vector.scalar_tensor_tensor(b2[:], b2h[:].bitcast(F32), sgn[:, 1:2], b2m[:], ALU.mult, ALU.add)

                statistics(0, 0, 0)

                def step(n, i, c):
                    if within(i - 1, NB):
                        gate(i - 1)
                    if within(i, NB):
                        normalise(n, i, c)
                    if within(i + 1, NB):
                        statistics(*behind(n, i, c, -1, 2))
                    if within(i - 1, NB):
                        route(*behind(n, i, c, 1, 2))

                rolled(dve, step, NB, 2, 1, head=2)
                deal()


def experts(nc, sb, pb, sem, ident, expert_of_tile, row_of_tile, h_dram, tags_dram, y_dram, mwp,
            biases):
    U, R = EXPERT_UNROLL, 3
    AHEAD = 7
    with ExitStack() as st:
        b1, b2, onesr, gbc = biases
        tag = [sb(f"x_tag{q}", [P, TAG], I32, st) for q in range(U)]
        xs = [sb(f"x_xs{q}", [P, D], stack=st) for q in range(U)]
        xf = sb("x_xf", [P, 2, P], stack=st)
        none = sb("x_none", [P, 1], stack=st)
        pace = sb("x_pace", [P, 1], stack=st)
        xh = sb("x_xh", [P, 2, P], F32R, st)
        xl = sb("x_xl", [P, 2, P], F32R, st)
        r = sb("x_r", [P, 2, FF], stack=st)
        hh = sb("x_hh", [P, 2, FF], F32R, st)
        hl = sb("x_hl", [P, 2, FF], F32R, st)
        yl = sb("x_yl", [P, 2, D], stack=st)
        y = sb("x_y", [P, R, D], stack=st)
        pT = [pb(f"x_pT{q}", [P, 512], stack=st) for q in range(2)]
        pz = [pb(f"x_pz{q}", [P, FF], stack=st) for q in range(2)]
        pt = [pb(f"x_pt{q}", [P, FF], stack=st) for q in range(2)]
        py = [pb(f"x_py{q}", [P, 4, D], stack=st) for q in range(2)]
        w1, w2 = (mwp[:, n * E * KF:(n + 1) * E * KF].rearrange("p (e k) w d -> p e k w d", e=E) for n in range(2))
        loaded = [sem(f"x_loaded{q}", st) for q in range(U)]
        gathered = [sem(f"x_gathered{q}", st) for q in range(U)]
        sent = [sem(f"x_sent{q}", st) for q in range(R)]
        names = ("x_turned xh_made xl_made z_made r_made r_turned hh_made hl_made y_summed yl_made y_made paced xf_made "
                 "none_made").split()
        (x_turned, xh_made, xl_made, z_made, r_made, r_turned, hh_made, hl_made, y_summed, yl_made, y_made, paced, xf_made,
         none_made) = (sem("x_" + n, st) for n in names)

        with nc.Block() as block:
            @block.sync
            def _(sp):
                def load(t, c):
                    r = sp.value_load(row_of_tile[0:1, bass.ds(t, 1)], min_val=0, max_val=TAG_ROWS - P)
                    sp.dma_start(tag[c][:], tags_dram[bass.ds(r, P), :]).then_inc(loaded[c], 16)

                for q in range(U):
                    load(q, q)

                def step(n, t, c):
                    if within(t + U, ET):
                        sp.wait_ge(sent[c % R], 16 * (U // R * n + c // R) + 16)
                        load(t + U, c)

                rolled(sp, step, ET, U, 0)

            @block.gpsimd
            def _(pool):
                def gather(c):
                    pool.indirect_dma_start(xs[c][:], None, h_dram.rearrange("b s d -> (b s) d"),
                                            bass.IndirectOffsetOnAxis(ap=tag[c][:, 0:1], axis=0)).then_inc(gathered[c], 16)

                pool.memset(none[:], 0.0).then_inc(none_made, 1)
                pool.wait_ge(none_made, 1)
                for c in range(AHEAD):
                    pool.wait_ge(loaded[c], 16)
                    gather(c)

                def step(n, t, c):
                    ahead = within(t + AHEAD, ET)
                    pool.wait_ge(y_made, t + 1)
                    after(pool, paced, t)
                    if ahead:
                        pool.wait_ge(loaded[(c + AHEAD) % U], 16 * (n + (c + AHEAD) // U) + 16)
                    pool.tensor_tensor(pace[:], none[:], none[:], ALU.add).then_inc(paced, 1)
                    carry(pool, none_made)
                    pool.wait_ge(paced, t + 1)
                    pool.indirect_dma_start(y_dram, bass.IndirectOffsetOnAxis(ap=tag[c][:, 1:2], axis=0),
                                            y[:, c % R, :], None).then_inc(sent[c % R], 16)
                    if ahead:
                        gather((c + AHEAD) % U)

                rolled(pool, step, ET, U, 0)
                for q in range(R):
                    pool.wait_ge(sent[q], 16 * (ET // R))

            @block.tensor
            def _(pe):
                held = {}

                def weights_of(t, place):
                    if place not in held:
                        held[place] = pe.value_load(expert_of_tile[0:1, bass.ds(t, 1)], min_val=0, max_val=E - 1)
                    return held[place]

                def turn(n, t, c):
                    q = c % 2
                    pe.wait_ge(gathered[c], 16 * n + 16)
                    nc.tensor.transpose(pT[q][:, 0:P], xs[c][:, 0:D], ident[:]).then_inc(x_turned, 1)

                def first(n, t, c):
                    q = c % 2
                    e = weights_of(t, c)
                    pe.wait_ge(xl_made, t + 1)
                    wh, wl = (w1[:, bass.ds(e, 1), :, n_, :].rearrange("p o k d -> p (o k) d") for n_ in range(2))
                    nc.tensor.matmul(pz[q][:], xh[:, q], wh, start=True, stop=False)
                    nc.tensor.matmul(pz[q][:], xh[:, q], wl, start=False, stop=False)
                    nc.tensor.matmul(pz[q][:], xl[:, q], wh, start=False, stop=True).then_inc(z_made, 1)

                def turn_hidden(n, t, c):
                    q = c % 2
                    pe.wait_ge(r_made, t + 1)
                    for k in range(KF):
                        last = nc.tensor.transpose(pt[q][:, k * P:(k + 1) * P], r[:, q, k * P:(k + 1) * P], ident[:])
                    last.then_inc(r_turned, 1)

                def second(n, t, c, place):
                    q = c % 2
                    e = weights_of(t, place)
                    pe.wait_ge(hl_made, t + 1)
                    after(pe, y_made, t - 1)
                    for k in range(KF):
                        w = w2[:, bass.ds(e, 1), k]
                        h = slice(k * P, (k + 1) * P)
                        nc.tensor.matmul(py[q][:, 0:2, :], hh[:, q, h], w.rearrange("p o w d -> p (o w) d"),
                                         start=(k == 0), stop=False)
                        nc.tensor.matmul(py[q][:, 0, :], hl[:, q, h], w[:, :, 0], start=False, stop=False)
                    nc.tensor.matmul(py[q][:, 0, :], onesr[:], b2[:, bass.ds(e * D, D)], start=False, stop=True)\
                        .then_inc(y_summed, 1)

                turn(0, 0, 0)
                turn(0, 1, 1)

                def step(n, t, c):
                    if c == 0:
                        held.clear()
                    if within(t, ET):
                        first(n, t, c)
                    if within(t - 1, ET):
                        turn_hidden(*behind(n, t, c, 1, U))
                    if within(t + 2, ET):
                        turn(*behind(n, t, c, -2, U))
                    if within(t - 2, ET):
                        second(*behind(n, t, c, 2, U), c - 2)

                rolled(pe, step, ET, U, 2)

            @block.scalar
            def _(act):
                def high(n, t, c):
                    q = c % 2
                    act.wait_ge(xf_made, t + 1)
                    act.activation(xh[:, q], xf[:, q], ACT.Copy).then_inc(xh_made, 1)

                def hidden_high(n, t, c):
                    q = c % 2
                    act.wait_ge(r_turned, t + 1)
                    act.activation(hh[:, q], pt[q][:], ACT.Relu).then_inc(hh_made, 1)

                def low_sums(n, t, c):
                    q = c % 2
                    act.wait_ge(y_summed, t + 1)
                    after(act, y_made, t - 1)
                    act.activation(yl[:, q], py[q][:, 1, :], ACT.Copy, scale=tag[c][:, 2:3].bitcast(F32)).then_inc(yl_made, 1)

                high(0, 0, 0)
                high(0, 1, 1)

                def step(n, t, c):
                    if within(t - 1, ET):
                        hidden_high(*behind(n, t, c, 1, U))
                    if within(t + 2, ET):
                        high(*behind(n, t, c, -2, U))
                    if within(t - 2, ET):
                        low_sums(*behind(n, t, c, 2, U))

                rolled(act, step, ET, U, 2)

            @block.vector
            def _(dve):
                def gained(n, t, c):
                    q = c % 2
                    dve.wait_ge(x_turned, t + 1)
                    nc.vector.tensor_scalar(xf[:, q], pT[q][:, 0:P], gbc[:, 0:1], gbc[:, 1:2], ALU.mult, ALU.add)\
                        .then_inc(xf_made, 1)

                def low(n, t, c):
                    q = c % 2
                    dve.wait_ge(xh_made, t + 1)
                    nc.vector.tensor_tensor(xl[:, q], xf[:, q], xh[:, q].bitcast(F32), ALU.subtract)\
                        .then_inc(xl_made, 1)

                def hidden(n, t, c):
                    q = c % 2
                    e = dve.value_load(expert_of_tile[0:1, bass.ds(t, 1)], min_val=0, max_val=E - 1)
                    dve.wait_ge(z_made, t + 1)
                    nc.vector.tensor_tensor(r[:, q], pz[q][:], b1[:, bass.ds(e * FF, FF)], ALU.add).then_inc(r_made, 1)

                def hidden_low(n, t, c):
                    q = c % 2
                    dve.wait_ge(hh_made, t + 1)
                    nc.vector.scalar_tensor_tensor(hl[:, q], pt[q][:], 0.0, hh[:, q].bitcast(F32), ALU.max, ALU.subtract)\
                        .then_inc(hl_made, 1)

                def result(n, t, c):
                    q = c % 2
                    dve.wait_ge(yl_made, t + 1)
                    after(dve, sent[c % R], 16 * (U // R * n + c // R))
                    nc.vector.scalar_tensor_tensor(y[:, c % R], py[q][:, 0, :], tag[c][:, 2:3].bitcast(F32), yl[:, q],
                                                   ALU.mult, ALU.add).then_inc(y_made, 1)

                for t in range(2):
                    gained(0, t, t)
                for t in range(2):
                    low(0, t, t)

                def step(n, t, c):
                    if within(t, ET):
                        hidden(n, t, c)
                    if within(t + 2, ET):
                        gained(*behind(n, t, c, -2, U))
                    if within(t - 1, ET):
                        hidden_low(*behind(n, t, c, 1, U))
                    if within(t + 2, ET):
                        low(*behind(n, t, c, -2, U))
                    if within(t - 2, ET):
                        result(*behind(n, t, c, 2, U))

                rolled(dve, step, ET, U, 2)


def combine(nc, sb, sem, x1, y_dram, out):
    with ExitStack() as st:
        y = sb("f_y", [P, 2, 2, SB, D], stack=st)
        t = sb("f_t", [P, 2, SB, D], stack=st)
        o = sb("f_o", [P, 2, SB, D], stack=st)
        loaded = [sem(f"f_loaded{q}", st) for q in range(2)]
        stored = [sem(f"f_stored{q}", st) for q in range(2)]
        t_made = sem("f_t_made", st)
        o_made = sem("f_o_made", st)
        y_view = y_dram[0:2 * T, :].rearrange("(k b s) d -> b k s d", k=2, b=B)

        with nc.Block() as block:
            @block.sync
            def _(sp):
                for i in range(2):
                    for k in range(2):
                        sp.dma_start(y[:, i, k], y_view[:, k, i * SB:(i + 1) * SB, :]).then_inc(loaded[i], 16)
                with sp.Fori(1, NB // 2) as j:
                    for q in range(2):
                        sp.wait_ge(o_made, 2 * j + q - 1)
                        for k in range(2):
                            sp.dma_start(y[:, q, k], y_view[:, k, bass.ds((2 * j + q) * SB, SB), :]).then_inc(loaded[q], 16)

            @block.scalar
            def _(act):
                with act.Fori(0, NB // 2) as j:
                    for q in range(2):
                        act.wait_ge(o_made, 2 * j + q + 1)
                        act.dma_start(out[:, bass.ds((2 * j + q) * SB, SB), :], o[:, q]).then_inc(stored[q], 16)
                for q in range(2):
                    act.wait_ge(stored[q], 16 * (NB // 2))

            @block.vector
            def _(dve):
                def total(n, i, q):
                    dve.wait_ge(loaded[q], 32 * n + 32)
                    nc.vector.tensor_tensor(t[:, q], y[:, q, 0], y[:, q, 1], ALU.add).then_inc(t_made, 1)
                    dve.wait_ge(t_made, i + 1)
                    after(dve, stored[q], 16 * n)
                    nc.vector.tensor_tensor(o[:, q], t[:, q], x1[:, bass.ds(i * SB, SB), :], ALU.add).then_inc(o_made, 1)

                rolled(dve, total, NB, 2, 0)


def constants():
    p = np.arange(P)
    f = np.float32
    parts = [np.eye(P, dtype=f), (p[:, None] < p[None, :]).astype(f), np.ones((P, P), f),
             ((p[:, None] // DK) % HG == np.arange(HG)[None, :]).astype(f), (p[:, None] % LO).astype(f),
             np.tile(np.arange(TYPES, dtype=f), (P, 1)), np.tile(np.arange(S, dtype=f), (P, 1)),
             np.tile(BT * np.arange(TT, dtype=f), (P, 1))]
    return np.ascontiguousarray(np.concatenate(parts, axis=1))


def route_constants():
    f = np.float32
    parts = [E - np.arange(E, dtype=f), T * np.arange(E, dtype=f), P * np.arange(ET, dtype=f)]
    return np.ascontiguousarray(np.tile(np.concatenate(parts), (P, 1)))


def choice_ids():
    ids = np.zeros((P, S, 2, TAG), np.int32)
    ids[..., 0] = (np.arange(P)[:, None] * S + np.arange(S)[None, :])[:, :, None]
    ids[..., 1] = ids[..., 0] + T * np.arange(2)
    return ids


def empty_tags():
    tags = np.zeros((TAG_ROWS, TAG), np.int32)
    tags[:, 1] = 2 * T + np.arange(TAG_ROWS)
    return tags


def arrays_of(inputs):
    g = {k: np.asarray(v) for k, v in inputs.items()}
    c = np.ascontiguousarray
    L0, C1, F1 = "L0_cond_", "L1_cond_", "L1_ffn_"
    return {
        "x": c(g["x"]),
        "langs": c(g["itok_B_0_8"].reshape(1, B)),
        "types": c(g["itok_B_0_2"].reshape(B, 1)),
        "consts": constants(),
        "W1": c(g[L0 + "W1"].transpose(1, 0, 2).reshape(D, LA)),
        "b1": c(g[L0 + "b1"].reshape(1, LA)),
        "W2": c(g[L0 + "W2"].reshape(LA, D)),
        "tab": c(np.stack([g[L0 + "gamma"], g[L0 + "beta"], g[L0 + "b2"]], axis=1)),
        "w_gate": c(g["L0_ffn_w_gate"].T),
        "w_up": c(g["L0_ffn_w_up"].T),
        "cw": c(np.concatenate(
            [g[C1 + "wi"].transpose(1, 0, 2).reshape(D, -1),
             g[C1 + "wo"].reshape(TYPES, KF, P, D).transpose(2, 0, 1, 3).reshape(P, -1),
             g[C1 + "swi"].transpose(1, 0, 2).reshape(D, -1),
             g[C1 + "swo"].reshape(NSH, KF, P, D).transpose(2, 0, 1, 3).reshape(P, -1)], axis=1).reshape(P, CB, D)),
        "mw": c(np.concatenate(
            [g[F1 + "W1"].transpose(1, 0, 2).reshape(D, -1),
             g[F1 + "W2"].reshape(E, KF, P, D).transpose(2, 0, 1, 3).reshape(P, -1)], axis=1).reshape(P, MB, D)),
        "m_b1": c(g[F1 + "b1"].reshape(1, -1)),
        "m_b2": c(g[F1 + "b2"].reshape(1, -1)),
        "signs": np.array([[0, 1], [1, -1]], np.float32),
        "quad": (np.arange(P)[:, None] // S == np.arange(BT)[None, :]).astype(np.float32),
        "rconsts": route_constants(),
        "ids": choice_ids(),
        "tags": empty_tags(),
        "w_o": c(g[F1 + "w_o"]),
        "b_o": c(g[F1 + "b_o"].reshape(1, D)),
        "ln2c": c(np.stack([g[F1 + "ln2_g"], g[F1 + "ln2_b"]], axis=1)),
        "gate_w": c(g[F1 + "gate_w"]),
        "gate_b": c(g[F1 + "gate_b"].reshape(1, E)),
        "g1": c(g[C1 + "g1"].reshape(3, D, D).transpose(1, 0, 2)),
        "g2": c(g[C1 + "g2"]),
        "w_qkv": c(g[F1 + "w_qkv"]),
        "b_qkv": c(g[F1 + "b_qkv"].reshape(1, 3 * D)),
        "ln1_g": c(g[F1 + "ln1_g"].reshape(D, 1)),
        "ln1_b": c(g[F1 + "ln1_b"].reshape(D, 1)),
        "w_down": c(g["L0_ffn_w_down"].T.reshape(KF, P, D).transpose(1, 0, 2).reshape(P, KF * D)),
    }


def kernel(**inputs):
    import concourse.bacc as bacc
    from concourse.bass_utils import run_bass_kernel_spmd

    nc = bacc.Bacc("TRN2", target_bir_lowering=False, num_devices=1)
    arrays = {f"in_{n}": v for n, v in arrays_of(inputs).items()}
    a = {n[3:]: nc.dram_tensor(n, v.shape, mybir.dt.from_np(v.dtype), kind="ExternalInput").ap()
         for n, v in arrays.items()}
    out = nc.dram_tensor("out_dram", (B, S, D), F32, kind="ExternalOutput").ap()
    adaln_ffn_moe_kernel(nc, a, out)
    r = run_bass_kernel_spmd(nc, [arrays], core_ids=[0])
    return r.results[0]["out_dram"]
```
